# Optimizing a Trainium2 kernel written in Bass

```python
import numpy as np
import jax
import jax.numpy as jnp

def _softmax(x, axis=-1):
    return jax.nn.softmax(x, axis=axis)

def _gelu(x):
    return jax.nn.gelu(x, approximate=True)

def _silu(x):
    return jax.nn.silu(x)

def _sigmoid(x):
    return jax.nn.sigmoid(x)

def _layernorm(x, axis=-1, eps=1e-05):
    m = jnp.mean(x, axis=axis, keepdims=True)
    v = jnp.var(x, axis=axis, keepdims=True)
    return (x - m) / jnp.sqrt(v + eps)

def _scatter_add(tgt, idx, src, axis=0):
    return tgt.at[idx].add(src)

def _segment_sum(src, seg, n):
    return jax.ops.segment_sum(src, seg, n)
kernel_name = 'mk_gnn_preln_d2_gnn_r8_bacae4'

def setup_inputs(seed: int=0):
    np.random.seed(seed)
    _w = jnp.asarray

    def _rec_inputs():
        import jax
        import jax.numpy as jnp
        _gk = jax.random.key(seed)
        x = -0.0005121 + 1.001 * jax.random.normal(jax.random.fold_in(_gk, 1), (6250, 64), jnp.float32)
        _s = jax.random.randint(jax.random.fold_in(_gk, 2), (100000,), 0, 6250, jnp.int32)
        _d = jax.random.randint(jax.random.fold_in(_gk, 3), (100000,), 0, 6250, jnp.int32)
        _loop = jnp.arange(6250, dtype=jnp.int32)
        src = jnp.concatenate([_s, _d, _loop])
        dst = jnp.concatenate([_d, _s, _loop])
        _o = jnp.argsort(dst, stable=True)
        src = src[_o]
        dst = dst[_o]
        edge_attr_32 = 0.000196303 + 1.00016 * jax.random.normal(jax.random.fold_in(_gk, 11), (206250, 32), jnp.float32)
        return (x, src, dst, edge_attr_32)
    x, src, dst, edge_attr_32 = _rec_inputs()

    def _L0_gnn_setup():
        import jax, jax.numpy as jnp
        import numpy as np
        N_NODES = 6250
        IN_CH = 64
        REL_DIM = 32
        N_EDGES = 100000
        NEG_SLOPE = 0.01

        def _kgconv(x, src, dst, e, W, b, ai_w, ai_b, aj_w, aj_b, ew_w, ew_b):
            x = x @ W.T + b
            x_i = x[dst]
            x_j = x[src]
            alpha = x_i @ ai_w.T + ai_b + (x_j @ aj_w.T + aj_b) + (e @ ew_w.T + ew_b)
            alpha = jax.nn.leaky_relu(alpha, NEG_SLOPE)
            m = jax.ops.segment_max(alpha, src, num_segments=N_NODES)
            ex = jnp.exp(alpha - m[src])
            s = jax.ops.segment_sum(ex, src, num_segments=N_NODES)
            alpha = ex / (s[src] + 1e-16)
            msg = alpha * (x_j + e)
            out = jax.ops.segment_sum(msg, dst, num_segments=N_NODES)
            return jax.nn.relu(out)
        key = jax.random.key(seed)
        ks = jax.random.split(key, 16)
        sc = 1.0 / np.sqrt(IN_CH)
        scr = 1.0 / np.sqrt(REL_DIM)

        def lin(k, out_d, in_d, s):
            k1, k2 = jax.random.split(k)
            return (jax.random.uniform(k1, (out_d, in_d), jnp.float32, -s, s), jax.random.uniform(k2, (out_d,), jnp.float32, -s, s))
        inp = {}
        inp['feat'] = jax.random.normal(ks[0], (N_NODES, IN_CH), jnp.float32)
        inp['edge_index'] = jax.random.randint(ks[1], (2, N_EDGES), 0, N_NODES)
        inp['r'] = jax.random.normal(ks[2], (N_EDGES, REL_DIM), jnp.float32)
        inp['rel_w'], inp['rel_b'] = lin(ks[3], IN_CH, REL_DIM, scr)
        for li, base in ((4, 'c1'), (10, 'c2')):
            inp[base + '_lin_w'], inp[base + '_lin_b'] = lin(ks[li], IN_CH, IN_CH, sc)
            inp[base + '_ai_w'], inp[base + '_ai_b'] = lin(ks[li + 1], 1, IN_CH, sc)
            inp[base + '_aj_w'], inp[base + '_aj_b'] = lin(ks[li + 2], 1, IN_CH, sc)
            inp[base + '_ew_w'], inp[base + '_ew_b'] = lin(ks[li + 3], 1, IN_CH, sc)
        return inp
    _L0_gnn_all = _L0_gnn_setup()
    _L0_gnn_in = {k: v for k, v in _L0_gnn_all.items() if k in ('rel_w', 'rel_b', 'c1_lin_w', 'c1_lin_b', 'c1_ai_w', 'c1_ai_b', 'c1_aj_w', 'c1_aj_b', 'c1_ew_w', 'c1_ew_b', 'c2_lin_w', 'c2_lin_b', 'c2_ai_w', 'c2_ai_b', 'c2_aj_w', 'c2_aj_b', 'c2_ew_w', 'c2_ew_b')}
    del _L0_gnn_all

    def _L1_gnn_setup():
        import jax, jax.numpy as jnp
        import numpy as np
        N_NODES = 12500
        N_EDGES = 200000
        IN_CH = 64
        OUT_CH = 64
        key = jax.random.key(seed)
        ks = jax.random.split(key, 6)
        x = jax.random.normal(ks[0], (N_NODES, IN_CH), dtype=jnp.float32)
        edge_index = jax.random.randint(ks[1], (2, N_EDGES), 0, N_NODES, dtype=jnp.int64)
        W1 = jax.random.normal(ks[2], (2 * IN_CH, OUT_CH), dtype=jnp.float32) * (1.0 / np.sqrt(2 * IN_CH))
        b1 = jnp.zeros((OUT_CH,), dtype=jnp.float32)
        W2 = jax.random.normal(ks[3], (OUT_CH, OUT_CH), dtype=jnp.float32) * (1.0 / np.sqrt(OUT_CH))
        b2 = jnp.zeros((OUT_CH,), dtype=jnp.float32)
        return {'x': x, 'edge_index': edge_index, 'W1': W1, 'b1': b1, 'W2': W2, 'b2': b2}
    _L1_gnn_all = _L1_gnn_setup()
    _L1_gnn_in = {k: v for k, v in _L1_gnn_all.items() if k in ('W1', 'b1', 'W2', 'b2')}
    del _L1_gnn_all
    return {'x': x, 'src': src, 'dst': dst, 'edge_attr_32': edge_attr_32, 'L0_gnn_rel_w': _L0_gnn_in['rel_w'], 'L0_gnn_rel_b': _L0_gnn_in['rel_b'], 'L0_gnn_c1_lin_w': _L0_gnn_in['c1_lin_w'], 'L0_gnn_c1_lin_b': _L0_gnn_in['c1_lin_b'], 'L0_gnn_c1_ai_w': _L0_gnn_in['c1_ai_w'], 'L0_gnn_c1_ai_b': _L0_gnn_in['c1_ai_b'], 'L0_gnn_c1_aj_w': _L0_gnn_in['c1_aj_w'], 'L0_gnn_c1_aj_b': _L0_gnn_in['c1_aj_b'], 'L0_gnn_c1_ew_w': _L0_gnn_in['c1_ew_w'], 'L0_gnn_c1_ew_b': _L0_gnn_in['c1_ew_b'], 'L0_gnn_c2_lin_w': _L0_gnn_in['c2_lin_w'], 'L0_gnn_c2_lin_b': _L0_gnn_in['c2_lin_b'], 'L0_gnn_c2_ai_w': _L0_gnn_in['c2_ai_w'], 'L0_gnn_c2_ai_b': _L0_gnn_in['c2_ai_b'], 'L0_gnn_c2_aj_w': _L0_gnn_in['c2_aj_w'], 'L0_gnn_c2_aj_b': _L0_gnn_in['c2_aj_b'], 'L0_gnn_c2_ew_w': _L0_gnn_in['c2_ew_w'], 'L0_gnn_c2_ew_b': _L0_gnn_in['c2_ew_b'], 'L1_gnn_W1': _L1_gnn_in['W1'], 'L1_gnn_b1': _L1_gnn_in['b1'], 'L1_gnn_W2': _L1_gnn_in['W2'], 'L1_gnn_b2': _L1_gnn_in['b2']}

def reference(x, src, dst, edge_attr_32, L0_gnn_rel_w, L0_gnn_rel_b, L0_gnn_c1_lin_w, L0_gnn_c1_lin_b, L0_gnn_c1_ai_w, L0_gnn_c1_ai_b, L0_gnn_c1_aj_w, L0_gnn_c1_aj_b, L0_gnn_c1_ew_w, L0_gnn_c1_ew_b, L0_gnn_c2_lin_w, L0_gnn_c2_lin_b, L0_gnn_c2_ai_w, L0_gnn_c2_ai_b, L0_gnn_c2_aj_w, L0_gnn_c2_aj_b, L0_gnn_c2_ew_w, L0_gnn_c2_ew_b, L1_gnn_W1, L1_gnn_b1, L1_gnn_W2, L1_gnn_b2):
    import jax
    import jax.numpy as jnp

    def _L0_gnn_ref(feat, edge_index, r, rel_w, rel_b, c1_lin_w, c1_lin_b, c1_ai_w, c1_ai_b, c1_aj_w, c1_aj_b, c1_ew_w, c1_ew_b, c2_lin_w, c2_lin_b, c2_ai_w, c2_ai_b, c2_aj_w, c2_aj_b, c2_ew_w, c2_ew_b):
        import jax, jax.numpy as jnp
        import numpy as np
        N_NODES = 6250
        IN_CH = 64
        REL_DIM = 32
        N_EDGES = 100000
        NEG_SLOPE = 0.01

        def _kgconv(x, src, dst, e, W, b, ai_w, ai_b, aj_w, aj_b, ew_w, ew_b):
            x = x @ W.T + b
            x_i = x[dst]
            x_j = x[src]
            alpha = x_i @ ai_w.T + ai_b + (x_j @ aj_w.T + aj_b) + (e @ ew_w.T + ew_b)
            alpha = jax.nn.leaky_relu(alpha, NEG_SLOPE)
            m = jax.ops.segment_max(alpha, src, num_segments=N_NODES)
            ex = jnp.exp(alpha - m[src])
            s = jax.ops.segment_sum(ex, src, num_segments=N_NODES)
            alpha = ex / (s[src] + 1e-16)
            msg = alpha * (x_j + e)
            out = jax.ops.segment_sum(msg, dst, num_segments=N_NODES)
            return jax.nn.relu(out)
        src, dst = (edge_index[0], edge_index[1])
        e = r @ rel_w.T + rel_b
        x = _kgconv(feat, src, dst, e, c1_lin_w, c1_lin_b, c1_ai_w, c1_ai_b, c1_aj_w, c1_aj_b, c1_ew_w, c1_ew_b)
        x = jax.nn.relu(x)
        x = _kgconv(x, src, dst, e, c2_lin_w, c2_lin_b, c2_ai_w, c2_ai_b, c2_aj_w, c2_aj_b, c2_ew_w, c2_ew_b)
        return x

    def _L1_gnn_ref(x, edge_index, W1, b1, W2, b2):
        import jax, jax.numpy as jnp
        import numpy as np
        N_NODES = 12500
        N_EDGES = 200000
        IN_CH = 64
        OUT_CH = 64
        src = edge_index[0]
        dst = edge_index[1]
        x_i = x[dst]
        x_j = x[src]
        edge_features = jnp.concatenate([x_i, x_j - x_i], axis=-1)
        h = jax.nn.relu(edge_features @ W1 + b1)
        edge_messages = h @ W2 + b2
        out = jax.ops.segment_max(edge_messages, dst, num_segments=x.shape[0])
        return jnp.where(jnp.isfinite(out), out, jnp.zeros_like(out))
    edge_index = jnp.stack([src, dst])
    h = jnp.maximum(_layernorm(x, axis=-1), 0.0)
    x = x + _L0_gnn_ref(h, edge_index, edge_attr_32, L0_gnn_rel_w, L0_gnn_rel_b, L0_gnn_c1_lin_w, L0_gnn_c1_lin_b, L0_gnn_c1_ai_w, L0_gnn_c1_ai_b, L0_gnn_c1_aj_w, L0_gnn_c1_aj_b, L0_gnn_c1_ew_w, L0_gnn_c1_ew_b, L0_gnn_c2_lin_w, L0_gnn_c2_lin_b, L0_gnn_c2_ai_w, L0_gnn_c2_ai_b, L0_gnn_c2_aj_w, L0_gnn_c2_aj_b, L0_gnn_c2_ew_w, L0_gnn_c2_ew_b)
    h = jnp.maximum(_layernorm(x, axis=-1), 0.0)
    x = x + _L1_gnn_ref(h, edge_index, L1_gnn_W1, L1_gnn_b1, L1_gnn_W2, L1_gnn_b2)
    return x

_drawn_inputs = setup_inputs


def setup_inputs(seed=0):
    import zlib

    import numpy as np

    out = dict(_drawn_inputs(seed))
    spreads = {'L1_gnn_b1': (0.0, 0.1), 'L1_gnn_b2': (0.0, 0.1)}
    factors = {'L0_gnn_c1_lin_b': 3.071,
     'L0_gnn_c1_ai_w': 8.0,
     'L0_gnn_c1_aj_w': 39.151,
     'L0_gnn_c1_ew_w': 5.815,
     'L0_gnn_c2_ai_w': 8.0,
     'L0_gnn_c2_aj_w': 8.0,
     'L0_gnn_c2_ew_w': 4.138}
    for name, (base, spread) in spreads.items():
        noise = np.random.default_rng([zlib.crc32(name.encode()), seed]).standard_normal(out[name].shape)
        drawn = base * np.exp(spread * noise) if base else spread * noise
        out[name] = jnp.asarray(drawn.astype(out[name].dtype))
    for name, factor in factors.items():
        out[name] = (out[name] * factor).astype(out[name].dtype)
    return out
```

```python
import concourse.bass as bass
from concourse import mybir
from contextlib import ExitStack, contextmanager

F32 = mybir.dt.float32
BF16 = mybir.dt.bfloat16
I32 = mybir.dt.int32
ALU = mybir.AluOpType
ACT = mybir.ActivationFunctionType
AX = mybir.AxisListType

N = 6250
E = 206250
D = 64
R = 32
P = 128
NB = -(-N // P)
NP = NB * P
TABLE = NP + P
PAD_NODE = TABLE - 1
GT = 4
UNROLL = 4
W = -(-E // (P * GT * UNROLL)) * GT * UNROLL
EP = P * W
NG = W // GT
TW = D + 3
M = D + R + 1
BITS = 13
DIGITS = 16
SIGN = 2.0 ** 50
BIG = SIGN * SIGN
SKIP = 1 << 29
EPS = 1e-5
assert N <= 1 << BITS and PAD_NODE < 1 << BITS


def bcast(ap, shape):
    return ap.unsqueeze(len(shape) - 1).to_broadcast(shape)


def mid(ap, shape):
    return ap.unsqueeze(1).to_broadcast(shape)


def over_groups(eng, stage):
    with eng.Fori(0, NG // UNROLL) as i:
        for u in range(UNROLL):
            stage(i * UNROLL + u, u)


def over_groups_skewed(eng, first, second):
    first(0, 0)
    with eng.Fori(0, NG // UNROLL - 1) as i:
        for u in range(UNROLL):
            first(i * UNROLL + (u + 1), (u + 1) % UNROLL)
            second(i * UNROLL + u, u)
    for g in range(NG - UNROLL, NG):
        if g + 1 < NG:
            first(g + 1, (g + 1) % UNROLL)
        second(g, g % UNROLL)


def over_groups_ahead(eng, first, second):
    for u in range(UNROLL):
        first(u, u)
    with eng.Fori(0, NG // UNROLL - 1) as i:
        for u in range(UNROLL):
            first(i * UNROLL + (UNROLL + u), u)
            second(i * UNROLL + u, u)
    for g in range(NG - UNROLL, NG):
        second(g, g % UNROLL)


def gnn_kernel(nc, x, src, dst, attr, rel_w, rel_b,
               c1_w, c1_b, c1_ai_w, c1_ai_b, c1_aj_w, c1_aj_b, c1_ew_w, c1_ew_b,
               c2_w, c2_b, c2_ai_w, c2_ai_b, c2_aj_w, c2_aj_b, c2_ew_w, c2_ew_b,
               w1, b1, w2, b2, out):
    ctx = ExitStack()
    with ctx:
        ctx.enter_context(nc.allow_non_contiguous_dma(reason="columns of a few numbers"))
        def sb(name, shape, dt, c=ctx):
            return c.enter_context(nc.sbuf_tensor(name, shape, dt))

        def pb(name, shape, dt, c):
            return c.enter_context(nc.psum_tensor(name, shape, dt))

        phases = []

        @contextmanager
        def phase():
            with ExitStack() as c:
                phases.append((c, []))
                yield c
                own = phases.pop()[1]
                if own:
                    with nc.Block() as block:
                        @block.gpsimd
                        def _(pool):
                            for s in own:
                                pool.sem_clear(s)

        def sem(name):
            c, own = phases[-1]
            own.append(c.enter_context(nc.semaphore(name)))
            return own[-1]

        def dram(name, shape, dt):
            return nc.dram_tensor(name, shape, dt, kind="Internal").ap()

        table = dram("table", [TABLE, TW], F32)
        rows = dram("rows", [EP + 1, M], F32)
        carries = dram("carries", [P + 1, M], F32)
        peak_rows = dram("peak_rows", [EP + 1, D], F32)
        peak_carries = dram("peak_carries", [P + 1, D], F32)
        a_starts = dram("a_starts", [EP, 1], F32)
        a_table = dram("a_table", [TABLE, D], F32)
        b_table = dram("b_table", [TABLE, D], F32)
        row_starts = dram("row_starts", [EP, D], F32)

        src_i = sb("src_i", [P, W], I32)
        lo = sb("lo", [P, W], F32)
        blk = sb("blk", [P, W], F32)
        lead = sb("lead", [P, W], F32)
        cont = sb("cont", [P, W], F32)
        z = [sb(f"z{k}", [P, W], F32) for k in range(2)]
        digits = sb("digits", [P, W * DIGITS], BF16)
        x_sb = sb("x_sb", [P, NB, D], F32)
        h = sb("h", [P, NB, D], F32)
        count = sb("count", [P, NB], F32)
        start_i = sb("start_i", [P, NB], I32)
        end_i = sb("end_i", [P, NB], I32)
        carry_i = sb("carry_i", [P, NB], I32)
        has = sb("has", [P, NB], F32)
        dst0_i = sb("dst0_i", [P, 1], I32)
        strad = sb("strad", [P, 1], F32)
        through = sb("through", [P, 1], F32)
        iota = sb("iota", [P, P], F32)
        lane = sb("lane", [P, 1], F32)
        ident = sb("ident", [P, P], F32)
        identb = sb("identb", [P, P], BF16)
        below = sb("below", [P, P], F32)
        ones = sb("ones", [P, P], F32)
        minus = sb("minus", [1, GT * P], F32)
        zero = sb("zero", [P, 8 * D], F32)
        rel_aug = sb("rel_aug", [D, R + 1], F32)
        rel_t = sb("rel_t", [R + 1, D], F32)
        v = sb("v", [P, 2, R + 1], F32)
        bias = sb("bias", [P, 2], F32)

        with phase() as c:
            dst_i = sb("dst_i", [P, W], I32, c)
            tmp_i = sb("tmp_i", [P, W], I32, c)
            dlo = sb("dlo", [P, W], F32, c)
            dblk = sb("dblk", [P, W], F32, c)
            pow_i = sb("pow_i", [P, DIGITS], I32, c)
            bit_i = sb("bit_i", [P, 16, DIGITS], I32, c)
            prev_i = sb("prev_i", [P, 1], I32, c)
            prev_f = sb("prev_f", [P, 1], F32, c)
            dst0_f = sb("dst0_f", [P, 1], F32, c)
            dstl_f = sb("dstl_f", [P, 1], F32, c)
            ew = sb("ew", [D, 2], F32, c)
            bias_in = sb("bias_in", [P, 6], F32, c)
            hot_lo = sb("hot_lo", [P, UNROLL, GT, P], BF16, c)
            hot_blk = sb("hot_blk", [P, UNROLL, GT, NB], BF16, c)
            start_f = sb("start_f", [P, NB], F32, c)
            end_f = sb("end_f", [P, NB], F32, c)
            chunk_f = sb("chunk_f", [P, NB], F32, c)
            total = sb("total", [P, NB], F32, c)
            tmp1 = sb("tmp1", [P, NB], F32, c)
            tmp2 = sb("tmp2", [P, NB], F32, c)
            bounds = sb("bounds", [P, P], F32, c)
            neutral = sb("neutral", [1, M], F32, c)
            hot_f = sb("hot_f", [P, P], F32, c)
            small = pb("small", [P, 512], F32, c)
            hist = pb("hist", [P, NB], F32, c)

            edges_in, small_in, made = sem("edges_in"), sem("small_in"), sem("made")
            chain, hot_ready, hot_used = sem("chain"), sem("hot_ready"), sem("hot_used")
            sums_ready, sums_done = sem("sums_ready"), sem("sums_done")
            proj_done, zeroed, filled = sem("proj_done"), sem("zeroed"), sem("filled")
            with nc.Block() as block:
                @block.sync
                def _(sp):
                    sp.dma_start(src_i[:, :], src).then_inc(edges_in, 16)
                    sp.dma_start(dst_i[:, :], dst).then_inc(edges_in, 16)
                    sp.dma_start(dst0_i[:, :], dst[:, 0:1]).then_inc(edges_in, 16)
                    sp.dma_start(prev_i[1:P, :], dst[0:P - 1, W - 1:W]).then_inc(edges_in, 16)
                    sp.dma_start(x_sb[:, :, :], x.rearrange("(b p) f -> p b f", p=P)).then_inc(small_in, 16)
                    sp.dma_start(rel_aug[:, 0:R], rel_w).then_inc(small_in, 16)
                    sp.dma_start(rel_aug[:, R:R + 1], bass_col(rel_b)).then_inc(small_in, 16)
                    sp.dma_start(ew[:, 0:1], c1_ew_w.rearrange("a d -> d a")).then_inc(small_in, 16)
                    sp.dma_start(ew[:, 1:2], c2_ew_w.rearrange("a d -> d a")).then_inc(small_in, 16)
                    for k, b in enumerate((c1_ai_b, c1_aj_b, c1_ew_b, c2_ai_b, c2_aj_b, c2_ew_b)):
                        sp.dma_start(bias_in[:, k:k + 1], b.partition_broadcast(P)).then_inc(small_in, 16)
                    sp.wait_ge(zeroed, 1)
                    sp.dma_start(a_starts.rearrange("(p t) f -> p (t f)", p=P), z[0][:, :]).then_inc(filled, 16)
                    sp.dma_start(table[NP:TABLE, :], zero[:, 0:TW]).then_inc(filled, 16)
                    sp.dma_start(a_table[NP:TABLE, :], zero[:, 0:D]).then_inc(filled, 16)
                    sp.dma_start(b_table[NP:TABLE, :], zero[:, 0:D]).then_inc(filled, 16)
                    sp.dma_start(rows[EP:EP + 1, :], zero[0:1, 0:M]).then_inc(filled, 16)
                    sp.dma_start(carries[P:P + 1, :], zero[0:1, 0:M]).then_inc(filled, 16)
                    sp.dma_start(peak_rows[EP:EP + 1, :], neutral[0:1, 0:D]).then_inc(filled, 16)
                    sp.dma_start(peak_carries[P:P + 1, :], neutral[0:1, 0:D]).then_inc(filled, 16)
                    wide = row_starts.rearrange("(p t) f -> p t f", p=P)
                    with sp.Fori(0, W // 8) as i:
                        sp.dma_start(wide[:, bass.ds(i * 8, 8), :],
                                     zero[:, :].rearrange("p (t f) -> p t f", f=D)).then_inc(filled, 16)
                    sp.wait_ge(filled, 16 * (8 + W // 8))

                @block.gpsimd
                def _(pool):
                    pool.iota(iota[:, :], [[1, P]], base=0, channel_multiplier=0,
                              allow_small_or_imprecise_dtypes=True).then_inc(made, 1)
                    pool.iota(lane[:, :], [[0, 1]], base=0, channel_multiplier=1,
                              allow_small_or_imprecise_dtypes=True).then_inc(made, 1)
                    pool.iota(bounds[:, :], [[W, P]], base=0, channel_multiplier=0,
                              allow_small_or_imprecise_dtypes=True).then_inc(made, 1)
                    pool.memset(ones[:, :], 1.0).then_inc(made, 1)
                    pool.memset(minus[:, :], -BITS * BIG).then_inc(made, 1)
                    for k in range(DIGITS):
                        pool.memset(pow_i[:, k:k + 1], 1 << k).then_inc(made, 1)
                    pool.memset(neutral[:, :], -BIG).then_inc(made, 1)

                @block.vector
                def _(dve):
                    n = [0]

                    def then(ins):
                        ins.then_inc(chain, 1)
                        n[0] += 1
                        dve.wait_ge(chain, n[0])

                    dve.memset(prev_i[0:1, :], -1).then_inc(chain, 1)
                    n[0] += 1
                    then(dve.memset(zero[:, :], 0.0))
                    dve.wait_ge(made, 6 + DIGITS)
                    dve.memset(z[0][:, :], 0.0).then_inc(zeroed, 1)
                    then(dve.tensor_scalar(ident[:, :], iota[:, :], lane[:, 0:1], None, ALU.is_equal))
                    then(dve.tensor_copy(identb[:, :], ident[:, :]))
                    then(dve.tensor_scalar(below[:, :], iota[:, :], lane[:, 0:1], None, ALU.is_gt))
                    dve.wait_ge(edges_in, 64)
                    dve.wait_ge(small_in, 16 * 11)
                    then(dve.tensor_scalar(tmp_i[:, :], dst_i[:, :], P - 1, None, ALU.bitwise_and))
                    then(dve.tensor_copy(dlo[:, :], tmp_i[:, :]))
                    then(dve.tensor_scalar(tmp_i[:, :], dst_i[:, :], 7, None, ALU.logical_shift_right))
                    then(dve.tensor_copy(dblk[:, :], tmp_i[:, :]))
                    then(dve.tensor_tensor(cont[:, 1:W], dst_i[:, 1:W], dst_i[:, 0:W - 1], ALU.is_equal))
                    then(dve.memset(cont[:, 0:1], 0.0))
                    then(dve.tensor_copy(prev_f[:, :], prev_i[:, :]))
                    then(dve.tensor_copy(dst0_f[:, :], dst_i[:, 0:1]))
                    then(dve.tensor_copy(dstl_f[:, :], dst_i[:, W - 1:W]))
                    then(dve.tensor_tensor(strad[:, :], prev_f[:, :], dst0_f[:, :], ALU.is_equal))
                    then(dve.tensor_tensor(through[:, :], dstl_f[:, :], dst0_f[:, :], ALU.is_equal))
                    then(dve.tensor_tensor(through[:, :], through[:, :], strad[:, :], ALU.mult))
                    then(dve.tensor_scalar(tmp_i[:, :], src_i[:, :], P - 1, None, ALU.bitwise_and))
                    then(dve.tensor_copy(lo[:, :], tmp_i[:, :]))
                    then(dve.tensor_scalar(tmp_i[:, :], src_i[:, :], 7, None, ALU.logical_shift_right))
                    then(dve.tensor_copy(blk[:, :], tmp_i[:, :]))
                    then(dve.memset(digits[:, :], 0.0))
                    dig = digits[:, :].rearrange("p (t k) -> p t k", k=DIGITS)
                    for k in range(BITS):
                        then(dve.tensor_scalar(tmp_i[:, :], src_i[:, :], 1 << k, None, ALU.bitwise_and))
                        then(dve.tensor_scalar(dig[:, :, k], tmp_i[:, :], 2.0 * SIGN / (1 << k), -SIGN,
                                               ALU.mult, ALU.add))
                    dve.wait_ge(proj_done, 2)
                    then(dve.tensor_copy(v[:, :, :], small[:, 0:2 * (R + 1)].rearrange("p (k r) -> p k r", k=2)))
                    then(dve.tensor_reduce(bias[:, :], bias_in[:, :].rearrange("p (k j) -> p k j", k=2), AX.X, ALU.add))
                    then(dve.tensor_tensor(bias[:, :], bias[:, :], v[:, :, R], ALU.add))
                    dve.wait_ge(proj_done, 2)
                    then(dve.tensor_copy(rel_t[:, :], small[0:R + 1, 128:128 + D]))

                    def onehots(g, u):
                        dve.wait_ge(hot_used, g + 1)
                        dve.tensor_tensor(hot_lo[:, u], mid(iota[:, :], [P, GT, P]),
                                          bcast(dlo[:, bass.ds(g * GT, GT)], [P, GT, P]), ALU.is_equal).then_inc(hot_ready, 1)
                        dve.tensor_tensor(hot_blk[:, u], mid(iota[:, 0:NB], [P, GT, NB]),
                                          bcast(dblk[:, bass.ds(g * GT, GT)], [P, GT, NB]), ALU.is_equal).then_inc(hot_ready, 1)

                    over_groups(dve, onehots)
                    dve.wait_ge(hot_used, UNROLL + NG)
                    dve.tensor_copy(count[:, :], hist[:, :]).then_inc(sums_ready, 1)
                    dve.wait_ge(sums_done, 1)
                    then(dve.tensor_copy(total[:, :], small[:, 256:256 + NB]))
                    then(dve.tensor_tensor_scan(tmp1[:, :], ones[:, 0:NB], total[:, :], 0.0, ALU.mult, ALU.add))
                    then(dve.tensor_tensor(tmp1[:, :], tmp1[:, :], total[:, :], ALU.subtract))
                    then(dve.tensor_tensor(start_f[:, :], tmp1[:, :], small[:, 320:320 + NB], ALU.add))
                    then(dve.tensor_tensor(end_f[:, :], start_f[:, :], count[:, :], ALU.add))
                    then(dve.tensor_scalar(end_f[:, :], end_f[:, :], -1.0, None, ALU.add))
                    then(dve.tensor_scalar(has[:, :], count[:, :], 0.0, None, ALU.is_gt))
                    for b in range(NB):
                        then(dve.tensor_scalar(hot_f[:, :], bounds[:, :], end_f[:, b:b + 1], None,
                                               ALU.is_le))
                        then(dve.tensor_reduce(chunk_f[:, b:b + 1], hot_f[:, :], AX.X, ALU.add))
                    then(dve.tensor_scalar(chunk_f[:, :], chunk_f[:, :], -1.0, None, ALU.add))
                    then(dve.tensor_scalar(tmp1[:, :], chunk_f[:, :], float(W), None, ALU.mult))
                    then(dve.tensor_tensor(tmp1[:, :], start_f[:, :], tmp1[:, :], ALU.is_lt))
                    then(dve.tensor_tensor(tmp1[:, :], tmp1[:, :], has[:, :], ALU.mult))
                    then(dve.tensor_scalar(tmp2[:, :], chunk_f[:, :], float(P), None, ALU.subtract))
                    then(dve.tensor_tensor(tmp2[:, :], tmp2[:, :], tmp1[:, :], ALU.mult))
                    then(dve.tensor_scalar(carry_i[:, :], tmp2[:, :], float(P), None, ALU.add))
                    then(dve.tensor_scalar(tmp2[:, :], end_f[:, :], float(EP), None, ALU.subtract))
                    then(dve.tensor_tensor(tmp2[:, :], tmp2[:, :], has[:, :], ALU.mult))
                    then(dve.tensor_scalar(end_i[:, :], tmp2[:, :], float(EP), None, ALU.add))
                    then(dve.tensor_tensor(tmp2[:, :], start_f[:, :], has[:, :], ALU.mult))
                    then(dve.tensor_scalar(tmp1[:, :], has[:, :], -float(SKIP), float(SKIP), ALU.mult, ALU.add))
                    then(dve.tensor_tensor(start_i[:, :], tmp1[:, :], tmp2[:, :], ALU.add))

                @block.tensor
                def _(pe):
                    pe.wait_ge(small_in, 16 * 11)
                    pe.wait_ge(chain, 5)
                    for k in range(2):
                        last = pe.matmul(small[:, k * (R + 1):(k + 1) * (R + 1)],
                                         ew[:, k:k + 1].to_broadcast([D, P]), rel_aug[:, :], start=True, stop=True)
                    last.then_inc(proj_done, 1)
                    pe.transpose(small[0:R + 1, 128:128 + D], rel_aug[:, :], ident[0:D, 0:D]).then_inc(proj_done, 1)
                    pe.sem_inc(hot_used, UNROLL)

                    def add_group(g, u, start=False, stop=False):
                        pe.wait_ge(hot_ready, g * 2 + 2)
                        for t in range(GT):
                            last = pe.matmul(hist[:, :], hot_lo[:, u, t], hot_blk[:, u, t],
                                             start=start and t == 0, stop=stop and t == GT - 1)
                        last.then_inc(hot_used, 1)

                    accumulate(pe, add_group)
                    pe.wait_ge(sums_ready, 1)
                    pe.matmul(small[:, 256:256 + NB], ones[:, :], count[:, :], start=True, stop=True)
                    pe.matmul(small[:, 320:320 + NB], below[:, :], count[:, :], start=True, stop=True).then_inc(sums_done, 1)


        def chained(eng, semaphore):
            n = [0]

            def then(ins):
                ins.then_inc(semaphore, 1)
                n[0] += 1
                eng.wait_ge(semaphore, n[0])

            return then

        def norm_relu(tag):
            with phase() as c:
                mean = sb(f"mean{tag}", [P, NB], F32, c)
                var = sb(f"var{tag}", [P, NB], F32, c)
                sq = sb(f"sq{tag}", [P, NB, D], F32, c)
                chain, var_ready, std_ready = sem(f"n_chain{tag}"), sem(f"n_var{tag}"), sem(f"n_std{tag}")
                with nc.Block() as block:
                    @block.vector
                    def _(dve):
                        then = chained(dve, chain)
                        then(dve.tensor_reduce(mean[:, :], x_sb[:, :, :], AX.X, ALU.add))
                        then(dve.tensor_scalar(mean[:, :], mean[:, :], 1.0 / D, None, ALU.mult))
                        then(dve.tensor_tensor(h[:, :, :], x_sb[:, :, :], bcast(mean[:, :], [P, NB, D]), ALU.subtract))
                        then(dve.tensor_tensor(sq[:, :, :], h[:, :, :], h[:, :, :], ALU.mult))
                        then(dve.tensor_reduce(var[:, :], sq[:, :, :], AX.X, ALU.add))
                        dve.tensor_scalar(var[:, :], var[:, :], 1.0 / D, EPS, ALU.mult, ALU.add).then_inc(var_ready, 1)
                        dve.wait_ge(std_ready, 1)
                        then(dve.reciprocal(var[:, :], var[:, :]))
                        then(dve.tensor_tensor(h[:, :, :], h[:, :, :], bcast(var[:, :], [P, NB, D]), ALU.mult))
                        then(dve.tensor_scalar(h[:, :, :], h[:, :, :], 0.0, None, ALU.max))

                    @block.scalar
                    def _(act):
                        act.wait_ge(var_ready, 1)
                        act.activation(var[:, :], var[:, :], ACT.Sqrt).then_inc(std_ready, 1)

        def edge_terms():
            with phase() as c:
                att = sb("att", [P, UNROLL, GT, R], F32, c)
                prod = sb("prod", [P, 2, GT, R], F32, c)
                att_in = [sem(f"att_in{u}") for u in range(UNROLL)]
                prod_ready, terms = sem("prod_ready"), sem("terms")
                with nc.Block() as block:
                    @block.sync
                    def _(sp):
                        with sp.Fori(0, NG // UNROLL) as i:
                            for u in range(UNROLL):
                                g = i * UNROLL + u
                                sp.wait_ge(prod_ready, g * 2 + 2)
                                sp.dma_start(att[:, u], attr[:, bass.ds(g * GT, GT), :]).then_inc(att_in[u], 16)

                    @block.vector
                    def _(dve):
                        dve.sem_inc(prod_ready, 2 * UNROLL)
                        dve.sem_inc(terms, 1)
                        with dve.Fori(0, NG // UNROLL) as i:
                            for u in range(UNROLL):
                                g = i * UNROLL + u
                                dve.wait_ge(att_in[u], i * 16 + 16)
                                dve.wait_ge(terms, g * 2 + 1)
                                for k in range(2):
                                    ins = dve.tensor_tensor(prod[:, k], att[:, u], mid(v[:, k, 0:R], [P, GT, R]), ALU.mult)
                                    ins.then_inc(prod_ready, 1)
                                dve.wait_ge(prod_ready, g * 2 + (2 * UNROLL + 2))
                                for k in range(2):
                                    dve.tensor_reduce(z[k][:, bass.ds(g * GT, GT)], prod[:, k], AX.X, ALU.add).then_inc(terms, 1)
                        dve.wait_ge(terms, NG * 2 + 1)
                        for k in range(2):
                            dve.tensor_scalar(z[k][:, :], z[k][:, :], bias[:, k:k + 1], None, ALU.add)

        def project(tag, w, b, ai_w, aj_w, xn):
            with phase() as c:
                wb = sb(f"wb{tag}", [D, D + 1], F32, c)
                aij = sb(f"aij{tag}", [D, 2], F32, c)
                waug = sb(f"waug{tag}", [D + 1, D + 2], F32, c)
                ht = sb(f"ht{tag}", [D + 1, 7 * P], F32, c)
                wp = pb(f"wp{tag}", [P, 512], F32, c)
                hp = pb(f"hp{tag}", [P, 1024], F32, c)
                xp = pb(f"xp{tag}", [P, 512], F32, c)
                w_in, w_ready, w_copied = sem(f"p_win{tag}"), sem(f"p_w{tag}"), sem(f"p_wc{tag}")
                turned, ht_ready, x_ready, x_copied, stored = (sem(f"p_{n}{tag}") for n in ("t", "h", "x", "xc", "st"))
                with nc.Block() as block:
                    @block.sync
                    def _(sp):
                        sp.dma_start(wb[:, 0:D], w).then_inc(w_in, 16)
                        sp.dma_start(wb[:, D:D + 1], bass_col(b)).then_inc(w_in, 16)
                        sp.dma_start(aij[:, 0:1], ai_w.rearrange("a d -> d a")).then_inc(w_in, 16)
                        sp.dma_start(aij[:, 1:2], aj_w.rearrange("a d -> d a")).then_inc(w_in, 16)
                        sp.wait_ge(x_copied, NB // 7)
                        sp.dma_start(table[0:NP, :].rearrange("(b p) f -> p b f", p=P), xn[:, :, :]).then_inc(stored, 16)
                        sp.wait_ge(stored, 16)

                    @block.tensor
                    def _(pe):
                        pe.wait_ge(w_in, 64)
                        pe.transpose(wp[0:D + 1, 0:D], wb[:, :], ident[0:D, 0:D])
                        pe.matmul(wp[0:D + 1, D:D + 2], wb[:, :], aij[:, :], start=True, stop=True).then_inc(w_ready, 1)
                        for j in range(NB // 7):
                            if j:
                                pe.wait_ge(ht_ready, j)
                            for b7 in range(7):
                                last = pe.transpose(hp[0:D, b7 * P:(b7 + 1) * P], h[:, 7 * j + b7, :], ident[:, :])
                            last.then_inc(turned, 1)
                            pe.wait_ge(ht_ready, j + 1)
                            if j == 0:
                                pe.wait_ge(w_copied, 2)
                            else:
                                pe.wait_ge(x_copied, j)
                            for b7 in range(7):
                                last = pe.matmul(xp[:, b7 * (D + 2):(b7 + 1) * (D + 2)], ht[:, b7 * P:(b7 + 1) * P],
                                                 waug[:, :], start=True, stop=True)
                            last.then_inc(x_ready, 1)

                    @block.scalar
                    def _(act):
                        for j in range(NB // 7):
                            act.wait_ge(turned, j + 1)
                            if j:
                                act.wait_ge(x_ready, j)
                            act.activation(ht[0:D, :], hp[0:D, 0:7 * P], ACT.Copy).then_inc(ht_ready, 1)

                    @block.vector
                    def _(dve):
                        dve.memset(ht[D:D + 1, :], 1.0).then_inc(w_copied, 1)
                        dve.memset(xn[:, :, D + 2:D + 3], 0.0)
                        dve.wait_ge(w_ready, 1)
                        dve.tensor_copy(waug[:, :], wp[0:D + 1, 0:D + 2]).then_inc(w_copied, 1)
                        for j in range(NB // 7):
                            dve.wait_ge(x_ready, j + 1)
                            dve.tensor_copy(xn[:, 7 * j:7 * j + 7, 0:D + 2],
                                            xp[:, 0:7 * (D + 2)].rearrange("p (b f) -> p b f", f=D + 2)).then_inc(x_copied, 1)

        def expand(tag, xn, zk):
            with phase() as c:
                at_start = sb(f"at_start{tag}", [P, W], F32, c)
                first = sb(f"first{tag}", [P, TW], F32, c)
                scattered, firsts, loaded, chain = (sem(f"e_{n}{tag}") for n in ("sc", "fi", "lo", "ch"))
                with nc.Block() as block:
                    @block.gpsimd
                    def _(pool):
                        for b in range(NB):
                            pool.indirect_dma_start(a_starts, bass.IndirectOffsetOnAxis(ap=start_i[:, b:b + 1], axis=0),
                                                    xn[:, b, D:D + 1], None, bounds_check=EP - 1,
                                                    oob_is_err=False).then_inc(scattered, 16)
                        pool.indirect_dma_start(first[:, :], None, table,
                                                bass.IndirectOffsetOnAxis(ap=dst0_i[:, 0:1], axis=0)).then_inc(firsts, 16)

                    @block.sync
                    def _(sp):
                        sp.wait_ge(scattered, 16 * NB)
                        sp.dma_start(at_start[:, :], a_starts.rearrange("(p t) f -> p (t f)", p=P)).then_inc(loaded, 16)

                    @block.vector
                    def _(dve):
                        then = chained(dve, chain)
                        dve.wait_ge(loaded, 16)
                        dve.wait_ge(firsts, 16)
                        then(dve.tensor_copy(at_start[:, 0:1], first[:, D:D + 1]))
                        then(dve.tensor_tensor_scan(at_start[:, :], cont[:, :], at_start[:, :], 0.0, ALU.mult, ALU.add))
                        then(dve.tensor_tensor(zk[:, :], zk[:, :], at_start[:, :], ALU.add))

        def tile_maxima(tag, values, peak):
            with phase() as c:
                dslot = sb(f"dslot{tag}", [P, UNROLL, GT, DIGITS], BF16, c)
                bits = sb(f"bits{tag}", [DIGITS, UNROLL, GT * P], BF16, c)
                slot = sb(f"slot{tag}", [P, UNROLL, GT], F32, c)
                top = sb(f"top{tag}", [P, UNROLL, GT], F32, c)
                hot_lo = sb(f"m_lo{tag}", [P, UNROLL, GT, P], F32, c)
                hot_blk = sb(f"m_blk{tag}", [P, UNROLL, GT, NB], F32, c)
                hot_big = sb(f"m_big{tag}", [P, UNROLL, GT, NB], F32, c)
                hot_val = sb(f"m_val{tag}", [P, UNROLL, GT, NB], F32, c)
                best = sb(f"best{tag}", [P, NB], F32, c)
                minus_big = sb(f"mb{tag}", [1, GT * NB], F32, c)
                column = sb(f"column{tag}", [1, GT, P], F32, c)
                bp = [pb(f"bp{tag}{j}", [DIGITS, GT * P], BF16, c) for j in range(2)]
                mp = [pb(f"mp{tag}{j}", [P, GT, P], F32, c) for j in range(2)]
                gp = [pb(f"gp{tag}{j}", [P, GT, NB], F32, c) for j in range(2)]
                dig_ready = sem(f"m_dr{tag}")
                names = ("set", "turned", "bits", "pairs", "top", "lo", "big", "val", "grid", "best", "peak")
                ready, turned, bits_ready, pairs, topped, lo_ready, big_ready, val_ready, grid, best_ready, peaked = (
                    sem(f"m_{n}{tag}") for n in names)
                dig = digits[:, :].rearrange("p (t k) -> p t k", k=DIGITS)
                with nc.Block() as block:
                    @block.tensor
                    def _(pe):
                        pe.wait_ge(ready, 2)

                        def turn(g, u):
                            pe.wait_ge(bits_ready, g + 1)
                            pe.wait_ge(dig_ready, g + 1)
                            for t in range(GT):
                                last = pe.transpose(bp[u % 2][:, t * P:(t + 1) * P], dslot[:, u, t], identb[:, :])
                            last.then_inc(turned, 1)

                        def pair(g, u):
                            pe.wait_ge(bits_ready, g + 3)
                            pe.wait_ge(topped, g + 1)
                            flat = mp[u % 2][:, :, :].rearrange("p t j -> p (t j)")
                            pe.matmul(flat, ones[0:1, :], minus[0:1, :], start=True, stop=False)
                            for t in range(GT):
                                pe.matmul(mp[u % 2][:, t], bits[:, u, t * P:(t + 1) * P], bits[:, u, t * P:(t + 1) * P],
                                          start=False, stop=False)
                            if values is None:
                                last = pe.matmul(flat, ones[0:1, :], column[0:1, :, :].rearrange("p t j -> p (t j)"),
                                                 start=False, stop=True)
                            else:
                                for t in range(GT):
                                    last = pe.matmul(mp[u % 2][:, t], slot[:, u, t:t + 1].to_broadcast([P, P]),
                                                     ident[:, :], start=False, stop=t == GT - 1)
                            last.then_inc(pairs, 1)

                        def scatter(g, u):
                            pe.wait_ge(lo_ready, g + 1)
                            pe.wait_ge(big_ready, g + 1)
                            pe.wait_ge(val_ready, g + 1)
                            pe.wait_ge(best_ready, g + 1)
                            pe.matmul(gp[u % 2][:, :, :].rearrange("p t b -> p (t b)"), ones[0:1, :], minus_big[0:1, :],
                                      start=True, stop=False)
                            for t in range(GT):
                                pe.matmul(gp[u % 2][:, t], hot_lo[:, u, t], hot_big[:, u, t], start=False, stop=False)
                                last = pe.matmul(gp[u % 2][:, t], hot_lo[:, u, t], hot_val[:, u, t], start=False,
                                                 stop=t == GT - 1)
                            last.then_inc(grid, 1)

                        def second(g, u):
                            pair(g, u)
                            if values is not None:
                                scatter(g, u)

                        over_groups_skewed(pe, turn, second)

                    @block.gpsimd
                    def _(pool):
                        pool.sem_inc(turned, UNROLL)

                        def copy_digits(g, u):
                            pool.wait_ge(turned, g + 1)
                            pool.wait_ge(ready, 1)
                            pool.tensor_copy(dslot[:, u], dig[:, bass.ds(g * GT, GT), :]).then_inc(dig_ready, 1)

                        over_groups(pool, copy_digits)

                    @block.scalar
                    def _(act):
                        act.sem_inc(bits_ready, 2)

                        def copy_bits(g, u):
                            act.wait_ge(turned, g + (UNROLL + 1))
                            if values is None:
                                act.wait_ge(topped, g + 1 )
                            else:
                                act.wait_ge(grid, g + 1)
                            if values is not None:
                                act.activation(slot[:, u], values[:, bass.ds(g * GT, GT)], ACT.Copy)
                            act.activation(bits[:, u], bp[u % 2][:, :], ACT.Copy).then_inc(bits_ready, 1)

                        def scale_big(g, u):
                            act.wait_ge(lo_ready, g + 1)
                            act.activation(hot_big[:, u], hot_blk[:, u], ACT.Copy, scale=BIG).then_inc(big_ready, 1)

                        if values is None:
                            over_groups(act, copy_bits)
                        else:
                            over_groups_skewed(act, copy_bits, scale_big)

                    @block.vector
                    def _(dve):
                        dve.memset(minus_big[:, :], -BIG).then_inc(ready, 1)
                        dve.tensor_copy(column[:, :, :], mid(iota[0:1, :], [1, GT, P])).then_inc(ready, 1)
                        dve.sem_inc(topped, 2)
                        if values is not None:
                            dve.memset(peak[:, :], -BIG).then_inc(ready, 1)
                            dve.wait_ge(ready, 3)
                            dve.sem_inc(best_ready, 2)
                            dve.sem_inc(grid, UNROLL)
                            dve.sem_inc(peaked, 1)

                        def leaders(g, u):
                            dve.wait_ge(pairs, g + 1)
                            dve.tensor_reduce(lead[:, bass.ds(g * GT, GT)], mp[u % 2][:, :, :], AX.X, ALU.max).then_inc(topped, 1)

                        def onehots(g, u):
                            dve.wait_ge(grid, g + 1)
                            dve.tensor_tensor(hot_lo[:, u], mid(iota[:, :], [P, GT, P]),
                                              bcast(lo[:, bass.ds(g * GT, GT)], [P, GT, P]), ALU.is_equal)
                            dve.tensor_tensor(hot_blk[:, u], mid(iota[:, 0:NB], [P, GT, NB]),
                                              bcast(lead[:, bass.ds(g * GT, GT)], [P, GT, NB]), ALU.is_equal).then_inc(lo_ready, 1)
                            dve.wait_ge(pairs, g + 1)
                            dve.tensor_reduce(top[:, u], mp[u % 2][:, :, :], AX.X, ALU.max).then_inc(topped, 1)
                            dve.wait_ge(topped, g + 3)
                            dve.wait_ge(lo_ready, g + 1)
                            dve.tensor_tensor(hot_val[:, u], hot_blk[:, u], bcast(top[:, u], [P, GT, NB]), ALU.mult).then_inc(val_ready, 1)

                        def maxima(g, u):
                            dve.wait_ge(grid, g + 5)
                            dve.wait_ge(peaked, g + 1)
                            dve.tensor_reduce(best[:, :], gp[u % 2][:, :, :].rearrange("p t b -> p b t"), AX.X, ALU.max).then_inc(best_ready, 1)
                            dve.wait_ge(best_ready, g + 3)
                            dve.tensor_tensor(peak[:, :], peak[:, :], best[:, :], ALU.max).then_inc(peaked, 1)

                        if values is None:
                            over_groups(dve, leaders)
                            then = chained(dve, peaked)
                            dve.wait_ge(topped, NG + 2)
                            then(dve.tensor_scalar(lead[:, :], lead[:, :], lane[:, 0:1], None, ALU.is_equal))
                            then(dve.scalar_tensor_tensor(lead[:, :], blk[:, :], 1.0, lead[:, :], ALU.add, ALU.mult))
                            then(dve.tensor_scalar(lead[:, :], lead[:, :], -1.0, None, ALU.add))
                        else:
                            over_groups_skewed(dve, onehots, maxima)

        def exponentials(tag, zk, xn, peak):
            with phase() as c:
                pair = sb(f"pair{tag}", [P, 2, NB], F32, c)
                hot_lo = sb(f"x_lo{tag}", [P, UNROLL, GT, P], F32, c)
                hot_t = sb(f"x_t{tag}", [P, 2, GT, P], F32, c)
                hot_blk = sb(f"x_blk{tag}", [P, UNROLL, GT, NB], F32, c)
                picked = sb(f"picked{tag}", [P, GT, 2, NB], F32, c)
                found = sb(f"found{tag}", [P, UNROLL, GT, 2], F32, c)
                logit = sb(f"logit{tag}", [P, UNROLL, GT], F32, c)
                sloped = sb(f"sloped{tag}", [P, UNROLL, GT], F32, c)
                hot_ex = sb(f"x_ex{tag}", [P, UNROLL, GT, NB], F32, c)
                tmp = sb(f"x_tmp{tag}", [P, NB], F32, c)
                tp = [pb(f"tp{tag}{j}", [P, GT, P], F32, c) for j in range(2)]
                fp = [pb(f"fp{tag}{j}", [P, GT, 2, NB], F32, c) for j in range(2)]
                sums = pb(f"sums{tag}", [P, NB], F32, c)
                names = ("pr", "lo", "tu", "t", "fo", "pi", "chain", "ex", "he", "ac", "st", "inv")
                pair_ready, lo_ready, turned, t_ready, found_ready, picked_ready, chain, ex_ready, hot_ready, \
                    added, stored, inverted = (sem(f"x_{n}{tag}") for n in names)
                with nc.Block() as block:
                    @block.vector
                    def _(dve):
                        dve.tensor_copy(pair[:, 0], xn[:, :, D + 1]).then_inc(pair_ready, 1)
                        dve.tensor_tensor(tmp[:, :], xn[:, :, D + 1], peak[:, :], ALU.add).then_inc(pair_ready, 1)
                        dve.wait_ge(pair_ready, 2)
                        dve.scalar_tensor_tensor(pair[:, 1], tmp[:, :], 0.01, tmp[:, :], ALU.mult, ALU.max).then_inc(pair_ready, 1)
                        dve.wait_ge(pair_ready, 3)
                        dve.sem_inc(chain, 1)
                        dve.sem_inc(picked_ready, 2)
                        dve.sem_inc(found_ready, 2)

                        def onehots(g, u):
                            dve.wait_ge(added, g + 1)
                            dve.tensor_tensor(hot_lo[:, u], mid(iota[:, :], [P, GT, P]),
                                              bcast(lo[:, bass.ds(g * GT, GT)], [P, GT, P]), ALU.is_equal)
                            dve.tensor_tensor(hot_blk[:, u], mid(iota[:, 0:NB], [P, GT, NB]),
                                              bcast(blk[:, bass.ds(g * GT, GT)], [P, GT, NB]), ALU.is_equal).then_inc(lo_ready, 1)

                        def logits(g, u):
                            dve.wait_ge(found_ready, g + 3)
                            dve.wait_ge(lo_ready, g + 1)
                            dve.wait_ge(chain, g * 4 + 1)
                            hot2 = hot_blk[:, u].unsqueeze(2).to_broadcast([P, GT, 2, NB])
                            dve.tensor_tensor(picked[:, :, :, :], fp[u % 2][:, :, :, :], hot2, ALU.mult).then_inc(picked_ready, 1)
                            dve.wait_ge(picked_ready, g + 3)
                            dve.tensor_reduce(found[:, u], picked[:, :, :, :], AX.X, ALU.add).then_inc(chain, 1)
                            dve.wait_ge(chain, g * 4 + 2)
                            dve.tensor_tensor(logit[:, u], found[:, u, :, 0], zk[:, bass.ds(g * GT, GT)], ALU.add).then_inc(chain, 1)
                            dve.wait_ge(chain, g * 4 + 3)
                            dve.scalar_tensor_tensor(sloped[:, u], logit[:, u], 0.01, logit[:, u], ALU.mult, ALU.max).then_inc(chain, 1)
                            dve.wait_ge(chain, g * 4 + 4)
                            dve.tensor_tensor(logit[:, u], sloped[:, u], found[:, u, :, 1], ALU.subtract).then_inc(chain, 1)

                        def weigh(g, u):
                            dve.wait_ge(ex_ready, g + 1)
                            dve.tensor_tensor(hot_ex[:, u], hot_blk[:, u], bcast(zk[:, bass.ds(g * GT, GT)], [P, GT, NB]),
                                              ALU.mult).then_inc(hot_ready, 1)

                        onehots(0, 0)
                        onehots(1, 1)
                        logits(0, 0)
                        with dve.Fori(0, NG // UNROLL - 1) as i:
                            for u in range(UNROLL):
                                g = i * UNROLL + u
                                onehots(g + 2, (u + 2) % UNROLL)
                                logits(g + 1, (u + 1) % UNROLL)
                                weigh(g, u)
                        for g in range(NG - UNROLL, NG):
                            if g + 2 < NG:
                                onehots(g + 2, (g + 2) % UNROLL)
                            if g + 1 < NG:
                                logits(g + 1, (g + 1) % UNROLL)
                            weigh(g, g % UNROLL)
                        dve.wait_ge(added, NG + 4)
                        dve.tensor_scalar(tmp[:, :], sums[:, :], 1e-16, None, ALU.add).then_inc(inverted, 1)
                        dve.wait_ge(inverted, 1)
                        dve.reciprocal(xn[:, :, D + 2], tmp[:, :]).then_inc(inverted, 1)

                    @block.tensor
                    def _(pe):
                        pe.wait_ge(pair_ready, 3)
                        pe.sem_inc(added, 4)

                        def turn(g, u):
                            pe.wait_ge(lo_ready, g + 1)
                            pe.wait_ge(t_ready, g + 1)
                            for t in range(GT):
                                last = pe.transpose(tp[u % 2][:, t], hot_lo[:, u, t], ident[:, :])
                            last.then_inc(turned, 1)

                        def find(g, u):
                            pe.wait_ge(t_ready, g + 3)
                            pe.wait_ge(picked_ready, g + 1)
                            for t in range(GT):
                                last = pe.matmul(fp[u % 2][:, t, :, :].rearrange("p k b -> p (k b)"), hot_t[:, u % 2, t],
                                                 pair[:, :, :].rearrange("p k b -> p (k b)"), start=True, stop=True)
                            last.then_inc(found_ready, 1)

                        def add(g, u, start=False, stop=False):
                            pe.wait_ge(hot_ready, g + 1)
                            for t in range(GT):
                                last = pe.matmul(sums[:, :], hot_lo[:, u, t], hot_ex[:, u, t],
                                                 start=start and t == 0, stop=stop and t == GT - 1)
                            last.then_inc(added, 1)

                        turn(0, 0)
                        find(0, 0)
                        turn(1, 1)
                        find(1, 1)
                        for g in range(UNROLL):
                            turn(g + 2, (g + 2) % UNROLL)
                            find(g + 2, (g + 2) % UNROLL)
                            add(g, g, start=g == 0)
                        with pe.Fori(0, NG // UNROLL - 2) as i:
                            for u in range(UNROLL):
                                g = i * UNROLL + (UNROLL + u)
                                turn(g + 2, (u + 2) % UNROLL)
                                find(g + 2, (u + 2) % UNROLL)
                                add(g, u)
                        for g in range(NG - UNROLL, NG):
                            if g + 2 < NG:
                                turn(g + 2, (g + 2) % UNROLL)
                                find(g + 2, (g + 2) % UNROLL)
                            add(g, g % UNROLL, stop=g == NG - 1)

                    @block.scalar
                    def _(act):
                        act.sem_inc(t_ready, 2)

                        def copy_hot(g, u):
                            act.wait_ge(turned, g + 1)
                            act.wait_ge(found_ready, g + 1)
                            act.activation(hot_t[:, u % 2], tp[u % 2][:, :, :], ACT.Copy).then_inc(t_ready, 1)

                        def exps(g, u):
                            act.wait_ge(chain, g * 4 + 5)
                            act.activation(zk[:, bass.ds(g * GT, GT)], logit[:, u], ACT.Exp).then_inc(ex_ready, 1)

                        over_groups_skewed(act, copy_hot, exps)

                    @block.sync
                    def _(sp):
                        sp.wait_ge(inverted, 2)
                        sp.dma_start(table[0:NP, :].rearrange("(b p) f -> p b f", p=P), xn[:, :, :]).then_inc(stored, 16)
                        sp.wait_ge(stored, 16)

        def chunk_carries(tag, last, width, peak, dest):
            with phase() as c:
                seg = sb(f"seg{tag}", [width, 3, P], F32, c)
                run = sb(f"run{tag}", [width, P], F32, c)
                carry = sb(f"carry{tag}", [width, P], F32, c)
                pen = sb(f"pen{tag}", [width, P], F32, c)
                back = sb(f"back{tag}", [P, width], F32, c)
                sp_full = pb(f"segp{tag}", [P, 512], F32, c)
                sp_ = sp_full[0:width, :]
                turned, chain, copied, stored = (sem(f"k_{n}{tag}") for n in ("tu", "ch", "co", "st"))
                chain_steps = 7 if peak else 4
                with nc.Block() as block:
                    @block.tensor
                    def _(pe):
                        for k, m in enumerate((last, through[:, 0:1].to_broadcast([P, width]),
                                               strad[:, 0:1].to_broadcast([P, width]))):
                            ins = pe.transpose(sp_[:, k * P:(k + 1) * P], m, ident[:, :])
                        ins.then_inc(turned, 1)
                        pe.wait_ge(chain, chain_steps)
                        pe.transpose(sp_full[:, 0:width], carry[:, :], ident[0:width, 0:width]).then_inc(turned, 1)

                    @block.vector
                    def _(dve):
                        then = chained(dve, chain)
                        dve.wait_ge(turned, 1)
                        then(dve.tensor_copy(seg[:, :, :], sp_[:, 0:3 * P].rearrange("f (k p) -> f k p", k=3)))
                        if peak:
                            then(dve.tensor_scalar(pen[:, :], seg[:, 1], BIG, -BIG, ALU.mult, ALU.add))
                            then(dve.tensor_tensor_scan(run[:, :], pen[:, :], seg[:, 0], -BIG, ALU.add, ALU.max))
                        else:
                            then(dve.tensor_tensor_scan(run[:, :], seg[:, 1], seg[:, 0], 0.0, ALU.mult, ALU.add))
                        then(dve.memset(carry[:, 0:1], -BIG if peak else 0.0))
                        then(dve.tensor_tensor(carry[:, 1:P], run[:, 0:P - 1], seg[:, 2, 1:P], ALU.mult))
                        if peak:
                            then(dve.tensor_scalar(pen[:, :], seg[:, 2], BIG, -BIG, ALU.mult, ALU.add))
                            then(dve.tensor_tensor(carry[:, 1:P], carry[:, 1:P], pen[:, 1:P], ALU.add))
                        dve.wait_ge(turned, 2)
                        dve.tensor_copy(back[:, :], sp_full[:, 0:width]).then_inc(copied, 1)

                    @block.sync
                    def _(sp):
                        sp.wait_ge(copied, 1)
                        sp.dma_start(dest[0:P, 0:width], back[:, :]).then_inc(stored, 16)
                        sp.wait_ge(stored, 16)

        def messages(tag, ex):
            with phase() as c:
                got = sb(f"got{tag}", [P, UNROLL, GT, TW], F32, c)
                att = sb(f"s_att{tag}", [P, UNROLL, GT, R], F32, c)
                msg = sb(f"msg{tag}", [P, UNROLL, GT, M], F32, c)
                acc = sb(f"acc{tag}", [P, UNROLL, GT, M], F32, c)
                gathered = [sem(f"s_ga{tag}{u}") for u in range(UNROLL)]
                att_in = [sem(f"s_at{tag}{u}") for u in range(UNROLL)]
                stored = [sem(f"s_st{tag}{u}") for u in range(UNROLL)]
                index = sb(f"index{tag}", [P, UNROLL, GT], I32, c)
                index_ready, begun = sem(f"s_ix{tag}"), sem(f"s_be{tag}")
                weighed, msg_ready, summed = sem(f"s_we{tag}"), sem(f"s_ms{tag}"), sem(f"s_su{tag}")
                with nc.Block() as block:
                    @block.gpsimd
                    def _(pool):
                        with pool.Fori(0, NG // UNROLL) as i:
                            for u in range(UNROLL):
                                g = i * UNROLL + u
                                pool.wait_ge(index_ready, g + 1)
                                pool.sem_inc(begun, 1)
                                for t in range(GT):
                                    pool.indirect_dma_start(got[:, u, t], None, table, bass.IndirectOffsetOnAxis(
                                        ap=index[:, u, t:t + 1], axis=0)).then_inc(gathered[u], 16)

                    @block.sync
                    def _(sp):
                        with sp.Fori(0, NG // UNROLL) as i:
                            for u in range(UNROLL):
                                g = i * UNROLL + u
                                sp.wait_ge(msg_ready, g * 2 + 2)
                                sp.dma_start(att[:, u], attr[:, bass.ds(g * GT, GT), :]).then_inc(att_in[u], 16)

                    @block.vector
                    def _(dve):
                        dve.sem_inc(msg_ready, 2 * UNROLL)
                        dve.memset(acc[:, UNROLL - 1, GT - 1], 0.0).then_inc(summed, 1)

                        def group(g, u, i=None):
                            dve.wait_ge(gathered[u], 16 * GT if i is None else i * (16 * GT) + 16 * GT)
                            dve.wait_ge(att_in[u], 16 if i is None else i * 16 + 16)
                            dve.wait_ge(summed, g * GT + 1)
                            w = msg[:, u, :, M - 1]
                            dve.tensor_tensor(w, got[:, u, :, D + 2], ex[:, bass.ds(g * GT, GT)], ALU.mult).then_inc(weighed, 1)
                            dve.wait_ge(weighed, g + 1)
                            dve.tensor_tensor(msg[:, u, :, 0:D], got[:, u, :, 0:D], bcast(w, [P, GT, D]), ALU.mult).then_inc(msg_ready, 1)
                            dve.tensor_tensor(msg[:, u, :, D:D + R], att[:, u], bcast(w, [P, GT, R]), ALU.mult).then_inc(msg_ready, 1)
                            dve.wait_ge(msg_ready, g * 2 + (2 * UNROLL + 2))
                            if i is not None:
                                dve.wait_ge(stored[u], i * 16)
                            for t in range(GT):
                                before = acc[:, u, t - 1] if t else acc[:, (u - 1) % UNROLL, GT - 1]
                                if t:
                                    dve.wait_ge(summed, g * GT + t + 1)
                                dve.scalar_tensor_tensor(acc[:, u, t], before, cont[:, bass.ds(g * GT + t, 1)], msg[:, u, t],
                                                         ALU.mult, ALU.add).then_inc(summed, 1)

                        for u in range(UNROLL):
                            group(u, u)
                        with dve.Fori(1, NG // UNROLL) as i:
                            for u in range(UNROLL):
                                group(i * UNROLL + u, u, i)

                    @block.scalar
                    def _(act):
                        wide = rows[0:EP, :].rearrange("(p t) f -> p t f", p=P)

                        def indices(g, u):
                            act.wait_ge(msg_ready, g * 2 + 2)
                            act.activation(index[:, u], src_i[:, bass.ds(g * GT, GT)], ACT.Copy).then_inc(index_ready, 1)

                        def store(g, u):
                            act.wait_ge(summed, g * GT + (GT + 1))
                            act.dma_start(wide[:, bass.ds(g * GT, GT), :], acc[:, u]).then_inc(stored[u], 16)

                        over_groups_ahead(act, indices, store)
                        for u in range(UNROLL):
                            act.wait_ge(stored[u], 16 * (NG // UNROLL))
                chunk_carries(f"s{tag}", acc[:, UNROLL - 1, GT - 1], M, False, carries)

        def node_rows(tag, source, carried, width, dest, extra):
            with phase() as c:
                fetched = sem(f"r_fe{tag}")
                with nc.Block() as block:
                    @block.gpsimd
                    def _(pool):
                        for b in range(NB):
                            pool.indirect_dma_start(dest[:, b], None, source, bass.IndirectOffsetOnAxis(
                                ap=end_i[:, b:b + 1], axis=0)).then_inc(fetched, 16)
                            pool.indirect_dma_start(extra[:, b], None, carried, bass.IndirectOffsetOnAxis(
                                ap=carry_i[:, b:b + 1], axis=0)).then_inc(fetched, 16)
                        pool.wait_ge(fetched, 32 * NB)

        def convolved(tag):
            with phase() as c:
                agg = sb(f"agg{tag}", [P, NB, M], F32, c)
                more = sb(f"more{tag}", [P, NB, M], F32, c)
                et = sb(f"et{tag}", [R + 1, 7 * P], F32, c)
                tp = pb(f"ctp{tag}", [R + 1, 1024], F32, c)
                ep = pb(f"cep{tag}", [P, 512], F32, c)
                node_rows(tag, rows, carries, M, agg, more)
                summed, turned, copied, e_ready, added = (sem(f"c_{n}{tag}") for n in ("su", "tu", "co", "e", "ad"))
                with nc.Block() as block:
                    @block.vector
                    def _(dve):
                        dve.tensor_tensor(agg[:, :, :], agg[:, :, :], more[:, :, :], ALU.add).then_inc(summed, 1)
                        dve.wait_ge(summed, 1)
                        for j in range(NB // 7):
                            part = slice(7 * j, 7 * j + 7)
                            dve.wait_ge(e_ready, j + 1)
                            dve.tensor_tensor(h[:, part, :], agg[:, part, 0:D], ep[:, 0:7 * D].rearrange("p (b f) -> p b f", f=D),
                                              ALU.add).then_inc(added, 1)
                        dve.wait_ge(added, NB // 7)
                        dve.tensor_scalar(h[:, :, :], h[:, :, :], 0.0, None, ALU.max)

                    @block.tensor
                    def _(pe):
                        pe.wait_ge(summed, 1)
                        for j in range(NB // 7):
                            if j:
                                pe.wait_ge(copied, j)
                            for b7 in range(7):
                                last = pe.transpose(tp[:, b7 * P:(b7 + 1) * P], agg[:, 7 * j + b7, D:M], ident[:, :])
                            last.then_inc(turned, 1)
                            pe.wait_ge(copied, j + 1)
                            if j:
                                pe.wait_ge(added, j)
                            for b7 in range(7):
                                last = pe.matmul(ep[:, b7 * D:(b7 + 1) * D], et[:, b7 * P:(b7 + 1) * P], rel_t[:, :],
                                                 start=True, stop=True)
                            last.then_inc(e_ready, 1)

                    @block.scalar
                    def _(act):
                        for j in range(NB // 7):
                            act.wait_ge(turned, j + 1)
                            if j:
                                act.wait_ge(e_ready, j)
                            act.activation(et[:, :], tp[:, 0:7 * P], ACT.Copy).then_inc(copied, 1)

        norm_relu("a")
        edge_terms()
        tile_maxima("l", None, None)
        for k, (w, b, ai_w, aj_w) in enumerate(((c1_w, c1_b, c1_ai_w, c1_aj_w), (c2_w, c2_b, c2_ai_w, c2_aj_w))):
            with phase() as c:
                xn = sb(f"xn{k}", [P, NB, TW], F32, c)
                peak = sb(f"peak{k}", [P, NB], F32, c)
                project(k, w, b, ai_w, aj_w, xn)
                expand(k, xn, z[k])
                tile_maxima(k, z[k], peak)
                exponentials(k, z[k], xn, peak)
            messages(k, z[k])
            convolved(k)
        with phase() as c:
            with nc.Block() as block:
                @block.vector
                def _(dve):
                    dve.tensor_tensor(x_sb[:, :, :], x_sb[:, :, :], h[:, :, :], ALU.add)
        norm_relu("b")

        w2_sb = sb("w2_sb", [2 * D, D], F32)
        b2_sb = sb("b2_sb", [P, D], F32)
        with phase() as c:
            wt = sb("wt", [D + 1, 2, D], F32, c)
            ht = sb("w_ht", [D + 1, 7 * P], F32, c)
            ab = sb("ab", [P, NB, 2, D], F32, c)
            hp = pb("w_hp", [P, 1024], F32, c)
            xp = pb("w_xp", [P, 1024], F32, c)
            w_in, w_ready, turned, ht_ready, x_ready, x_copied, stored = (sem(f"w_{n}") for n in ("in", "re", "tu", "ht", "xr", "xc", "st"))
            starts, firsts = sem("w_starts"), sem("w_firsts")
            first = sb("w_first", [P, D], F32, c)
            with nc.Block() as block:
                @block.sync
                def _(sp):
                    sp.dma_start(wt[0:D, 0], w1[0:D, :]).then_inc(w_in, 16)
                    sp.dma_start(wt[0:D, 1], w1[D:2 * D, :]).then_inc(w_in, 16)
                    sp.dma_start(wt[D:D + 1, 0], b1.rearrange("(a d) -> a d", a=1)).then_inc(w_in, 16)
                    sp.dma_start(w2_sb[0:D, :], w2).then_inc(w_in, 16)
                    sp.dma_start(w2_sb[D:2 * D, :], w2).then_inc(w_in, 16)
                    sp.dma_start(b2_sb[:, :], b2.partition_broadcast(P)).then_inc(w_in, 16)
                    sp.wait_ge(x_copied, NB // 7)
                    sp.dma_start(a_table[0:NP, :].rearrange("(b p) f -> p b f", p=P), ab[:, :, 0]).then_inc(stored, 16)
                    sp.dma_start(b_table[0:NP, :].rearrange("(b p) f -> p b f", p=P), ab[:, :, 1]).then_inc(stored, 16)
                    sp.wait_ge(stored, 32)
                    sp.wait_ge(firsts, 16)
                    sp.wait_ge(starts, 16 * NB)
                    sp.dma_start(row_starts.rearrange("(p t) f -> p t f", p=P)[:, 0, :], first[:, :]).then_inc(stored, 16)
                    sp.wait_ge(stored, 48)

                @block.gpsimd
                def _(pool):
                    pool.wait_ge(x_copied, NB // 7)
                    for b in range(NB):
                        pool.indirect_dma_start(row_starts, bass.IndirectOffsetOnAxis(ap=start_i[:, b:b + 1], axis=0),
                                                ab[:, b, 0], None, bounds_check=EP - 1, oob_is_err=False).then_inc(starts, 16)
                    pool.wait_ge(stored, 32)
                    pool.indirect_dma_start(first[:, :], None, a_table, bass.IndirectOffsetOnAxis(
                        ap=dst0_i[:, 0:1], axis=0)).then_inc(firsts, 16)

                @block.tensor
                def _(pe):
                    for j in range(NB // 7):
                        if j:
                            pe.wait_ge(ht_ready, j)
                        for b7 in range(7):
                            last = pe.transpose(hp[0:D, b7 * P:(b7 + 1) * P], h[:, 7 * j + b7, :], ident[:, :])
                        last.then_inc(turned, 1)
                        pe.wait_ge(ht_ready, j + 1)
                        pe.wait_ge(w_ready, 3)
                        if j:
                            pe.wait_ge(x_copied, j)
                        for b7 in range(7):
                            last = pe.matmul(xp[:, b7 * 2 * D:(b7 + 1) * 2 * D], ht[:, b7 * P:(b7 + 1) * P],
                                             wt[:, :, :].rearrange("p k f -> p (k f)"), start=True, stop=True)
                        last.then_inc(x_ready, 1)

                @block.scalar
                def _(act):
                    for j in range(NB // 7):
                        act.wait_ge(turned, j + 1)
                        if j:
                            act.wait_ge(x_ready, j)
                        act.activation(ht[0:D, :], hp[0:D, 0:7 * P], ACT.Copy).then_inc(ht_ready, 1)

                @block.vector
                def _(dve):
                    dve.memset(ht[D:D + 1, :], 1.0).then_inc(w_ready, 1)
                    dve.memset(wt[D:D + 1, 1], 0.0).then_inc(w_ready, 1)
                    dve.wait_ge(w_in, 96)
                    dve.tensor_tensor(wt[0:D, 0], wt[0:D, 0], wt[0:D, 1], ALU.subtract).then_inc(w_ready, 1)
                    for j in range(NB // 7):
                        dve.wait_ge(x_ready, j + 1)
                        dve.tensor_copy(ab[:, 7 * j:7 * j + 7].rearrange("p b k f -> p (b k f)"), xp[:, 0:14 * D]).then_inc(x_copied, 1)

        with phase() as c:
            got = sb("e_got", [P, UNROLL, GT, D], F32, c)
            rs = sb("e_rs", [P, UNROLL, GT, D], F32, c)
            a_row = sb("e_a", [P, UNROLL, GT, D], F32, c)
            pre = sb("e_pre", [P, UNROLL, GT, D], F32, c)
            hid = sb("e_hid", [2 * D, UNROLL, GT // 2 * P], F32, c)
            acc = sb("e_acc", [P, UNROLL, GT, D], F32, c)
            pen = sb("e_pen", [P, W], F32, c)
            tp = [pb(f"e_tp{j}", [2 * D, GT // 2 * P], F32, c) for j in range(2)]
            mp = [[pb(f"e_mp{j}{k}", [P, GT // 2, D], F32, c) for k in range(2)] for j in range(2)]
            index = sb("e_index", [P, UNROLL, GT], I32, c)
            index_ready, begun = sem("e_ix"), sem("e_be")
            gathered = [sem(f"e_ga{u}") for u in range(UNROLL)]
            rs_in = [sem(f"e_rs{u}") for u in range(UNROLL)]
            stored = [sem(f"e_st{u}") for u in range(UNROLL)]
            ready, a_ready, pre_ready, turned, hid_ready, m_ready, maxed = (sem(f"e_{n}") for n in ("re", "ar", "pr", "tu", "hi", "me", "ma"))
            with nc.Block() as block:
                @block.gpsimd
                def _(pool):
                    with pool.Fori(0, NG // UNROLL) as i:
                        for u in range(UNROLL):
                            g = i * UNROLL + u
                            pool.wait_ge(index_ready, g + 1)
                            pool.sem_inc(begun, 1)
                            for t in range(GT):
                                pool.indirect_dma_start(got[:, u, t], None, b_table, bass.IndirectOffsetOnAxis(
                                    ap=index[:, u, t:t + 1], axis=0)).then_inc(gathered[u], 16)

                @block.sync
                def _(sp):
                    wide = row_starts.rearrange("(p t) f -> p t f", p=P)
                    with sp.Fori(0, NG // UNROLL) as i:
                        for u in range(UNROLL):
                            g = i * UNROLL + u
                            sp.wait_ge(pre_ready, g + 1)
                            sp.dma_start(rs[:, u], wide[:, bass.ds(g * GT, GT), :]).then_inc(rs_in[u], 16)

                @block.vector
                def _(dve):
                    dve.memset(acc[:, UNROLL - 1, GT - 1], -BIG).then_inc(ready, 1)
                    dve.memset(a_row[:, UNROLL - 1, GT - 1], 0.0).then_inc(ready, 1)
                    dve.tensor_scalar(pen[:, :], cont[:, :], BIG, -BIG, ALU.mult, ALU.add).then_inc(ready, 1)
                    dve.wait_ge(ready, 3)
                    dve.sem_inc(pre_ready, UNROLL)
                    dve.sem_inc(a_ready, 1)
                    dve.sem_inc(maxed, 2 * GT)

                    def before(g, u, i=None):
                        dve.wait_ge(rs_in[u], i * 16 + 16)
                        for t in range(GT):
                            prev = a_row[:, u, t - 1] if t else a_row[:, (u - 1) % UNROLL, GT - 1]
                            dve.wait_ge(a_ready, g * GT + (t + 1))
                            dve.scalar_tensor_tensor(a_row[:, u, t], prev, cont[:, bass.ds(g * GT + t, 1)], rs[:, u, t],
                                                     ALU.mult, ALU.add).then_inc(a_ready, 1)
                        dve.wait_ge(a_ready, g * GT + (GT + 1))
                        dve.wait_ge(gathered[u], i * (16 * GT) + 16 * GT)
                        dve.wait_ge(turned, g + 1)
                        dve.tensor_tensor(pre[:, u], a_row[:, u], got[:, u], ALU.add).then_inc(pre_ready, 1)

                    def after(g, u, i=None):
                        dve.wait_ge(m_ready, g + 1)
                        if i is not None:
                            dve.wait_ge(stored[u], i * 16)
                        for t in range(GT):
                            prev = acc[:, u, t - 1] if t else acc[:, (u - 1) % UNROLL, GT - 1]
                            dve.wait_ge(maxed, g * GT + (t + 2 * GT))
                            dve.scalar_tensor_tensor(acc[:, u, t], prev, pen[:, bass.ds(g * GT + t, 1)],
                                                     mp[u % 2][t % 2][:, t // 2],
                                                     ALU.add, ALU.max).then_inc(maxed, 1)

                    dve.sem_inc(turned, UNROLL)
                    before(0, 0, 0)
                    for u in range(UNROLL):
                        before(u + 1, (u + 1) % UNROLL, (u + 1) // UNROLL)
                        after(u, u)
                    with dve.Fori(1, NG // UNROLL - 1) as i:
                        for u in range(UNROLL):
                            before(i * UNROLL + (u + 1), (u + 1) % UNROLL, i + (u + 1) // UNROLL)
                            after(i * UNROLL + u, u, i)
                    for g in range(NG - UNROLL, NG):
                        if g + 1 < NG:
                            before(g + 1, (g + 1) % UNROLL, (g + 1) // UNROLL)
                        after(g, g % UNROLL, g // UNROLL)

                @block.tensor
                def _(pe):
                    def turn(g, u):
                        pe.wait_ge(pre_ready, g + (UNROLL + 1))
                        pe.wait_ge(hid_ready, g + 1)
                        for t in range(0, GT, 2):
                            last = pe.transpose(tp[u % 2][:, t // 2 * P:(t // 2 + 1) * P],
                                                pre[:, u, t:t + 2].rearrange("p t f -> p (t f)"), ident[:, :])
                        last.then_inc(turned, 1)

                    def multiply(g, u):
                        pe.wait_ge(hid_ready, g + 3)
                        pe.wait_ge(maxed, g * GT + GT)
                        for t in range(GT):
                            half = slice(t % 2 * D, t % 2 * D + D)
                            last = pe.matmul(mp[u % 2][t % 2][:, t // 2], hid[half, u, t // 2 * P:(t // 2 + 1) * P], w2_sb[half, :],
                                             start=True, stop=True)
                        last.then_inc(m_ready, 1)

                    over_groups_skewed(pe, turn, multiply)

                @block.scalar
                def _(act):
                    act.sem_inc(hid_ready, 2)
                    wide = peak_rows[0:EP, :].rearrange("(p t) f -> p t f", p=P)

                    def relu(g, u):
                        act.wait_ge(turned, g + (UNROLL + 1))
                        act.activation(hid[:, u], tp[u % 2][:, :], ACT.Relu).then_inc(hid_ready, 1)

                    def store(g, u):
                        act.wait_ge(maxed, g * GT + 3 * GT)
                        act.dma_start(wide[:, bass.ds(g * GT, GT), :], acc[:, u]).then_inc(stored[u], 16)

                    def indices(g, u):
                        act.wait_ge(pre_ready, g + 1)
                        act.activation(index[:, u], src_i[:, bass.ds(g * GT, GT)], ACT.Copy).then_inc(index_ready, 1)

                    for u in range(UNROLL):
                        indices(u, u)
                    relu(0, 0)
                    relu(1, 1)
                    with act.Fori(0, NG // UNROLL - 1) as i:
                        for u in range(UNROLL):
                            indices(i * UNROLL + (u + UNROLL), u)
                            relu(i * UNROLL + (u + 2), (u + 2) % UNROLL)
                            store(i * UNROLL + u, u)
                    for g in range(NG - UNROLL, NG):
                        if g + 2 < NG:
                            relu(g + 2, (g + 2) % UNROLL)
                        store(g, g % UNROLL)
                    for u in range(UNROLL):
                        act.wait_ge(stored[u], 16 * (NG // UNROLL))
            chunk_carries("m", acc[:, UNROLL - 1, GT - 1], D, True, peak_carries)

        with phase() as c:
            agg = sb("f_agg", [P, NB, D], F32, c)
            more = sb("f_more", [P, NB, D], F32, c)
            node_rows("m", peak_rows, peak_carries, D, agg, more)
            chain, done, stored = sem("f_chain"), sem("f_done"), sem("f_stored")
            with nc.Block() as block:
                @block.vector
                def _(dve):
                    then = chained(dve, chain)
                    then(dve.tensor_tensor(agg[:, :, :], agg[:, :, :], more[:, :, :], ALU.max))
                    then(dve.tensor_tensor(agg[:, :, :], agg[:, :, :], mid(b2_sb[:, :], [P, NB, D]), ALU.add))
                    then(dve.tensor_tensor(agg[:, :, :], agg[:, :, :], bcast(has[:, :], [P, NB, D]), ALU.mult))
                    dve.tensor_tensor(agg[:, :, :], agg[:, :, :], x_sb[:, :, :], ALU.add).then_inc(done, 1)

                @block.sync
                def _(sp):
                    sp.wait_ge(done, 1)
                    full = N // P
                    sp.dma_start(out[0:full * P, :].rearrange("(b p) f -> p b f", p=P), agg[:, 0:full]).then_inc(stored, 16)
                    sp.dma_start(out[full * P:N, :], agg[0:N - full * P, full]).then_inc(stored, 16)
                    sp.wait_ge(stored, 32)


def bass_col(ap):
    return ap.rearrange("(d a) -> d a", a=1)


def accumulate(pe, add_group):
    for g in range(UNROLL):
        add_group(g, g, start=g == 0)
    with pe.Fori(0, NG // UNROLL - 2) as i:
        for u in range(UNROLL):
            add_group(i * UNROLL + (UNROLL + u), u)
    for g in range(NG - UNROLL, NG):
        add_group(g, g % UNROLL, stop=g == NG - 1)

_C = ("lin_w", "lin_b", "ai_w", "ai_b", "aj_w", "aj_b", "ew_w", "ew_b")
ORDER = (["x", "src", "dst", "edge_attr_32", "L0_gnn_rel_w", "L0_gnn_rel_b"]
         + [f"L0_gnn_c{k}_{n}" for k in (1, 2) for n in _C]
         + ["L1_gnn_W1", "L1_gnn_b1", "L1_gnn_W2", "L1_gnn_b2"])


def kernel(**inputs):
    import numpy as np
    import concourse.bacc as bacc
    from concourse.bass_utils import run_bass_kernel_spmd

    def edges(a, fill):
        a = np.asarray(a)
        pad = [(0, EP - E)] + [(0, 0)] * (a.ndim - 1)
        return np.ascontiguousarray(np.pad(a, pad, constant_values=fill).reshape((P, W) + a.shape[1:]))

    arrays = {k: np.ascontiguousarray(np.asarray(a)) for k, a in inputs.items()}
    arrays["x"] = np.pad(arrays["x"], [(0, NP - N), (0, 0)])
    arrays["src"] = edges(inputs["src"], PAD_NODE)
    arrays["dst"] = edges(inputs["dst"], PAD_NODE)
    arrays["edge_attr_32"] = edges(inputs["edge_attr_32"], 0)
    nc = bacc.Bacc("TRN2", target_bir_lowering=False, num_devices=1)
    fed, args = {}, []
    for name in ORDER:
        fed[f"in_{name}"] = arrays[name]
        args.append(nc.dram_tensor(f"in_{name}", arrays[name].shape, mybir.dt.from_np(arrays[name].dtype),
                                   kind="ExternalInput").ap())
    out = nc.dram_tensor("out", [N, D], F32, kind="ExternalOutput").ap()
    gnn_kernel(nc, *args, out)
    return run_bass_kernel_spmd(nc, [fed], core_ids=[0]).results[0]["out"]
```

```python
import concourse.bass as bass
from concourse import mybir
from contextlib import ExitStack, contextmanager

F32 = mybir.dt.float32
BF16 = mybir.dt.bfloat16
I32 = mybir.dt.int32
ALU = mybir.AluOpType
ACT = mybir.ActivationFunctionType
AX = mybir.AxisListType

N = 6250
E = 206250
D = 64
R = 32
P = 128
NB = -(-N // P)
NP = NB * P
TABLE = NP + P
PAD_NODE = TABLE - 1
GT = 4
UNROLL = 4
W = -(-E // (P * GT * UNROLL)) * GT * UNROLL
EP = P * W
NG = W // GT
TW = D + 3
M = D + R + 1
BITS = 13
DIGITS = 16
VALUE = 32
TALL = VALUE + 3
SIGN = 2.0 ** 50
BIG = SIGN * SIGN
SKIP = 1 << 29
EPS = 1e-5
assert N <= 1 << BITS and PAD_NODE < 1 << BITS


def bcast(ap, shape):
    return ap.unsqueeze(len(shape) - 1).to_broadcast(shape)


def mid(ap, shape):
    return ap.unsqueeze(1).to_broadcast(shape)


def over_groups(eng, stage):
    with eng.Fori(0, NG // UNROLL) as i:
        for u in range(UNROLL):
            stage(i * UNROLL + u, u)


def over_groups_skewed(eng, first, second):
    first(0, 0)
    with eng.Fori(0, NG // UNROLL - 1) as i:
        for u in range(UNROLL):
            first(i * UNROLL + (u + 1), (u + 1) % UNROLL)
            second(i * UNROLL + u, u)
    for g in range(NG - UNROLL, NG):
        if g + 1 < NG:
            first(g + 1, (g + 1) % UNROLL)
        second(g, g % UNROLL)


def over_groups_ahead(eng, first, second):
    for u in range(UNROLL):
        first(u, u)
    with eng.Fori(0, NG // UNROLL - 1) as i:
        for u in range(UNROLL):
            first(i * UNROLL + (UNROLL + u), u)
            second(i * UNROLL + u, u)
    for g in range(NG - UNROLL, NG):
        second(g, g % UNROLL)


def gnn_kernel(nc, x, src, dst, attr, rel_w, rel_b,
               c1_w, c1_b, c1_ai_w, c1_ai_b, c1_aj_w, c1_aj_b, c1_ew_w, c1_ew_b,
               c2_w, c2_b, c2_ai_w, c2_ai_b, c2_aj_w, c2_aj_b, c2_ew_w, c2_ew_b,
               w1, b1, w2, b2, out):
    ctx = ExitStack()
    with ctx:
        ctx.enter_context(nc.allow_non_contiguous_dma(reason="columns of a few numbers"))
        def sb(name, shape, dt, c=ctx):
            return c.enter_context(nc.sbuf_tensor(name, shape, dt))

        def pb(name, shape, dt, c):
            return c.enter_context(nc.psum_tensor(name, shape, dt))

        phases = []

        @contextmanager
        def phase():
            with ExitStack() as c:
                phases.append((c, []))
                yield c
                own = phases.pop()[1]
                if own:
                    with nc.Block() as block:
                        @block.gpsimd
                        def _(pool):
                            for s in own:
                                pool.sem_clear(s)

        def sem(name):
            c, own = phases[-1]
            own.append(c.enter_context(nc.semaphore(name)))
            return own[-1]

        def dram(name, shape, dt):
            return nc.dram_tensor(name, shape, dt, kind="Internal").ap()

        def lasting(name):
            return ctx.enter_context(nc.semaphore(name))

        table = dram("table", [TABLE, TW], F32)
        rows = dram("rows", [EP + 1, M], F32)
        carries = dram("carries", [P + 1, M], F32)
        peak_rows = dram("peak_rows", [EP + 1, D], F32)
        peak_carries = dram("peak_carries", [P + 1, D], F32)
        a_starts = dram("a_starts", [EP, 1], F32)
        a_table = dram("a_table", [TABLE, D], F32)
        b_table = dram("b_table", [TABLE, D], F32)
        row_starts = dram("row_starts", [EP, D], F32)

        src_i = sb("src_i", [P, W], I32)
        lo = sb("lo", [P, W], F32)
        blk = sb("blk", [P, W], F32)
        lead = sb("lead", [P, W], F32)
        cont = sb("cont", [P, W], F32)
        z = [sb(f"z{k}", [P, W], F32) for k in range(2)]
        digits = sb("digits", [P, W * DIGITS], BF16)
        x_sb = sb("x_sb", [P, NB, D], F32)
        h = sb("h", [P, NB, D], F32)
        count = sb("count", [P, NB], F32)
        start_i = sb("start_i", [P, NB], I32)
        end_i = sb("end_i", [P, NB], I32)
        carry_i = sb("carry_i", [P, NB], I32)
        has = sb("has", [P, NB], F32)
        dst0_i = sb("dst0_i", [P, 1], I32)
        strad = sb("strad", [P, 1], F32)
        through = sb("through", [P, 1], F32)
        iota = sb("iota", [P, P], F32)
        lane = sb("lane", [P, 1], F32)
        ident = sb("ident", [P, P], F32)
        identb = sb("identb", [P, P], BF16)
        below = sb("below", [P, P], F32)
        ones = sb("ones", [P, P], F32)
        zero = sb("zero", [P, 8 * D], F32)
        rel_aug = sb("rel_aug", [D, R + 1], F32)
        rel_t = sb("rel_t", [R + 1, D], F32)
        v = sb("v", [P, 2, R + 1], F32)
        bias = sb("bias", [P, 2], F32)

        with phase() as c:
            dst_i = sb("dst_i", [P, W], I32, c)
            tmp_i = sb("tmp_i", [P, W], I32, c)
            dlo = sb("dlo", [P, W], F32, c)
            dblk = sb("dblk", [P, W], F32, c)
            prev_i = sb("prev_i", [P, 1], I32, c)
            prev_f = sb("prev_f", [P, 1], F32, c)
            dst0_f = sb("dst0_f", [P, 1], F32, c)
            dstl_f = sb("dstl_f", [P, 1], F32, c)
            ew = sb("ew", [D, 2], F32, c)
            bias_in = sb("bias_in", [P, 6], F32, c)
            hot_lo = sb("hot_lo", [P, UNROLL, GT, P], BF16, c)
            hot_blk = sb("hot_blk", [P, UNROLL, GT, NB], BF16, c)
            start_f = sb("start_f", [P, NB], F32, c)
            end_f = sb("end_f", [P, NB], F32, c)
            chunk_f = sb("chunk_f", [P, NB], F32, c)
            total = sb("total", [P, NB], F32, c)
            tmp1 = sb("tmp1", [P, NB], F32, c)
            tmp2 = sb("tmp2", [P, NB], F32, c)
            bounds = sb("bounds", [P, P], F32, c)
            neutral = sb("neutral", [1, M], F32, c)
            hot_f = sb("hot_f", [P, P], F32, c)
            small = pb("small", [P, 512], F32, c)
            hist = pb("hist", [P, NB], F32, c)

            edges_in, small_in, made = sem("edges_in"), sem("small_in"), sem("made")
            chain, hot_ready, hot_used = sem("chain"), sem("hot_ready"), sem("hot_used")
            sums_ready, sums_done = sem("sums_ready"), sem("sums_done")
            proj_done, zeroed, filled = sem("proj_done"), sem("zeroed"), sem("filled")
            with nc.Block() as block:
                @block.sync
                def _(sp):
                    sp.dma_start(src_i[:, :], src).then_inc(edges_in, 16)
                    sp.dma_start(dst_i[:, :], dst).then_inc(edges_in, 16)
                    sp.dma_start(dst0_i[:, :], dst[:, 0:1]).then_inc(edges_in, 16)
                    sp.dma_start(prev_i[1:P, :], dst[0:P - 1, W - 1:W]).then_inc(edges_in, 16)
                    sp.dma_start(x_sb[:, :, :], x.rearrange("(b p) f -> p b f", p=P)).then_inc(small_in, 16)
                    sp.dma_start(rel_aug[:, 0:R], rel_w).then_inc(small_in, 16)
                    sp.dma_start(rel_aug[:, R:R + 1], bass_col(rel_b)).then_inc(small_in, 16)
                    sp.dma_start(ew[:, 0:1], c1_ew_w.rearrange("a d -> d a")).then_inc(small_in, 16)
                    sp.dma_start(ew[:, 1:2], c2_ew_w.rearrange("a d -> d a")).then_inc(small_in, 16)
                    for k, b in enumerate((c1_ai_b, c1_aj_b, c1_ew_b, c2_ai_b, c2_aj_b, c2_ew_b)):
                        sp.dma_start(bias_in[:, k:k + 1], b.partition_broadcast(P)).then_inc(small_in, 16)
                    sp.wait_ge(zeroed, 1)
                    sp.dma_start(a_starts.rearrange("(p t) f -> p (t f)", p=P), z[0][:, :]).then_inc(filled, 16)
                    sp.dma_start(table[NP:TABLE, :], zero[:, 0:TW]).then_inc(filled, 16)
                    sp.dma_start(a_table[NP:TABLE, :], zero[:, 0:D]).then_inc(filled, 16)
                    sp.dma_start(b_table[NP:TABLE, :], zero[:, 0:D]).then_inc(filled, 16)
                    sp.dma_start(rows[EP:EP + 1, :], zero[0:1, 0:M]).then_inc(filled, 16)
                    sp.dma_start(carries[P:P + 1, :], zero[0:1, 0:M]).then_inc(filled, 16)
                    sp.dma_start(peak_rows[EP:EP + 1, :], neutral[0:1, 0:D]).then_inc(filled, 16)
                    sp.dma_start(peak_carries[P:P + 1, :], neutral[0:1, 0:D]).then_inc(filled, 16)
                    wide = row_starts.rearrange("(p t) f -> p t f", p=P)
                    with sp.Fori(0, W // 8) as i:
                        sp.dma_start(wide[:, bass.ds(i * 8, 8), :],
                                     zero[:, :].rearrange("p (t f) -> p t f", f=D)).then_inc(filled, 16)
                    sp.wait_ge(filled, 16 * (8 + W // 8))

                @block.gpsimd
                def _(pool):
                    pool.iota(iota[:, :], [[1, P]], base=0, channel_multiplier=0,
                              allow_small_or_imprecise_dtypes=True).then_inc(made, 1)
                    pool.iota(lane[:, :], [[0, 1]], base=0, channel_multiplier=1,
                              allow_small_or_imprecise_dtypes=True).then_inc(made, 1)
                    pool.iota(bounds[:, :], [[W, P]], base=0, channel_multiplier=0,
                              allow_small_or_imprecise_dtypes=True).then_inc(made, 1)
                    pool.memset(ones[:, :], 1.0).then_inc(made, 1)
                    pool.memset(neutral[:, :], -BIG).then_inc(made, 1)

                @block.vector
                def _(dve):
                    n = [0]

                    def then(ins):
                        ins.then_inc(chain, 1)
                        n[0] += 1
                        dve.wait_ge(chain, n[0])

                    dve.memset(prev_i[0:1, :], -1).then_inc(chain, 1)
                    n[0] += 1
                    then(dve.memset(zero[:, :], 0.0))
                    dve.wait_ge(made, 5)
                    dve.memset(z[0][:, :], 0.0).then_inc(zeroed, 1)
                    then(dve.tensor_scalar(ident[:, :], iota[:, :], lane[:, 0:1], None, ALU.is_equal))
                    then(dve.tensor_copy(identb[:, :], ident[:, :]))
                    then(dve.tensor_scalar(below[:, :], iota[:, :], lane[:, 0:1], None, ALU.is_gt))
                    dve.wait_ge(edges_in, 64)
                    dve.wait_ge(small_in, 16 * 11)
                    then(dve.tensor_scalar(tmp_i[:, :], dst_i[:, :], P - 1, None, ALU.bitwise_and))
                    then(dve.tensor_copy(dlo[:, :], tmp_i[:, :]))
                    then(dve.tensor_scalar(tmp_i[:, :], dst_i[:, :], 7, None, ALU.logical_shift_right))
                    then(dve.tensor_copy(dblk[:, :], tmp_i[:, :]))
                    then(dve.tensor_tensor(cont[:, 1:W], dst_i[:, 1:W], dst_i[:, 0:W - 1], ALU.is_equal))
                    then(dve.memset(cont[:, 0:1], 0.0))
                    then(dve.tensor_copy(prev_f[:, :], prev_i[:, :]))
                    then(dve.tensor_copy(dst0_f[:, :], dst_i[:, 0:1]))
                    then(dve.tensor_copy(dstl_f[:, :], dst_i[:, W - 1:W]))
                    then(dve.tensor_tensor(strad[:, :], prev_f[:, :], dst0_f[:, :], ALU.is_equal))
                    then(dve.tensor_tensor(through[:, :], dstl_f[:, :], dst0_f[:, :], ALU.is_equal))
                    then(dve.tensor_tensor(through[:, :], through[:, :], strad[:, :], ALU.mult))
                    then(dve.tensor_scalar(tmp_i[:, :], src_i[:, :], P - 1, None, ALU.bitwise_and))
                    then(dve.tensor_copy(lo[:, :], tmp_i[:, :]))
                    then(dve.tensor_scalar(tmp_i[:, :], src_i[:, :], 7, None, ALU.logical_shift_right))
                    then(dve.tensor_copy(blk[:, :], tmp_i[:, :]))
                    then(dve.memset(digits[:, :], 0.0))
                    dig = digits[:, :].rearrange("p (t k) -> p t k", k=DIGITS)
                    then(dve.memset(dig[:, :, BITS], SIGN))
                    for k in range(BITS):
                        then(dve.tensor_scalar(tmp_i[:, :], src_i[:, :], 1 << k, None, ALU.bitwise_and))
                        then(dve.tensor_scalar(dig[:, :, k], tmp_i[:, :], 2.0 * SIGN / (1 << k), -SIGN,
                                               ALU.mult, ALU.add))
                    dve.wait_ge(proj_done, 2)
                    then(dve.tensor_copy(v[:, :, :], small[:, 0:2 * (R + 1)].rearrange("p (k r) -> p k r", k=2)))
                    then(dve.tensor_reduce(bias[:, :], bias_in[:, :].rearrange("p (k j) -> p k j", k=2), AX.X, ALU.add))
                    then(dve.tensor_tensor(bias[:, :], bias[:, :], v[:, :, R], ALU.add))
                    dve.wait_ge(proj_done, 2)
                    then(dve.tensor_copy(rel_t[:, :], small[0:R + 1, 128:128 + D]))

                    def onehots(g, u):
                        dve.wait_ge(hot_used, g + 1)
                        dve.tensor_tensor(hot_lo[:, u], mid(iota[:, :], [P, GT, P]),
                                          bcast(dlo[:, bass.ds(g * GT, GT)], [P, GT, P]), ALU.is_equal).then_inc(hot_ready, 1)
                        dve.tensor_tensor(hot_blk[:, u], mid(iota[:, 0:NB], [P, GT, NB]),
                                          bcast(dblk[:, bass.ds(g * GT, GT)], [P, GT, NB]), ALU.is_equal).then_inc(hot_ready, 1)

                    over_groups(dve, onehots)
                    dve.wait_ge(hot_used, UNROLL + NG)
                    dve.tensor_copy(count[:, :], hist[:, :]).then_inc(sums_ready, 1)
                    dve.wait_ge(sums_done, 1)
                    then(dve.tensor_copy(total[:, :], small[:, 256:256 + NB]))
                    then(dve.tensor_tensor_scan(tmp1[:, :], ones[:, 0:NB], total[:, :], 0.0, ALU.mult, ALU.add))
                    then(dve.tensor_tensor(tmp1[:, :], tmp1[:, :], total[:, :], ALU.subtract))
                    then(dve.tensor_tensor(start_f[:, :], tmp1[:, :], small[:, 320:320 + NB], ALU.add))
                    then(dve.tensor_tensor(end_f[:, :], start_f[:, :], count[:, :], ALU.add))
                    then(dve.tensor_scalar(end_f[:, :], end_f[:, :], -1.0, None, ALU.add))
                    then(dve.tensor_scalar(has[:, :], count[:, :], 0.0, None, ALU.is_gt))
                    for b in range(NB):
                        then(dve.tensor_scalar(hot_f[:, :], bounds[:, :], end_f[:, b:b + 1], None,
                                               ALU.is_le))
                        then(dve.tensor_reduce(chunk_f[:, b:b + 1], hot_f[:, :], AX.X, ALU.add))
                    then(dve.tensor_scalar(chunk_f[:, :], chunk_f[:, :], -1.0, None, ALU.add))
                    then(dve.tensor_scalar(tmp1[:, :], chunk_f[:, :], float(W), None, ALU.mult))
                    then(dve.tensor_tensor(tmp1[:, :], start_f[:, :], tmp1[:, :], ALU.is_lt))
                    then(dve.tensor_tensor(tmp1[:, :], tmp1[:, :], has[:, :], ALU.mult))
                    then(dve.tensor_scalar(tmp2[:, :], chunk_f[:, :], float(P), None, ALU.subtract))
                    then(dve.tensor_tensor(tmp2[:, :], tmp2[:, :], tmp1[:, :], ALU.mult))
                    then(dve.tensor_scalar(carry_i[:, :], tmp2[:, :], float(P), None, ALU.add))
                    then(dve.tensor_scalar(tmp2[:, :], end_f[:, :], float(EP), None, ALU.subtract))
                    then(dve.tensor_tensor(tmp2[:, :], tmp2[:, :], has[:, :], ALU.mult))
                    then(dve.tensor_scalar(end_i[:, :], tmp2[:, :], float(EP), None, ALU.add))
                    then(dve.tensor_tensor(tmp2[:, :], start_f[:, :], has[:, :], ALU.mult))
                    then(dve.tensor_scalar(tmp1[:, :], has[:, :], -float(SKIP), float(SKIP), ALU.mult, ALU.add))
                    then(dve.tensor_tensor(start_i[:, :], tmp1[:, :], tmp2[:, :], ALU.add))

                @block.tensor
                def _(pe):
                    pe.wait_ge(small_in, 16 * 11)
                    pe.wait_ge(chain, 5)
                    for k in range(2):
                        last = pe.matmul(small[:, k * (R + 1):(k + 1) * (R + 1)],
                                         ew[:, k:k + 1].to_broadcast([D, P]), rel_aug[:, :], start=True, stop=True)
                    last.then_inc(proj_done, 1)
                    pe.transpose(small[0:R + 1, 128:128 + D], rel_aug[:, :], ident[0:D, 0:D]).then_inc(proj_done, 1)
                    pe.sem_inc(hot_used, UNROLL)

                    def add_group(g, u, start=False, stop=False):
                        pe.wait_ge(hot_ready, g * 2 + 2)
                        for t in range(GT):
                            last = pe.matmul(hist[:, :], hot_lo[:, u, t], hot_blk[:, u, t],
                                             start=start and t == 0, stop=stop and t == GT - 1)
                        last.then_inc(hot_used, 1)

                    accumulate(pe, add_group)
                    pe.wait_ge(sums_ready, 1)
                    pe.matmul(small[:, 256:256 + NB], ones[:, :], count[:, :], start=True, stop=True)
                    pe.matmul(small[:, 320:320 + NB], below[:, :], count[:, :], start=True, stop=True).then_inc(sums_done, 1)


        def chained(eng, semaphore):
            n = [0]

            def then(ins):
                ins.then_inc(semaphore, 1)
                n[0] += 1
                eng.wait_ge(semaphore, n[0])

            return then

        def norm_relu(tag):
            with phase() as c:
                mean = sb(f"mean{tag}", [P, NB], F32, c)
                var = sb(f"var{tag}", [P, NB], F32, c)
                sq = sb(f"sq{tag}", [P, NB, D], F32, c)
                chain, var_ready, std_ready = sem(f"n_chain{tag}"), sem(f"n_var{tag}"), sem(f"n_std{tag}")
                with nc.Block() as block:
                    @block.vector
                    def _(dve):
                        then = chained(dve, chain)
                        then(dve.tensor_reduce(mean[:, :], x_sb[:, :, :], AX.X, ALU.add))
                        then(dve.tensor_scalar(mean[:, :], mean[:, :], 1.0 / D, None, ALU.mult))
                        then(dve.tensor_tensor(h[:, :, :], x_sb[:, :, :], bcast(mean[:, :], [P, NB, D]), ALU.subtract))
                        then(dve.tensor_tensor(sq[:, :, :], h[:, :, :], h[:, :, :], ALU.mult))
                        then(dve.tensor_reduce(var[:, :], sq[:, :, :], AX.X, ALU.add))
                        dve.tensor_scalar(var[:, :], var[:, :], 1.0 / D, EPS, ALU.mult, ALU.add).then_inc(var_ready, 1)
                        dve.wait_ge(std_ready, 1)
                        then(dve.reciprocal(var[:, :], var[:, :]))
                        then(dve.tensor_tensor(h[:, :, :], h[:, :, :], bcast(var[:, :], [P, NB, D]), ALU.mult))
                        then(dve.tensor_scalar(h[:, :, :], h[:, :, :], 0.0, None, ALU.max))

                    @block.scalar
                    def _(act):
                        act.wait_ge(var_ready, 1)
                        act.activation(var[:, :], var[:, :], ACT.Sqrt).then_inc(std_ready, 1)

        def edge_terms():
            with phase() as c:
                att = sb("att", [P, UNROLL, GT, R], F32, c)
                prod = sb("prod", [P, 2, GT, R], F32, c)
                att_in = [sem(f"att_in{u}") for u in range(UNROLL)]
                prod_ready, terms = sem("prod_ready"), sem("terms")
                with nc.Block() as block:
                    @block.sync
                    def _(sp):
                        with sp.Fori(0, NG // UNROLL) as i:
                            for u in range(UNROLL):
                                g = i * UNROLL + u
                                sp.wait_ge(prod_ready, g * 2 + 2)
                                sp.dma_start(att[:, u], attr[:, bass.ds(g * GT, GT), :]).then_inc(att_in[u], 16)

                    @block.vector
                    def _(dve):
                        dve.sem_inc(prod_ready, 2 * UNROLL)
                        dve.sem_inc(terms, 1)
                        with dve.Fori(0, NG // UNROLL) as i:
                            for u in range(UNROLL):
                                g = i * UNROLL + u
                                dve.wait_ge(att_in[u], i * 16 + 16)
                                dve.wait_ge(terms, g * 2 + 1)
                                for k in range(2):
                                    ins = dve.tensor_tensor(prod[:, k], att[:, u], mid(v[:, k, 0:R], [P, GT, R]), ALU.mult)
                                    ins.then_inc(prod_ready, 1)
                                dve.wait_ge(prod_ready, g * 2 + (2 * UNROLL + 2))
                                for k in range(2):
                                    dve.tensor_reduce(z[k][:, bass.ds(g * GT, GT)], prod[:, k], AX.X, ALU.add).then_inc(terms, 1)
                        dve.wait_ge(terms, NG * 2 + 1)
                        for k in range(2):
                            dve.tensor_scalar(z[k][:, :], z[k][:, :], bias[:, k:k + 1], None, ALU.add)

        def project(tag, w, b, ai_w, aj_w, xn):
            with phase() as c:
                wb = sb(f"wb{tag}", [D, D + 1], F32, c)
                aij = sb(f"aij{tag}", [D, 2], F32, c)
                waug = sb(f"waug{tag}", [D + 1, D + 2], F32, c)
                ht = sb(f"ht{tag}", [D + 1, 7 * P], F32, c)
                wp = pb(f"wp{tag}", [P, 512], F32, c)
                hp = pb(f"hp{tag}", [P, 1024], F32, c)
                xp = pb(f"xp{tag}", [P, 512], F32, c)
                w_in, w_ready, w_copied = sem(f"p_win{tag}"), sem(f"p_w{tag}"), sem(f"p_wc{tag}")
                turned, ht_ready, x_ready, x_copied, stored = (sem(f"p_{n}{tag}") for n in ("t", "h", "x", "xc", "st"))
                with nc.Block() as block:
                    @block.sync
                    def _(sp):
                        sp.dma_start(wb[:, 0:D], w).then_inc(w_in, 16)
                        sp.dma_start(wb[:, D:D + 1], bass_col(b)).then_inc(w_in, 16)
                        sp.dma_start(aij[:, 0:1], ai_w.rearrange("a d -> d a")).then_inc(w_in, 16)
                        sp.dma_start(aij[:, 1:2], aj_w.rearrange("a d -> d a")).then_inc(w_in, 16)
                        sp.wait_ge(x_copied, NB // 7)
                        sp.dma_start(table[0:NP, :].rearrange("(b p) f -> p b f", p=P), xn[:, :, :]).then_inc(stored, 16)
                        sp.wait_ge(stored, 16)

                    @block.tensor
                    def _(pe):
                        pe.wait_ge(w_in, 64)
                        pe.transpose(wp[0:D + 1, 0:D], wb[:, :], ident[0:D, 0:D])
                        pe.matmul(wp[0:D + 1, D:D + 2], wb[:, :], aij[:, :], start=True, stop=True).then_inc(w_ready, 1)
                        for j in range(NB // 7):
                            if j:
                                pe.wait_ge(ht_ready, j)
                            for b7 in range(7):
                                last = pe.transpose(hp[0:D, b7 * P:(b7 + 1) * P], h[:, 7 * j + b7, :], ident[:, :])
                            last.then_inc(turned, 1)
                            pe.wait_ge(ht_ready, j + 1)
                            if j == 0:
                                pe.wait_ge(w_copied, 2)
                            else:
                                pe.wait_ge(x_copied, j)
                            for b7 in range(7):
                                last = pe.matmul(xp[:, b7 * (D + 2):(b7 + 1) * (D + 2)], ht[:, b7 * P:(b7 + 1) * P],
                                                 waug[:, :], start=True, stop=True)
                            last.then_inc(x_ready, 1)

                    @block.scalar
                    def _(act):
                        for j in range(NB // 7):
                            act.wait_ge(turned, j + 1)
                            if j:
                                act.wait_ge(x_ready, j)
                            act.activation(ht[0:D, :], hp[0:D, 0:7 * P], ACT.Copy).then_inc(ht_ready, 1)

                    @block.vector
                    def _(dve):
                        dve.memset(ht[D:D + 1, :], 1.0).then_inc(w_copied, 1)
                        dve.memset(xn[:, :, D + 2:D + 3], 0.0)
                        dve.wait_ge(w_ready, 1)
                        dve.tensor_copy(waug[:, :], wp[0:D + 1, 0:D + 2]).then_inc(w_copied, 1)
                        for j in range(NB // 7):
                            dve.wait_ge(x_ready, j + 1)
                            dve.tensor_copy(xn[:, 7 * j:7 * j + 7, 0:D + 2],
                                            xp[:, 0:7 * (D + 2)].rearrange("p (b f) -> p b f", f=D + 2)).then_inc(x_copied, 1)

        def expand(tag, xn, zk):
            with phase() as c:
                at_start = sb(f"at_start{tag}", [P, W], F32, c)
                first = sb(f"first{tag}", [P, TW], F32, c)
                scattered, firsts = lasting(f"e_sc{tag}"), lasting(f"e_fi{tag}")
                loaded, chain = sem(f"e_lo{tag}"), sem(f"e_ch{tag}")
                with nc.Block() as block:
                    @block.gpsimd
                    def _(pool):
                        for b in range(NB):
                            pool.indirect_dma_start(a_starts, bass.IndirectOffsetOnAxis(ap=start_i[:, b:b + 1], axis=0),
                                                    xn[:, b, D:D + 1], None, bounds_check=EP - 1,
                                                    oob_is_err=False).then_inc(scattered, 16)
                        pool.indirect_dma_start(first[:, :], None, table,
                                                bass.IndirectOffsetOnAxis(ap=dst0_i[:, 0:1], axis=0)).then_inc(firsts, 16)

                    @block.sync
                    def _(sp):
                        sp.wait_ge(scattered, 16 * NB)
                        sp.dma_start(at_start[:, :], a_starts.rearrange("(p t) f -> p (t f)", p=P)).then_inc(loaded, 16)

                    @block.vector
                    def _(dve):
                        then = chained(dve, chain)
                        dve.wait_ge(loaded, 16)
                        dve.wait_ge(firsts, 16)
                        then(dve.tensor_copy(at_start[:, 0:1], first[:, D:D + 1]))
                        then(dve.tensor_tensor_scan(at_start[:, :], cont[:, :], at_start[:, :], 0.0, ALU.mult, ALU.add))
                        then(dve.tensor_tensor(zk[:, :], zk[:, :], at_start[:, :], ALU.add))

        def split(dve, then, value, rest, parts):
            then(dve.tensor_copy(parts[..., 0], value))
            then(dve.tensor_tensor(rest, value, parts[..., 0], ALU.subtract))
            then(dve.tensor_copy(parts[..., 1], rest))
            then(dve.tensor_tensor(parts[..., 2], rest, parts[..., 1], ALU.subtract))

        def onehot(dve, out, values, g, width):
            return dve.tensor_tensor(out, mid(iota[:, 0:width], [P, GT, width]),
                                     bcast(values[:, bass.ds(g * GT, GT)], [P, GT, width]), ALU.is_equal)

        def tile_maxima(tag, parts, dest):
            with phase() as c:
                slot = sb(f"slot{tag}", [P, UNROLL, GT, TALL], BF16, c)
                left = sb(f"left{tag}", [TALL, UNROLL, GT * P], BF16, c)
                right = sb(f"right{tag}", [TALL, UNROLL, GT * P], BF16, c)
                scales = sb(f"scales{tag}", [TALL, 2], F32, c)
                pick = sb(f"pick{tag}", [TALL, P], BF16, c)
                bp = [pb(f"bp{tag}{j}", [TALL, GT * P], BF16, c) for j in range(2)]
                mp = [pb(f"mp{tag}{j}", [P, GT, P], F32, c) for j in range(2)]
                ready, cleared, slot_ready, turned, sides, pairs, topped, begun, chain = (
                    sem(f"m_{n}{tag}") for n in ("re", "cl", "sl", "tu", "si", "pa", "to", "be", "ch"))
                dig = digits[:, :].rearrange("p (t k) -> p t k", k=DIGITS)
                with nc.Block() as block:
                    @block.gpsimd
                    def _(pool):
                        static = parts.shape[1] == 1
                        pool.memset(slot[:, :, :, :], 0.0).then_inc(cleared, 1)
                        pool.wait_ge(cleared, 1)
                        if static:
                            pool.tensor_copy(slot[:, :, :, VALUE:TALL],
                                             parts[:, 0:1, :].unsqueeze(1).to_broadcast([P, UNROLL, GT, 3])).then_inc(cleared, 1)
                            pool.wait_ge(cleared, 2)
                        pool.sem_inc(turned, UNROLL)

                        def fill(g, u):
                            pool.wait_ge(turned, g + 1)
                            pool.sem_inc(begun, 1)
                            if not static:
                                pool.tensor_copy(slot[:, u, :, VALUE:TALL], parts[:, bass.ds(g * GT, GT), :])
                            pool.tensor_copy(slot[:, u, :, 0:DIGITS], dig[:, bass.ds(g * GT, GT), :]).then_inc(slot_ready, 1)

                        over_groups(pool, fill)

                    @block.tensor
                    def _(pe):
                        pe.wait_ge(ready, 2)

                        def turn(g, u):
                            pe.wait_ge(sides, g * 2 + 2)
                            pe.wait_ge(slot_ready, g + 1)
                            pe.sem_inc(begun, 1)
                            for t in range(GT):
                                last = pe.transpose(bp[u % 2][:, t * P:(t + 1) * P], slot[:, u, t], identb[:, :])
                            last.then_inc(turned, 1)

                        def pair(g, u):
                            pe.wait_ge(sides, g * 2 + 6)
                            pe.wait_ge(topped, g + 1)
                            for t in range(GT):
                                edge = slice(t * P, (t + 1) * P)
                                pe.matmul(mp[u % 2][:, t], left[:, u, edge], right[:, u, edge], start=t == 0, stop=False)
                            pe.matmul(mp[u % 2][:, :, :].rearrange("p t j -> p (t j)"), pick[:, :], right[:, u],
                                      start=False, stop=True).then_inc(pairs, 1)

                        over_groups_skewed(pe, turn, pair)

                    @block.scalar
                    def _(act):
                        act.sem_inc(sides, 4)
                        act.wait_ge(ready, 2)

                        def copy_rows(g, u):
                            act.wait_ge(turned, g + (UNROLL + 1))
                            act.wait_ge(topped, g + 1)
                            act.activation(left[:, u], bp[u % 2][:, :], ACT.Copy, scale=scales[:, 0:1]).then_inc(sides, 1)
                            act.activation(right[:, u], bp[u % 2][:, :], ACT.Copy, scale=scales[:, 1:2]).then_inc(sides, 1)

                        over_groups(act, copy_rows)

                    @block.vector
                    def _(dve):
                        dve.sem_inc(topped, 2)
                        then = chained(dve, chain)
                        then(dve.tensor_scalar(scales[:, 0:1], lane[0:TALL, :], float(BITS), None, ALU.is_le))
                        then(dve.tensor_scalar(scales[:, 1:2], lane[0:TALL, :], float(BITS), -(BITS + 1.0), ALU.is_equal, ALU.mult))
                        then(dve.tensor_scalar(scales[:, 1:2], scales[:, 1:2], 1.0, None, ALU.add))
                        dve.tensor_scalar(pick[:, :], ones[0:TALL, :], lane[0:TALL, 0:1], None, ALU.mult).then_inc(ready, 1)
                        dve.wait_ge(ready, 1)
                        dve.tensor_scalar(pick[:, :], pick[:, :], float(VALUE), None, ALU.is_ge).then_inc(ready, 1)

                        def maxima(g, u):
                            dve.wait_ge(pairs, g + 1)
                            dve.tensor_reduce(dest[:, bass.ds(g * GT, GT)], mp[u % 2][:, :, :], AX.X, ALU.max).then_inc(topped, 1)

                        over_groups(dve, maxima)

        def leaders():
            with phase() as c:
                own = sb("own", [P, 1, 3], BF16, c)
                begin = sem("l_be")
                with nc.Block() as block:
                    @block.vector
                    def _(dve):
                        dve.memset(own[:, :, :], 0.0).then_inc(begin, 1)
                        dve.wait_ge(begin, 1)
                        dve.tensor_copy(own[:, 0, 0:1], lane[:, :])
                tile_maxima("l", own[:, :, :], lead)
                chain = sem("l_ch")
                with nc.Block() as block:
                    @block.vector
                    def _(dve):
                        then = chained(dve, chain)
                        then(dve.tensor_scalar(lead[:, :], lead[:, :], lane[:, 0:1], None, ALU.is_equal))
                        then(dve.scalar_tensor_tensor(lead[:, :], blk[:, :], 1.0, lead[:, :], ALU.add, ALU.mult))
                        then(dve.tensor_scalar(lead[:, :], lead[:, :], -1.0, None, ALU.add))

        def peaks(tag, parts, peak):
            with phase() as c:
                hot_lo = sb(f"g_lo{tag}", [P, UNROLL, GT, P], BF16, c)
                hot_blk = sb(f"g_blk{tag}", [P, UNROLL, GT, NB], BF16, c)
                hot_big = sb(f"g_big{tag}", [P, UNROLL, GT, NB], BF16, c)
                hot_val = sb(f"g_val{tag}", [P, UNROLL, GT, 3, NB], BF16, c)
                best = sb(f"best{tag}", [P, NB], F32, c)
                minus_big = sb(f"mb{tag}", [1, GT * NB], BF16, c)
                one = sb(f"one{tag}", [1, P], BF16, c)
                gp = [pb(f"gp{tag}{j}", [P, GT, NB], F32, c) for j in range(2)]
                ready, hot_ready, big_ready, val_ready, grid, best_ready, peaked = (
                    sem(f"g_{n}{tag}") for n in ("re", "ho", "bi", "va", "gr", "be", "pe"))
                with nc.Block() as block:
                    @block.vector
                    def _(dve):
                        dve.memset(minus_big[:, :], -BIG).then_inc(ready, 1)
                        dve.memset(one[:, :], 1.0).then_inc(ready, 1)
                        dve.memset(peak[:, :], -BIG).then_inc(ready, 1)
                        dve.wait_ge(ready, 3)
                        dve.sem_inc(best_ready, 2)
                        dve.sem_inc(grid, UNROLL)
                        dve.sem_inc(peaked, 1)

                        def onehots(g, u):
                            dve.wait_ge(grid, g + 1)
                            onehot(dve, hot_blk[:, u], lead, g, NB).then_inc(hot_ready, 1)
                            onehot(dve, hot_lo[:, u], lo, g, P)
                            dve.wait_ge(hot_ready, g + 1)
                            dve.tensor_tensor(hot_val[:, u], hot_blk[:, u].unsqueeze(2).to_broadcast([P, GT, 3, NB]),
                                              parts[:, bass.ds(g * GT, GT), :].unsqueeze(3).to_broadcast([P, GT, 3, NB]),
                                              ALU.mult).then_inc(val_ready, 1)

                        def maxima(g, u):
                            dve.wait_ge(grid, g + (UNROLL + 1))
                            dve.wait_ge(peaked, g + 1)
                            dve.tensor_reduce(best[:, :], gp[u % 2][:, :, :].rearrange("p t b -> p b t"), AX.X,
                                              ALU.max).then_inc(best_ready, 1)
                            dve.wait_ge(best_ready, g + 3)
                            dve.tensor_tensor(peak[:, :], peak[:, :], best[:, :], ALU.max).then_inc(peaked, 1)

                        over_groups_skewed(dve, onehots, maxima)

                    @block.scalar
                    def _(act):
                        def scale_big(g, u):
                            act.wait_ge(hot_ready, g + 1)
                            act.activation(hot_big[:, u], hot_blk[:, u], ACT.Copy, scale=BIG).then_inc(big_ready, 1)

                        over_groups(act, scale_big)

                    @block.tensor
                    def _(pe):
                        pe.wait_ge(ready, 3)

                        def scatter(g, u):
                            pe.wait_ge(big_ready, g + 1)
                            pe.wait_ge(val_ready, g + 1)
                            pe.wait_ge(best_ready, g + 1)
                            pe.matmul(gp[u % 2][:, :, :].rearrange("p t b -> p (t b)"), one[:, :], minus_big[:, :],
                                      start=True, stop=False)
                            for t in range(GT):
                                pe.matmul(gp[u % 2][:, t], hot_lo[:, u, t], hot_big[:, u, t], start=False, stop=False)
                                for k in range(3):
                                    last = pe.matmul(gp[u % 2][:, t], hot_lo[:, u, t], hot_val[:, u, t, k], start=False,
                                                     stop=t == GT - 1 and k == 2)
                            last.then_inc(grid, 1)

                        over_groups(pe, scatter)

        def lookups(tag, pair, found):
            with phase() as c:
                pair_parts = sb(f"pp{tag}", [P, 3, 2 * NB], BF16, c)
                rest = sb(f"pr{tag}", [P, 2 * NB], F32, c)
                hot_lo = sb(f"x_lo{tag}", [P, UNROLL, GT, P], BF16, c)
                hot_t = sb(f"x_t{tag}", [P, 2, GT, P], BF16, c)
                hot_blk = sb(f"x_blk{tag}", [P, UNROLL, GT, NB], BF16, c)
                picked = sb(f"picked{tag}", [P, 2, GT, 2, NB], F32, c)
                tp = [pb(f"tp{tag}{j}", [P, GT, P], BF16, c) for j in range(2)]
                fp = [pb(f"fp{tag}{j}", [P, GT, 2, NB], F32, c) for j in range(2)]
                chain, hot_ready, turned, t_ready, found_ready, picked_ready, summed = (
                    sem(f"x_{n}{tag}") for n in ("ch", "ho", "tu", "t", "fo", "pi", "su"))
                with nc.Block() as block:
                    @block.vector
                    def _(dve):
                        then = chained(dve, chain)
                        split(dve, then, pair[:, :, :].rearrange("p k b -> p (k b)"), rest[:, :],
                              pair_parts[:, :, :].rearrange("p k n -> p n k"))
                        dve.sem_inc(picked_ready, 2)
                        dve.sem_inc(found_ready, 2)
                        dve.sem_inc(summed, 2)

                        def onehots(g, u):
                            dve.wait_ge(picked_ready, g + 1)
                            dve.wait_ge(t_ready, g + 1)
                            onehot(dve, hot_lo[:, u], lo, g, P).then_inc(hot_ready, 1)
                            onehot(dve, hot_blk[:, u], blk, g, NB).then_inc(hot_ready, 1)

                        def select(g, u):
                            dve.wait_ge(found_ready, g + 3)
                            dve.wait_ge(hot_ready, g * 2 + 2)
                            dve.wait_ge(summed, g + 1)
                            dve.tensor_tensor(picked[:, u % 2], fp[u % 2][:, :, :, :],
                                              hot_blk[:, u].unsqueeze(2).to_broadcast([P, GT, 2, NB]), ALU.mult).then_inc(picked_ready, 1)

                        def total(g, u):
                            dve.wait_ge(picked_ready, g + 3)
                            dve.tensor_reduce(found[:, bass.ds(g * GT, GT), :], picked[:, u % 2], AX.X, ALU.add).then_inc(summed, 1)

                        onehots(0, 0)
                        onehots(1, 1)
                        with dve.Fori(0, NG // UNROLL - 1) as i:
                            for u in range(UNROLL):
                                g = i * UNROLL + u
                                select(g, u)
                                onehots(g + 2, (u + 2) % UNROLL)
                                total(g, u)
                        for g in range(NG - UNROLL, NG):
                            select(g, g % UNROLL)
                            if g + 2 < NG:
                                onehots(g + 2, (g + 2) % UNROLL)
                            total(g, g % UNROLL)

                    @block.tensor
                    def _(pe):
                        pe.wait_ge(chain, 4)

                        def turn(g, u):
                            pe.wait_ge(hot_ready, g * 2 + 1)
                            pe.wait_ge(t_ready, g + 1)
                            for t in range(GT):
                                last = pe.transpose(tp[u % 2][:, t], hot_lo[:, u, t], identb[:, :])
                            last.then_inc(turned, 1)

                        def find(g, u):
                            pe.wait_ge(t_ready, g + 3)
                            pe.wait_ge(picked_ready, g + 1)
                            for t in range(GT):
                                for k in range(3):
                                    last = pe.matmul(fp[u % 2][:, t, :, :].rearrange("p k b -> p (k b)"), hot_t[:, u % 2, t],
                                                     pair_parts[:, k], start=k == 0, stop=k == 2)
                            last.then_inc(found_ready, 1)

                        over_groups_skewed(pe, turn, find)

                    @block.scalar
                    def _(act):
                        act.sem_inc(t_ready, 2)

                        def copy_hot(g, u):
                            act.wait_ge(turned, g + 1)
                            act.wait_ge(found_ready, g + 1)
                            act.activation(hot_t[:, u % 2], tp[u % 2][:, :, :], ACT.Copy).then_inc(t_ready, 1)

                        over_groups(act, copy_hot)

        def sums_by_src(tag, parts, total):
            with phase() as c:
                hot_lo = sb(f"u_lo{tag}", [P, UNROLL, GT, P], BF16, c)
                hot_blk = sb(f"u_blk{tag}", [P, UNROLL, GT, NB], BF16, c)
                hot_val = sb(f"u_val{tag}", [P, UNROLL, GT, 3, NB], BF16, c)
                sums = pb(f"sums{tag}", [P, NB], F32, c)
                hot_ready, val_ready, added = (sem(f"u_{n}{tag}") for n in ("ho", "va", "ad"))
                with nc.Block() as block:
                    @block.vector
                    def _(dve):
                        def weighed(g, u):
                            dve.wait_ge(added, g + 1)
                            onehot(dve, hot_blk[:, u], blk, g, NB).then_inc(hot_ready, 1)
                            onehot(dve, hot_lo[:, u], lo, g, P)
                            dve.wait_ge(hot_ready, g + 1)
                            dve.tensor_tensor(hot_val[:, u], hot_blk[:, u].unsqueeze(2).to_broadcast([P, GT, 3, NB]),
                                              parts[:, bass.ds(g * GT, GT), :].unsqueeze(3).to_broadcast([P, GT, 3, NB]),
                                              ALU.mult).then_inc(val_ready, 1)

                        over_groups(dve, weighed)
                        dve.wait_ge(added, NG + UNROLL)
                        dve.tensor_copy(total, sums[:, :])

                    @block.tensor
                    def _(pe):
                        pe.sem_inc(added, UNROLL)

                        def add(g, u, start=False, stop=False):
                            pe.wait_ge(val_ready, g + 1)
                            for t in range(GT):
                                for k in range(3):
                                    last = pe.matmul(sums[:, :], hot_lo[:, u, t], hot_val[:, u, t, k],
                                                     start=start and t == 0 and k == 0, stop=stop and t == GT - 1 and k == 2)
                            last.then_inc(added, 1)

                        accumulate(pe, add)

        def softmax_terms(tag, zk, xn):
            with phase() as c:
                parts = sb(f"parts{tag}", [P, W, 3], BF16, c)
                top = sb(f"top{tag}", [P, W], F32, c)
                peak = sb(f"peak{tag}", [P, NB], F32, c)
                pair = sb(f"pair{tag}", [P, 2, NB], F32, c)
                tmp = sb(f"a_tmp{tag}", [P, NB], F32, c)
                found = sb(f"found{tag}", [P, W, 2], F32, c)
                chain, chain2, exped, chain3, chain4, inverted, stored = (
                    sem(f"a_{n}{tag}") for n in ("c1", "c2", "ex", "c3", "c4", "in", "st"))
                with nc.Block() as block:
                    @block.vector
                    def _(dve):
                        split(dve, chained(dve, chain), zk[:, :], top[:, :], parts[:, :, :])
                tile_maxima(tag, parts[:, :, :], top)
                with nc.Block() as block:
                    @block.vector
                    def _(dve):
                        split(dve, chained(dve, chain2), top[:, :], found[:, :, 0], parts[:, :, :])
                peaks(tag, parts, peak)
                with nc.Block() as block:
                    @block.vector
                    def _(dve):
                        then = chained(dve, chain3)
                        then(dve.tensor_copy(pair[:, 0], xn[:, :, D + 1]))
                        then(dve.tensor_tensor(tmp[:, :], xn[:, :, D + 1], peak[:, :], ALU.add))
                        then(dve.scalar_tensor_tensor(pair[:, 1], tmp[:, :], 0.01, tmp[:, :], ALU.mult, ALU.max))
                lookups(tag, pair, found)
                with nc.Block() as block:
                    @block.vector
                    def _(dve):
                        then = chained(dve, chain4)
                        then(dve.tensor_tensor(zk[:, :], zk[:, :], found[:, :, 0], ALU.add))
                        then(dve.scalar_tensor_tensor(zk[:, :], zk[:, :], 0.01, zk[:, :], ALU.mult, ALU.max))
                        then(dve.tensor_tensor(zk[:, :], zk[:, :], found[:, :, 1], ALU.subtract))
                        dve.wait_ge(exped, 1)
                        split(dve, then, zk[:, :], top[:, :], parts[:, :, :])

                    @block.scalar
                    def _(act):
                        act.wait_ge(chain4, 3)
                        act.activation(zk[:, :], zk[:, :], ACT.Exp).then_inc(exped, 1)
                sums_by_src(tag, parts, tmp[:, :])
                with nc.Block() as block:
                    @block.vector
                    def _(dve):
                        dve.tensor_scalar(tmp[:, :], tmp[:, :], 1e-16, None, ALU.add).then_inc(inverted, 1)
                        dve.wait_ge(inverted, 1)
                        dve.reciprocal(xn[:, :, D + 2], tmp[:, :]).then_inc(inverted, 1)

                    @block.sync
                    def _(sp):
                        sp.wait_ge(inverted, 2)
                        sp.dma_start(table[0:NP, :].rearrange("(b p) f -> p b f", p=P), xn[:, :, :]).then_inc(stored, 16)
                        sp.wait_ge(stored, 16)

        def chunk_carries(tag, last, width, peak, dest):
            with phase() as c:
                seg = sb(f"seg{tag}", [width, 3, P], F32, c)
                run = sb(f"run{tag}", [width, P], F32, c)
                carry = sb(f"carry{tag}", [width, P], F32, c)
                pen = sb(f"pen{tag}", [width, P], F32, c)
                back = sb(f"back{tag}", [P, width], F32, c)
                sp_full = pb(f"segp{tag}", [P, 512], F32, c)
                sp_ = sp_full[0:width, :]
                turned, chain, copied, stored = (sem(f"k_{n}{tag}") for n in ("tu", "ch", "co", "st"))
                chain_steps = 7 if peak else 4
                with nc.Block() as block:
                    @block.tensor
                    def _(pe):
                        for k, m in enumerate((last, through[:, 0:1].to_broadcast([P, width]),
                                               strad[:, 0:1].to_broadcast([P, width]))):
                            ins = pe.transpose(sp_[:, k * P:(k + 1) * P], m, ident[:, :])
                        ins.then_inc(turned, 1)
                        pe.wait_ge(chain, chain_steps)
                        pe.transpose(sp_full[:, 0:width], carry[:, :], ident[0:width, 0:width]).then_inc(turned, 1)

                    @block.vector
                    def _(dve):
                        then = chained(dve, chain)
                        dve.wait_ge(turned, 1)
                        then(dve.tensor_copy(seg[:, :, :], sp_[:, 0:3 * P].rearrange("f (k p) -> f k p", k=3)))
                        if peak:
                            then(dve.tensor_scalar(pen[:, :], seg[:, 1], BIG, -BIG, ALU.mult, ALU.add))
                            then(dve.tensor_tensor_scan(run[:, :], pen[:, :], seg[:, 0], -BIG, ALU.add, ALU.max))
                        else:
                            then(dve.tensor_tensor_scan(run[:, :], seg[:, 1], seg[:, 0], 0.0, ALU.mult, ALU.add))
                        then(dve.memset(carry[:, 0:1], -BIG if peak else 0.0))
                        then(dve.tensor_tensor(carry[:, 1:P], run[:, 0:P - 1], seg[:, 2, 1:P], ALU.mult))
                        if peak:
                            then(dve.tensor_scalar(pen[:, :], seg[:, 2], BIG, -BIG, ALU.mult, ALU.add))
                            then(dve.tensor_tensor(carry[:, 1:P], carry[:, 1:P], pen[:, 1:P], ALU.add))
                        dve.wait_ge(turned, 2)
                        dve.tensor_copy(back[:, :], sp_full[:, 0:width]).then_inc(copied, 1)

                    @block.sync
                    def _(sp):
                        sp.wait_ge(copied, 1)
                        sp.dma_start(dest[0:P, 0:width], back[:, :]).then_inc(stored, 16)
                        sp.wait_ge(stored, 16)

        def messages(tag, ex):
            with phase() as c:
                got = sb(f"got{tag}", [P, UNROLL, GT, TW], F32, c)
                att = sb(f"s_att{tag}", [P, UNROLL, GT, R], F32, c)
                msg = sb(f"msg{tag}", [P, UNROLL, GT, M], F32, c)
                acc = sb(f"acc{tag}", [P, UNROLL, GT, M], F32, c)
                gathered = [lasting(f"s_ga{tag}{u}") for u in range(UNROLL)]
                att_in = [sem(f"s_at{tag}{u}") for u in range(UNROLL)]
                stored = [sem(f"s_st{tag}{u}") for u in range(UNROLL)]
                index = sb(f"index{tag}", [P, UNROLL, GT], I32, c)
                index_ready, begun = sem(f"s_ix{tag}"), sem(f"s_be{tag}")
                weighed, msg_ready, summed = sem(f"s_we{tag}"), sem(f"s_ms{tag}"), sem(f"s_su{tag}")
                with nc.Block() as block:
                    @block.gpsimd
                    def _(pool):
                        with pool.Fori(0, NG // UNROLL) as i:
                            for u in range(UNROLL):
                                g = i * UNROLL + u
                                pool.wait_ge(index_ready, g + 1)
                                pool.sem_inc(begun, 1)
                                for t in range(GT):
                                    pool.indirect_dma_start(got[:, u, t], None, table, bass.IndirectOffsetOnAxis(
                                        ap=index[:, u, t:t + 1], axis=0)).then_inc(gathered[u], 16)

                    @block.sync
                    def _(sp):
                        with sp.Fori(0, NG // UNROLL) as i:
                            for u in range(UNROLL):
                                g = i * UNROLL + u
                                sp.wait_ge(msg_ready, g * 2 + 2)
                                sp.dma_start(att[:, u], attr[:, bass.ds(g * GT, GT), :]).then_inc(att_in[u], 16)

                    @block.vector
                    def _(dve):
                        dve.sem_inc(msg_ready, 2 * UNROLL)
                        dve.memset(acc[:, UNROLL - 1, GT - 1], 0.0).then_inc(summed, 1)

                        def group(g, u, i=None):
                            dve.wait_ge(gathered[u], 16 * GT if i is None else i * (16 * GT) + 16 * GT)
                            dve.wait_ge(att_in[u], 16 if i is None else i * 16 + 16)
                            dve.wait_ge(summed, g * GT + 1)
                            w = msg[:, u, :, M - 1]
                            dve.tensor_tensor(w, got[:, u, :, D + 2], ex[:, bass.ds(g * GT, GT)], ALU.mult).then_inc(weighed, 1)
                            dve.wait_ge(weighed, g + 1)
                            dve.tensor_tensor(msg[:, u, :, 0:D], got[:, u, :, 0:D], bcast(w, [P, GT, D]), ALU.mult).then_inc(msg_ready, 1)
                            dve.tensor_tensor(msg[:, u, :, D:D + R], att[:, u], bcast(w, [P, GT, R]), ALU.mult).then_inc(msg_ready, 1)
                            dve.wait_ge(msg_ready, g * 2 + (2 * UNROLL + 2))
                            if i is not None:
                                dve.wait_ge(stored[u], i * 16)
                            for t in range(GT):
                                before = acc[:, u, t - 1] if t else acc[:, (u - 1) % UNROLL, GT - 1]
                                if t:
                                    dve.wait_ge(summed, g * GT + t + 1)
                                dve.scalar_tensor_tensor(acc[:, u, t], before, cont[:, bass.ds(g * GT + t, 1)], msg[:, u, t],
                                                         ALU.mult, ALU.add).then_inc(summed, 1)

                        for u in range(UNROLL):
                            group(u, u)
                        with dve.Fori(1, NG // UNROLL) as i:
                            for u in range(UNROLL):
                                group(i * UNROLL + u, u, i)

                    @block.scalar
                    def _(act):
                        wide = rows[0:EP, :].rearrange("(p t) f -> p t f", p=P)

                        def indices(g, u):
                            act.wait_ge(msg_ready, g * 2 + 2)
                            act.activation(index[:, u], src_i[:, bass.ds(g * GT, GT)], ACT.Copy).then_inc(index_ready, 1)

                        def store(g, u):
                            act.wait_ge(summed, g * GT + (GT + 1))
                            act.dma_start(wide[:, bass.ds(g * GT, GT), :], acc[:, u]).then_inc(stored[u], 16)

                        over_groups_ahead(act, indices, store)
                        for u in range(UNROLL):
                            act.wait_ge(stored[u], 16 * (NG // UNROLL))
                chunk_carries(f"s{tag}", acc[:, UNROLL - 1, GT - 1], M, False, carries)

        def node_rows(tag, source, carried, width, dest, extra):
            with phase() as c:
                fetched = lasting(f"r_fe{tag}")
                with nc.Block() as block:
                    @block.gpsimd
                    def _(pool):
                        for b in range(NB):
                            pool.indirect_dma_start(dest[:, b], None, source, bass.IndirectOffsetOnAxis(
                                ap=end_i[:, b:b + 1], axis=0)).then_inc(fetched, 16)
                            pool.indirect_dma_start(extra[:, b], None, carried, bass.IndirectOffsetOnAxis(
                                ap=carry_i[:, b:b + 1], axis=0)).then_inc(fetched, 16)
                        pool.wait_ge(fetched, 32 * NB)

        def convolved(tag):
            with phase() as c:
                agg = sb(f"agg{tag}", [P, NB, M], F32, c)
                more = sb(f"more{tag}", [P, NB, M], F32, c)
                et = sb(f"et{tag}", [R + 1, 7 * P], F32, c)
                tp = pb(f"ctp{tag}", [R + 1, 1024], F32, c)
                ep = pb(f"cep{tag}", [P, 512], F32, c)
                node_rows(tag, rows, carries, M, agg, more)
                summed, turned, copied, e_ready, added = (sem(f"c_{n}{tag}") for n in ("su", "tu", "co", "e", "ad"))
                with nc.Block() as block:
                    @block.vector
                    def _(dve):
                        dve.tensor_tensor(agg[:, :, :], agg[:, :, :], more[:, :, :], ALU.add).then_inc(summed, 1)
                        dve.wait_ge(summed, 1)
                        for j in range(NB // 7):
                            part = slice(7 * j, 7 * j + 7)
                            dve.wait_ge(e_ready, j + 1)
                            dve.tensor_tensor(h[:, part, :], agg[:, part, 0:D], ep[:, 0:7 * D].rearrange("p (b f) -> p b f", f=D),
                                              ALU.add).then_inc(added, 1)
                        dve.wait_ge(added, NB // 7)
                        dve.tensor_scalar(h[:, :, :], h[:, :, :], 0.0, None, ALU.max)

                    @block.tensor
                    def _(pe):
                        pe.wait_ge(summed, 1)
                        for j in range(NB // 7):
                            if j:
                                pe.wait_ge(copied, j)
                            for b7 in range(7):
                                last = pe.transpose(tp[:, b7 * P:(b7 + 1) * P], agg[:, 7 * j + b7, D:M], ident[:, :])
                            last.then_inc(turned, 1)
                            pe.wait_ge(copied, j + 1)
                            if j:
                                pe.wait_ge(added, j)
                            for b7 in range(7):
                                last = pe.matmul(ep[:, b7 * D:(b7 + 1) * D], et[:, b7 * P:(b7 + 1) * P], rel_t[:, :],
                                                 start=True, stop=True)
                            last.then_inc(e_ready, 1)

                    @block.scalar
                    def _(act):
                        for j in range(NB // 7):
                            act.wait_ge(turned, j + 1)
                            if j:
                                act.wait_ge(e_ready, j)
                            act.activation(et[:, :], tp[:, 0:7 * P], ACT.Copy).then_inc(copied, 1)

        norm_relu("a")
        edge_terms()
        leaders()
        for k, (w, b, ai_w, aj_w) in enumerate(((c1_w, c1_b, c1_ai_w, c1_aj_w), (c2_w, c2_b, c2_ai_w, c2_aj_w))):
            with phase() as c:
                xn = sb(f"xn{k}", [P, NB, TW], F32, c)
                project(k, w, b, ai_w, aj_w, xn)
                expand(k, xn, z[k])
                softmax_terms(k, z[k], xn)
            messages(k, z[k])
            convolved(k)
        with phase() as c:
            with nc.Block() as block:
                @block.vector
                def _(dve):
                    dve.tensor_tensor(x_sb[:, :, :], x_sb[:, :, :], h[:, :, :], ALU.add)
        norm_relu("b")

        w2_sb = sb("w2_sb", [2 * D, D], F32)
        b2_sb = sb("b2_sb", [P, D], F32)
        with phase() as c:
            wt = sb("wt", [D + 1, 2, D], F32, c)
            ht = sb("w_ht", [D + 1, 7 * P], F32, c)
            ab = sb("ab", [P, NB, 2, D], F32, c)
            hp = pb("w_hp", [P, 1024], F32, c)
            xp = pb("w_xp", [P, 1024], F32, c)
            w_in, w_ready, turned, ht_ready, x_ready, x_copied, stored = (sem(f"w_{n}") for n in ("in", "re", "tu", "ht", "xr", "xc", "st"))
            starts, firsts = lasting("w_starts"), lasting("w_firsts")
            first = sb("w_first", [P, D], F32, c)
            with nc.Block() as block:
                @block.sync
                def _(sp):
                    sp.dma_start(wt[0:D, 0], w1[0:D, :]).then_inc(w_in, 16)
                    sp.dma_start(wt[0:D, 1], w1[D:2 * D, :]).then_inc(w_in, 16)
                    sp.dma_start(wt[D:D + 1, 0], b1.rearrange("(a d) -> a d", a=1)).then_inc(w_in, 16)
                    sp.dma_start(w2_sb[0:D, :], w2).then_inc(w_in, 16)
                    sp.dma_start(w2_sb[D:2 * D, :], w2).then_inc(w_in, 16)
                    sp.dma_start(b2_sb[:, :], b2.partition_broadcast(P)).then_inc(w_in, 16)
                    sp.wait_ge(x_copied, NB // 7)
                    sp.dma_start(a_table[0:NP, :].rearrange("(b p) f -> p b f", p=P), ab[:, :, 0]).then_inc(stored, 16)
                    sp.dma_start(b_table[0:NP, :].rearrange("(b p) f -> p b f", p=P), ab[:, :, 1]).then_inc(stored, 16)
                    sp.wait_ge(stored, 32)
                    sp.wait_ge(firsts, 16)
                    sp.wait_ge(starts, 16 * NB)
                    sp.dma_start(row_starts.rearrange("(p t) f -> p t f", p=P)[:, 0, :], first[:, :]).then_inc(stored, 16)
                    sp.wait_ge(stored, 48)

                @block.gpsimd
                def _(pool):
                    pool.wait_ge(x_copied, NB // 7)
                    for b in range(NB):
                        pool.indirect_dma_start(row_starts, bass.IndirectOffsetOnAxis(ap=start_i[:, b:b + 1], axis=0),
                                                ab[:, b, 0], None, bounds_check=EP - 1, oob_is_err=False).then_inc(starts, 16)
                    pool.wait_ge(stored, 32)
                    pool.indirect_dma_start(first[:, :], None, a_table, bass.IndirectOffsetOnAxis(
                        ap=dst0_i[:, 0:1], axis=0)).then_inc(firsts, 16)

                @block.tensor
                def _(pe):
                    for j in range(NB // 7):
                        if j:
                            pe.wait_ge(ht_ready, j)
                        for b7 in range(7):
                            last = pe.transpose(hp[0:D, b7 * P:(b7 + 1) * P], h[:, 7 * j + b7, :], ident[:, :])
                        last.then_inc(turned, 1)
                        pe.wait_ge(ht_ready, j + 1)
                        pe.wait_ge(w_ready, 3)
                        if j:
                            pe.wait_ge(x_copied, j)
                        for b7 in range(7):
                            last = pe.matmul(xp[:, b7 * 2 * D:(b7 + 1) * 2 * D], ht[:, b7 * P:(b7 + 1) * P],
                                             wt[:, :, :].rearrange("p k f -> p (k f)"), start=True, stop=True)
                        last.then_inc(x_ready, 1)

                @block.scalar
                def _(act):
                    for j in range(NB // 7):
                        act.wait_ge(turned, j + 1)
                        if j:
                            act.wait_ge(x_ready, j)
                        act.activation(ht[0:D, :], hp[0:D, 0:7 * P], ACT.Copy).then_inc(ht_ready, 1)

                @block.vector
                def _(dve):
                    dve.memset(ht[D:D + 1, :], 1.0).then_inc(w_ready, 1)
                    dve.memset(wt[D:D + 1, 1], 0.0).then_inc(w_ready, 1)
                    dve.wait_ge(w_in, 96)
                    dve.tensor_tensor(wt[0:D, 0], wt[0:D, 0], wt[0:D, 1], ALU.subtract).then_inc(w_ready, 1)
                    for j in range(NB // 7):
                        dve.wait_ge(x_ready, j + 1)
                        dve.tensor_copy(ab[:, 7 * j:7 * j + 7].rearrange("p b k f -> p (b k f)"), xp[:, 0:14 * D]).then_inc(x_copied, 1)

        with phase() as c:
            got = sb("e_got", [P, UNROLL, GT, D], F32, c)
            rs = sb("e_rs", [P, UNROLL, GT, D], F32, c)
            a_row = sb("e_a", [P, UNROLL, GT, D], F32, c)
            pre = sb("e_pre", [P, UNROLL, GT, D], F32, c)
            hid = sb("e_hid", [2 * D, UNROLL, GT // 2 * P], F32, c)
            acc = sb("e_acc", [P, UNROLL, GT, D], F32, c)
            pen = sb("e_pen", [P, W], F32, c)
            tp = [pb(f"e_tp{j}", [2 * D, GT // 2 * P], F32, c) for j in range(2)]
            mp = [[pb(f"e_mp{j}{k}", [P, GT // 2, D], F32, c) for k in range(2)] for j in range(2)]
            index = sb("e_index", [P, UNROLL, GT], I32, c)
            index_ready, begun = sem("e_ix"), sem("e_be")
            gathered = [lasting(f"e_ga{u}") for u in range(UNROLL)]
            rs_in = [sem(f"e_rs{u}") for u in range(UNROLL)]
            stored = [sem(f"e_st{u}") for u in range(UNROLL)]
            ready, a_ready, pre_ready, turned, hid_ready, m_ready, maxed = (sem(f"e_{n}") for n in ("re", "ar", "pr", "tu", "hi", "me", "ma"))
            with nc.Block() as block:
                @block.gpsimd
                def _(pool):
                    with pool.Fori(0, NG // UNROLL) as i:
                        for u in range(UNROLL):
                            g = i * UNROLL + u
                            pool.wait_ge(index_ready, g + 1)
                            pool.sem_inc(begun, 1)
                            for t in range(GT):
                                pool.indirect_dma_start(got[:, u, t], None, b_table, bass.IndirectOffsetOnAxis(
                                    ap=index[:, u, t:t + 1], axis=0)).then_inc(gathered[u], 16)

                @block.sync
                def _(sp):
                    wide = row_starts.rearrange("(p t) f -> p t f", p=P)
                    with sp.Fori(0, NG // UNROLL) as i:
                        for u in range(UNROLL):
                            g = i * UNROLL + u
                            sp.wait_ge(pre_ready, g + 1)
                            sp.dma_start(rs[:, u], wide[:, bass.ds(g * GT, GT), :]).then_inc(rs_in[u], 16)

                @block.vector
                def _(dve):
                    dve.memset(acc[:, UNROLL - 1, GT - 1], -BIG).then_inc(ready, 1)
                    dve.memset(a_row[:, UNROLL - 1, GT - 1], 0.0).then_inc(ready, 1)
                    dve.tensor_scalar(pen[:, :], cont[:, :], BIG, -BIG, ALU.mult, ALU.add).then_inc(ready, 1)
                    dve.wait_ge(ready, 3)
                    dve.sem_inc(pre_ready, UNROLL)
                    dve.sem_inc(a_ready, 1)
                    dve.sem_inc(maxed, 2 * GT)

                    def before(g, u, i):
                        dve.wait_ge(rs_in[u], i * 16 + 16)
                        for t in range(GT):
                            prev = a_row[:, u, t - 1] if t else a_row[:, (u - 1) % UNROLL, GT - 1]
                            dve.wait_ge(a_ready, g * GT + (t + 1))
                            dve.scalar_tensor_tensor(a_row[:, u, t], prev, cont[:, bass.ds(g * GT + t, 1)], rs[:, u, t],
                                                     ALU.mult, ALU.add).then_inc(a_ready, 1)
                            yield

                    def plus(g, u, i):
                        dve.wait_ge(a_ready, g * GT + (GT + 1))
                        dve.wait_ge(gathered[u], i * (16 * GT) + 16 * GT)
                        dve.wait_ge(turned, g + 1)
                        dve.tensor_tensor(pre[:, u], a_row[:, u], got[:, u], ALU.add).then_inc(pre_ready, 1)

                    def after(g, u, i=None):
                        dve.wait_ge(m_ready, g + 1)
                        if i is not None:
                            dve.wait_ge(stored[u], i * 16)
                        for t in range(GT):
                            prev = acc[:, u, t - 1] if t else acc[:, (u - 1) % UNROLL, GT - 1]
                            dve.wait_ge(maxed, g * GT + (t + 2 * GT))
                            dve.scalar_tensor_tensor(acc[:, u, t], prev, pen[:, bass.ds(g * GT + t, 1)],
                                                     mp[u % 2][t % 2][:, t // 2],
                                                     ALU.add, ALU.max).then_inc(maxed, 1)
                            yield

                    dve.sem_inc(turned, UNROLL)

                    def step(g, u, i, iu=None):
                        ahead, au = i + (u + 2) // UNROLL, (u + 2) % UNROLL
                        for _ in zip(before(g + 2, au, ahead), after(g, u, iu)):
                            pass
                        plus(g + 2, au, ahead)

                    for g in range(2):
                        for _ in before(g, g, 0):
                            pass
                        plus(g, g, 0)
                    for u in range(UNROLL):
                        step(u, u, 0)
                    with dve.Fori(1, NG // UNROLL - 1) as i:
                        for u in range(UNROLL):
                            step(i * UNROLL + u, u, i, i)
                    for g in range(NG - UNROLL, NG):
                        if g + 2 < NG:
                            step(g, g % UNROLL, g // UNROLL, g // UNROLL)
                        else:
                            for _ in after(g, g % UNROLL, g // UNROLL):
                                pass

                @block.tensor
                def _(pe):
                    def turn(g, u):
                        pe.wait_ge(pre_ready, g + (UNROLL + 1))
                        pe.wait_ge(hid_ready, g + 1)
                        for t in range(0, GT, 2):
                            last = pe.transpose(tp[u % 2][:, t // 2 * P:(t // 2 + 1) * P],
                                                pre[:, u, t:t + 2].rearrange("p t f -> p (t f)"), ident[:, :])
                        last.then_inc(turned, 1)

                    def multiply(g, u):
                        pe.wait_ge(hid_ready, g + 3)
                        pe.wait_ge(maxed, g * GT + GT)
                        for t in range(GT):
                            half = slice(t % 2 * D, t % 2 * D + D)
                            last = pe.matmul(mp[u % 2][t % 2][:, t // 2], hid[half, u, t // 2 * P:(t // 2 + 1) * P], w2_sb[half, :],
                                             start=True, stop=True)
                        last.then_inc(m_ready, 1)

                    over_groups_skewed(pe, turn, multiply)

                @block.scalar
                def _(act):
                    act.sem_inc(hid_ready, 2)
                    wide = peak_rows[0:EP, :].rearrange("(p t) f -> p t f", p=P)

                    def relu(g, u):
                        act.wait_ge(turned, g + (UNROLL + 1))
                        act.activation(hid[:, u], tp[u % 2][:, :], ACT.Relu).then_inc(hid_ready, 1)

                    def store(g, u):
                        act.wait_ge(maxed, g * GT + 3 * GT)
                        act.dma_start(wide[:, bass.ds(g * GT, GT), :], acc[:, u]).then_inc(stored[u], 16)

                    def indices(g, u):
                        act.wait_ge(pre_ready, g + 1)
                        act.activation(index[:, u], src_i[:, bass.ds(g * GT, GT)], ACT.Copy).then_inc(index_ready, 1)

                    for u in range(UNROLL):
                        indices(u, u)
                    relu(0, 0)
                    relu(1, 1)
                    with act.Fori(0, NG // UNROLL - 1) as i:
                        for u in range(UNROLL):
                            indices(i * UNROLL + (u + UNROLL), u)
                            relu(i * UNROLL + (u + 2), (u + 2) % UNROLL)
                            store(i * UNROLL + u, u)
                    for g in range(NG - UNROLL, NG):
                        if g + 2 < NG:
                            relu(g + 2, (g + 2) % UNROLL)
                        store(g, g % UNROLL)
                    for u in range(UNROLL):
                        act.wait_ge(stored[u], 16 * (NG // UNROLL))
            chunk_carries("m", acc[:, UNROLL - 1, GT - 1], D, True, peak_carries)

        with phase() as c:
            agg = sb("f_agg", [P, NB, D], F32, c)
            more = sb("f_more", [P, NB, D], F32, c)
            node_rows("m", peak_rows, peak_carries, D, agg, more)
            chain, done, stored = sem("f_chain"), sem("f_done"), sem("f_stored")
            with nc.Block() as block:
                @block.vector
                def _(dve):
                    then = chained(dve, chain)
                    then(dve.tensor_tensor(agg[:, :, :], agg[:, :, :], more[:, :, :], ALU.max))
                    then(dve.tensor_tensor(agg[:, :, :], agg[:, :, :], mid(b2_sb[:, :], [P, NB, D]), ALU.add))
                    then(dve.tensor_tensor(agg[:, :, :], agg[:, :, :], bcast(has[:, :], [P, NB, D]), ALU.mult))
                    dve.tensor_tensor(agg[:, :, :], agg[:, :, :], x_sb[:, :, :], ALU.add).then_inc(done, 1)

                @block.sync
                def _(sp):
                    sp.wait_ge(done, 1)
                    full = N // P
                    sp.dma_start(out[0:full * P, :].rearrange("(b p) f -> p b f", p=P), agg[:, 0:full]).then_inc(stored, 16)
                    sp.dma_start(out[full * P:N, :], agg[0:N - full * P, full]).then_inc(stored, 16)
                    sp.wait_ge(stored, 32)


def bass_col(ap):
    return ap.rearrange("(d a) -> d a", a=1)


def accumulate(pe, add_group):
    for g in range(UNROLL):
        add_group(g, g, start=g == 0)
    with pe.Fori(0, NG // UNROLL - 2) as i:
        for u in range(UNROLL):
            add_group(i * UNROLL + (UNROLL + u), u)
    for g in range(NG - UNROLL, NG):
        add_group(g, g % UNROLL, stop=g == NG - 1)

_C = ("lin_w", "lin_b", "ai_w", "ai_b", "aj_w", "aj_b", "ew_w", "ew_b")
ORDER = (["x", "src", "dst", "edge_attr_32", "L0_gnn_rel_w", "L0_gnn_rel_b"]
         + [f"L0_gnn_c{k}_{n}" for k in (1, 2) for n in _C]
         + ["L1_gnn_W1", "L1_gnn_b1", "L1_gnn_W2", "L1_gnn_b2"])


def kernel(**inputs):
    import numpy as np
    import concourse.bacc as bacc
    from concourse.bass_utils import run_bass_kernel_spmd

    def edges(a, fill):
        a = np.asarray(a)
        pad = [(0, EP - E)] + [(0, 0)] * (a.ndim - 1)
        return np.ascontiguousarray(np.pad(a, pad, constant_values=fill).reshape((P, W) + a.shape[1:]))

    arrays = {k: np.ascontiguousarray(np.asarray(a)) for k, a in inputs.items()}
    arrays["x"] = np.pad(arrays["x"], [(0, NP - N), (0, 0)])
    arrays["src"] = edges(inputs["src"], PAD_NODE)
    arrays["dst"] = edges(inputs["dst"], PAD_NODE)
    arrays["edge_attr_32"] = edges(inputs["edge_attr_32"], 0)
    nc = bacc.Bacc("TRN2", target_bir_lowering=False, num_devices=1)
    fed, args = {}, []
    for name in ORDER:
        fed[f"in_{name}"] = arrays[name]
        args.append(nc.dram_tensor(f"in_{name}", arrays[name].shape, mybir.dt.from_np(arrays[name].dtype),
                                   kind="ExternalInput").ap())
    out = nc.dram_tensor("out", [N, D], F32, kind="ExternalOutput").ap()
    gnn_kernel(nc, *args, out)
    return run_bass_kernel_spmd(nc, [fed], core_ids=[0]).results[0]["out"]
```

```python
import concourse.bass as bass
from concourse import mybir
from contextlib import ExitStack, contextmanager

F32 = mybir.dt.float32
BF16 = mybir.dt.bfloat16
I32 = mybir.dt.int32
ALU = mybir.AluOpType
ACT = mybir.ActivationFunctionType
AX = mybir.AxisListType

N = 6250
E = 206250
D = 64
R = 32
P = 128
NB = -(-N // P)
NP = NB * P
TABLE = NP + P
PAD_NODE = TABLE - 1
GT = 4
UNROLL = 4
W = -(-E // (P * GT * UNROLL)) * GT * UNROLL
EP = P * W
NG = W // GT
TW = D + 3
M = D + R + 1
BITS = 13
DIGITS = 16
LOW = P.bit_length() - 1
FB = 2
VALUE = BITS + 1
TALL = 64
HALF = GT // 2
SIGN = 2.0 ** 50
BIG = SIGN * SIGN
SKIP = 1 << 29
EPS = 1e-5
assert N <= 1 << BITS and PAD_NODE < 1 << BITS


def bcast(ap, shape):
    return ap.unsqueeze(len(shape) - 1).to_broadcast(shape)


def mid(ap, shape):
    return ap.unsqueeze(1).to_broadcast(shape)


def over_groups(eng, stage):
    with eng.Fori(0, NG // UNROLL) as i:
        for u in range(UNROLL):
            stage(i * UNROLL + u, u)


def over_groups_skewed(eng, first, second, ahead=1):
    for g in range(ahead):
        first(g, g)
    with eng.Fori(0, NG // UNROLL - 1) as i:
        for u in range(UNROLL):
            first(i * UNROLL + (u + ahead), (u + ahead) % UNROLL)
            second(i * UNROLL + u, u)
    for g in range(NG - UNROLL, NG):
        if g + ahead < NG:
            first(g + ahead, (g + ahead) % UNROLL)
        second(g, g % UNROLL)


def gnn_kernel(nc, x, src, dst, attr, rel_w, rel_b,
               c1_w, c1_b, c1_ai_w, c1_ai_b, c1_aj_w, c1_aj_b, c1_ew_w, c1_ew_b,
               c2_w, c2_b, c2_ai_w, c2_ai_b, c2_aj_w, c2_aj_b, c2_ew_w, c2_ew_b,
               w1, b1, w2, b2, out):
    ctx = ExitStack()
    with ctx:
        ctx.enter_context(nc.allow_non_contiguous_dma(reason="columns of a few numbers"))
        def sb(name, shape, dt, c=ctx):
            return c.enter_context(nc.sbuf_tensor(name, shape, dt))

        def pb(name, shape, dt, c):
            return c.enter_context(nc.psum_tensor(name, shape, dt))

        phases = []

        @contextmanager
        def phase():
            with ExitStack() as c:
                phases.append((c, []))
                yield c
                own = phases.pop()[1]
                if own:
                    with nc.Block() as block:
                        @block.gpsimd
                        def _(pool):
                            for s in own:
                                pool.sem_clear(s)

        def sem(name):
            c, own = phases[-1]
            own.append(c.enter_context(nc.semaphore(name)))
            return own[-1]

        def dram(name, shape, dt):
            return nc.dram_tensor(name, shape, dt, kind="Internal").ap()

        def lasting(name):
            return ctx.enter_context(nc.semaphore(name))

        table = dram("table", [TABLE, TW], F32)
        rows = dram("rows", [EP + 1, M], F32)
        peak_rows = dram("peak_rows", [EP + 1, D], F32)
        a_starts = dram("a_starts", [EP, 1], F32)
        a_table = dram("a_table", [TABLE, D], F32)
        b_table = dram("b_table", [TABLE, D], F32)
        row_starts = dram("row_starts", [EP, D], F32)

        src_i = sb("src_i", [P, W], I32)
        lo = sb("lo", [P, W], F32)
        blk = sb("blk", [P, W], F32)
        lead = sb("lead", [P, W], F32)
        cont = sb("cont", [P, W], F32)
        z = [sb(f"z{k}", [P, W], F32) for k in range(2)]
        digits = sb("digits", [P, W * DIGITS], BF16)
        x_sb = sb("x_sb", [P, NB, D], F32)
        h = sb("h", [P, NB, D], F32)
        count = sb("count", [P, NB], F32)
        start_i = sb("start_i", [P, NB], I32)
        end_i = sb("end_i", [P, NB], I32)
        has = sb("has", [P, NB], F32)
        dst0_i = sb("dst0_i", [P, 1], I32)
        strad = sb("strad", [P, 1], F32)
        through = sb("through", [P, 1], F32)
        first_end_i = sb("first_end_i", [P, 1], I32)
        iota = sb("iota", [P, P], F32)
        lane = sb("lane", [P, 1], F32)
        ident = sb("ident", [P, P], F32)
        identb = sb("identb", [P, P], BF16)
        below = sb("below", [P, P], F32)
        ones = sb("ones", [P, P], F32)
        zero = sb("zero", [P, 8 * D], F32)
        rel_aug = sb("rel_aug", [D, R + 1], F32)
        rel_t = sb("rel_t", [R + 1, D], F32)
        v = sb("v", [P, 2, R + 1], F32)
        bias = sb("bias", [P, 2], F32)

        with phase() as c:
            dst_i = sb("dst_i", [P, W], I32, c)
            tmp_i = sb("tmp_i", [P, W], I32, c)
            dlo = sb("dlo", [P, W], F32, c)
            dblk = sb("dblk", [P, W], F32, c)
            prev_i = sb("prev_i", [P, 1], I32, c)
            prev_f = sb("prev_f", [P, 1], F32, c)
            dst0_f = sb("dst0_f", [P, 1], F32, c)
            dstl_f = sb("dstl_f", [P, 1], F32, c)
            ew = sb("ew", [D, 2], F32, c)
            bias_in = sb("bias_in", [P, 6], F32, c)
            hot_lo = sb("hot_lo", [P, UNROLL, GT, P], BF16, c)
            hot_blk = sb("hot_blk", [P, UNROLL, GT, NB], BF16, c)
            start_f = sb("start_f", [P, NB], F32, c)
            end_f = sb("end_f", [P, NB], F32, c)
            total = sb("total", [P, NB], F32, c)
            tmp1 = sb("tmp1", [P, NB], F32, c)
            tmp2 = sb("tmp2", [P, NB], F32, c)
            neutral = sb("neutral", [1, M], F32, c)
            zeros = sb("zeros", [P, W], F32, c)
            goes_on = sb("goes_on", [P, W], F32, c)
            first_end = sb("first_end", [P, 1], F32, c)
            small = pb("small", [P, 512], F32, c)
            hist = pb("hist", [P, NB], F32, c)

            edges_in, small_in, made = sem("edges_in"), sem("small_in"), sem("made")
            chain, hot_ready, hot_used = sem("chain"), sem("hot_ready"), sem("hot_used")
            sums_ready, sums_done = sem("sums_ready"), sem("sums_done")
            proj_done, zeroed, filled = sem("proj_done"), sem("zeroed"), sem("filled")
            with nc.Block() as block:
                @block.sync
                def _(sp):
                    sp.dma_start(src_i[:, :], src).then_inc(edges_in, 16)
                    sp.dma_start(dst_i[:, :], dst).then_inc(edges_in, 16)
                    sp.dma_start(dst0_i[:, :], dst[:, 0:1]).then_inc(edges_in, 16)
                    sp.dma_start(prev_i[1:P, :], dst[0:P - 1, W - 1:W]).then_inc(edges_in, 16)
                    sp.dma_start(x_sb[:, :, :], x.rearrange("(b p) f -> p b f", p=P)).then_inc(small_in, 16)
                    sp.dma_start(rel_aug[:, 0:R], rel_w).then_inc(small_in, 16)
                    sp.dma_start(rel_aug[:, R:R + 1], bass_col(rel_b)).then_inc(small_in, 16)
                    sp.dma_start(ew[:, 0:1], c1_ew_w.rearrange("a d -> d a")).then_inc(small_in, 16)
                    sp.dma_start(ew[:, 1:2], c2_ew_w.rearrange("a d -> d a")).then_inc(small_in, 16)
                    for k, b in enumerate((c1_ai_b, c1_aj_b, c1_ew_b, c2_ai_b, c2_aj_b, c2_ew_b)):
                        sp.dma_start(bias_in[:, k:k + 1], b.partition_broadcast(P)).then_inc(small_in, 16)
                    sp.wait_ge(zeroed, 1)
                    sp.dma_start(a_starts.rearrange("(p t) f -> p (t f)", p=P), z[0][:, :]).then_inc(filled, 16)
                    sp.dma_start(table[NP:TABLE, :], zero[:, 0:TW]).then_inc(filled, 16)
                    sp.dma_start(a_table[NP:TABLE, :], zero[:, 0:D]).then_inc(filled, 16)
                    sp.dma_start(b_table[NP:TABLE, :], zero[:, 0:D]).then_inc(filled, 16)
                    sp.dma_start(rows[EP:EP + 1, :], zero[0:1, 0:M]).then_inc(filled, 16)
                    sp.dma_start(peak_rows[EP:EP + 1, :], neutral[0:1, 0:D]).then_inc(filled, 16)
                    wide = row_starts.rearrange("(p t) f -> p t f", p=P)
                    with sp.Fori(0, W // 8) as i:
                        sp.dma_start(wide[:, bass.ds(i * 8, 8), :],
                                     zero[:, :].rearrange("p (t f) -> p t f", f=D)).then_inc(filled, 16)
                    sp.wait_ge(filled, 16 * (6 + W // 8))

                @block.gpsimd
                def _(pool):
                    pool.iota(iota[:, :], [[1, P]], base=0, channel_multiplier=0,
                              allow_small_or_imprecise_dtypes=True).then_inc(made, 1)
                    pool.iota(lane[:, :], [[0, 1]], base=0, channel_multiplier=1,
                              allow_small_or_imprecise_dtypes=True).then_inc(made, 1)
                    pool.iota(first_end[:, :], [[0, 1]], base=0, channel_multiplier=W,
                              allow_small_or_imprecise_dtypes=True).then_inc(made, 1)
                    pool.memset(ones[:, :], 1.0).then_inc(made, 1)
                    pool.memset(neutral[:, :], -BIG).then_inc(made, 1)

                @block.vector
                def _(dve):
                    n = [0]

                    def then(ins):
                        ins.then_inc(chain, 1)
                        n[0] += 1
                        dve.wait_ge(chain, n[0])

                    dve.memset(prev_i[0:1, :], -1).then_inc(chain, 1)
                    n[0] += 1
                    then(dve.memset(zero[:, :], 0.0))
                    dve.wait_ge(made, 5)
                    dve.memset(z[0][:, :], 0.0).then_inc(zeroed, 1)
                    then(dve.tensor_scalar(ident[:, :], iota[:, :], lane[:, 0:1], None, ALU.is_equal))
                    then(dve.tensor_copy(identb[:, :], ident[:, :]))
                    then(dve.tensor_scalar(below[:, :], iota[:, :], lane[:, 0:1], None, ALU.is_gt))
                    dve.wait_ge(edges_in, 64)
                    dve.wait_ge(small_in, 16 * 11)
                    then(dve.tensor_scalar(tmp_i[:, :], dst_i[:, :], P - 1, None, ALU.bitwise_and))
                    then(dve.tensor_copy(dlo[:, :], tmp_i[:, :]))
                    then(dve.tensor_scalar(tmp_i[:, :], dst_i[:, :], 7, None, ALU.logical_shift_right))
                    then(dve.tensor_copy(dblk[:, :], tmp_i[:, :]))
                    then(dve.tensor_tensor(cont[:, 1:W], dst_i[:, 1:W], dst_i[:, 0:W - 1], ALU.is_equal))
                    then(dve.memset(cont[:, 0:1], 0.0))
                    then(dve.tensor_copy(prev_f[:, :], prev_i[:, :]))
                    then(dve.tensor_copy(dst0_f[:, :], dst_i[:, 0:1]))
                    then(dve.tensor_copy(dstl_f[:, :], dst_i[:, W - 1:W]))
                    then(dve.tensor_tensor(strad[:, :], prev_f[:, :], dst0_f[:, :], ALU.is_equal))
                    then(dve.tensor_tensor(through[:, :], dstl_f[:, :], dst0_f[:, :], ALU.is_equal))
                    then(dve.tensor_tensor(through[:, :], through[:, :], strad[:, :], ALU.mult))
                    then(dve.memset(zeros[:, :], 0.0))
                    then(dve.tensor_tensor_scan(goes_on[:, 1:W], cont[:, 1:W], zeros[:, 1:W], 1.0, ALU.mult, ALU.add))
                    then(dve.tensor_reduce(dst0_f[:, :], goes_on[:, 1:W], AX.X, ALU.add))
                    then(dve.tensor_tensor(first_end[:, :], first_end[:, :], dst0_f[:, :], ALU.add))
                    then(dve.tensor_copy(first_end_i[:, :], first_end[:, :]))
                    then(dve.tensor_scalar(tmp_i[:, :], src_i[:, :], P - 1, None, ALU.bitwise_and))
                    then(dve.tensor_copy(lo[:, :], tmp_i[:, :]))
                    then(dve.tensor_scalar(tmp_i[:, :], src_i[:, :], 7, None, ALU.logical_shift_right))
                    then(dve.tensor_copy(blk[:, :], tmp_i[:, :]))
                    then(dve.memset(digits[:, :], 0.0))
                    dig = digits[:, :].rearrange("p (t k) -> p t k", k=DIGITS)
                    then(dve.memset(dig[:, :, BITS], SIGN))
                    for k in range(BITS):
                        then(dve.tensor_scalar(tmp_i[:, :], src_i[:, :], 1 << k, None, ALU.bitwise_and))
                        then(dve.tensor_scalar(dig[:, :, k], tmp_i[:, :], 2.0 * SIGN / (1 << k), -SIGN,
                                               ALU.mult, ALU.add))
                    dve.wait_ge(proj_done, 2)
                    then(dve.tensor_copy(v[:, :, :], small[:, 0:2 * (R + 1)].rearrange("p (k r) -> p k r", k=2)))
                    then(dve.tensor_reduce(bias[:, :], bias_in[:, :].rearrange("p (k j) -> p k j", k=2), AX.X, ALU.add))
                    then(dve.tensor_tensor(bias[:, :], bias[:, :], v[:, :, R], ALU.add))
                    dve.wait_ge(proj_done, 2)
                    then(dve.tensor_copy(rel_t[:, :], small[0:R + 1, 128:128 + D]))

                    def onehots(g, u):
                        dve.wait_ge(hot_used, g + 1)
                        dve.tensor_tensor(hot_lo[:, u], mid(iota[:, :], [P, GT, P]),
                                          bcast(dlo[:, bass.ds(g * GT, GT)], [P, GT, P]), ALU.is_equal).then_inc(hot_ready, 1)
                        dve.tensor_tensor(hot_blk[:, u], mid(iota[:, 0:NB], [P, GT, NB]),
                                          bcast(dblk[:, bass.ds(g * GT, GT)], [P, GT, NB]), ALU.is_equal).then_inc(hot_ready, 1)

                    over_groups(dve, onehots)
                    dve.wait_ge(hot_used, UNROLL + NG)
                    dve.tensor_copy(count[:, :], hist[:, :]).then_inc(sums_ready, 1)
                    dve.wait_ge(sums_done, 1)
                    then(dve.tensor_copy(total[:, :], small[:, 256:256 + NB]))
                    then(dve.tensor_tensor_scan(tmp1[:, :], ones[:, 0:NB], total[:, :], 0.0, ALU.mult, ALU.add))
                    then(dve.tensor_tensor(tmp1[:, :], tmp1[:, :], total[:, :], ALU.subtract))
                    then(dve.tensor_tensor(start_f[:, :], tmp1[:, :], small[:, 320:320 + NB], ALU.add))
                    then(dve.tensor_tensor(end_f[:, :], start_f[:, :], count[:, :], ALU.add))
                    then(dve.tensor_scalar(end_f[:, :], end_f[:, :], -1.0, None, ALU.add))
                    then(dve.tensor_scalar(has[:, :], count[:, :], 0.0, None, ALU.is_gt))
                    then(dve.tensor_scalar(tmp2[:, :], end_f[:, :], float(EP), None, ALU.subtract))
                    then(dve.tensor_tensor(tmp2[:, :], tmp2[:, :], has[:, :], ALU.mult))
                    then(dve.tensor_scalar(end_i[:, :], tmp2[:, :], float(EP), None, ALU.add))
                    then(dve.tensor_tensor(tmp2[:, :], start_f[:, :], has[:, :], ALU.mult))
                    then(dve.tensor_scalar(tmp1[:, :], has[:, :], -float(SKIP), float(SKIP), ALU.mult, ALU.add))
                    then(dve.tensor_tensor(start_i[:, :], tmp1[:, :], tmp2[:, :], ALU.add))

                @block.tensor
                def _(pe):
                    pe.wait_ge(small_in, 16 * 11)
                    pe.wait_ge(chain, 5)
                    for k in range(2):
                        last = pe.matmul(small[:, k * (R + 1):(k + 1) * (R + 1)],
                                         ew[:, k:k + 1].to_broadcast([D, P]), rel_aug[:, :], start=True, stop=True)
                    last.then_inc(proj_done, 1)
                    pe.transpose(small[0:R + 1, 128:128 + D], rel_aug[:, :], ident[0:D, 0:D]).then_inc(proj_done, 1)
                    pe.sem_inc(hot_used, UNROLL)

                    def add_group(g, u, start=False, stop=False):
                        pe.wait_ge(hot_ready, g * 2 + 2)
                        for t in range(GT):
                            last = pe.matmul(hist[:, :], hot_lo[:, u, t], hot_blk[:, u, t],
                                             start=start and t == 0, stop=stop and t == GT - 1)
                        last.then_inc(hot_used, 1)

                    accumulate(pe, add_group)
                    pe.wait_ge(sums_ready, 1)
                    pe.matmul(small[:, 256:256 + NB], ones[:, :], count[:, :], start=True, stop=True)
                    pe.matmul(small[:, 320:320 + NB], below[:, :], count[:, :], start=True, stop=True).then_inc(sums_done, 1)


        def chained(eng, semaphore):
            n = [0]

            def then(ins):
                ins.then_inc(semaphore, 1)
                n[0] += 1
                eng.wait_ge(semaphore, n[0])

            return then

        def norm_relu(tag):
            with phase() as c:
                mean = sb(f"mean{tag}", [P, NB], F32, c)
                var = sb(f"var{tag}", [P, NB], F32, c)
                sq = sb(f"sq{tag}", [P, NB, D], F32, c)
                chain, var_ready, std_ready = sem(f"n_chain{tag}"), sem(f"n_var{tag}"), sem(f"n_std{tag}")
                with nc.Block() as block:
                    @block.vector
                    def _(dve):
                        then = chained(dve, chain)
                        then(dve.tensor_reduce(mean[:, :], x_sb[:, :, :], AX.X, ALU.add))
                        then(dve.tensor_scalar(mean[:, :], mean[:, :], 1.0 / D, None, ALU.mult))
                        then(dve.tensor_tensor(h[:, :, :], x_sb[:, :, :], bcast(mean[:, :], [P, NB, D]), ALU.subtract))
                        then(dve.tensor_tensor(sq[:, :, :], h[:, :, :], h[:, :, :], ALU.mult))
                        then(dve.tensor_reduce(var[:, :], sq[:, :, :], AX.X, ALU.add))
                        dve.tensor_scalar(var[:, :], var[:, :], 1.0 / D, EPS, ALU.mult, ALU.add).then_inc(var_ready, 1)
                        dve.wait_ge(std_ready, 1)
                        then(dve.reciprocal(var[:, :], var[:, :]))
                        then(dve.tensor_tensor(h[:, :, :], h[:, :, :], bcast(var[:, :], [P, NB, D]), ALU.mult))
                        then(dve.tensor_scalar(h[:, :, :], h[:, :, :], 0.0, None, ALU.max))

                    @block.scalar
                    def _(act):
                        act.wait_ge(var_ready, 1)
                        act.activation(var[:, :], var[:, :], ACT.Sqrt).then_inc(std_ready, 1)

        def project(tag, w, b, ai_w, aj_w, xn):
            with phase() as c:
                wb = sb(f"wb{tag}", [D, D + 1], F32, c)
                aij = sb(f"aij{tag}", [D, 2], F32, c)
                waug = sb(f"waug{tag}", [D + 1, D + 2], F32, c)
                ht = sb(f"ht{tag}", [D + 1, 7 * P], F32, c)
                wp = pb(f"wp{tag}", [P, 512], F32, c)
                hp = pb(f"hp{tag}", [P, 1024], F32, c)
                xp = pb(f"xp{tag}", [P, 512], F32, c)
                w_in, w_ready, w_copied = sem(f"p_win{tag}"), sem(f"p_w{tag}"), sem(f"p_wc{tag}")
                turned, ht_ready, x_ready, x_copied, stored = (sem(f"p_{n}{tag}") for n in ("t", "h", "x", "xc", "st"))
                with nc.Block() as block:
                    @block.sync
                    def _(sp):
                        sp.dma_start(wb[:, 0:D], w).then_inc(w_in, 16)
                        sp.dma_start(wb[:, D:D + 1], bass_col(b)).then_inc(w_in, 16)
                        sp.dma_start(aij[:, 0:1], ai_w.rearrange("a d -> d a")).then_inc(w_in, 16)
                        sp.dma_start(aij[:, 1:2], aj_w.rearrange("a d -> d a")).then_inc(w_in, 16)
                        sp.wait_ge(x_copied, NB // 7)
                        sp.dma_start(table[0:NP, :].rearrange("(b p) f -> p b f", p=P), xn[:, :, :]).then_inc(stored, 16)
                        sp.wait_ge(stored, 16)

                    @block.tensor
                    def _(pe):
                        pe.wait_ge(w_in, 64)
                        pe.transpose(wp[0:D + 1, 0:D], wb[:, :], ident[0:D, 0:D])
                        pe.matmul(wp[0:D + 1, D:D + 2], wb[:, :], aij[:, :], start=True, stop=True).then_inc(w_ready, 1)
                        for j in range(NB // 7):
                            if j:
                                pe.wait_ge(ht_ready, j)
                            for b7 in range(7):
                                last = pe.transpose(hp[0:D, b7 * P:(b7 + 1) * P], h[:, 7 * j + b7, :], ident[:, :])
                            last.then_inc(turned, 1)
                            pe.wait_ge(ht_ready, j + 1)
                            if j == 0:
                                pe.wait_ge(w_copied, 2)
                            else:
                                pe.wait_ge(x_copied, j)
                            for b7 in range(7):
                                last = pe.matmul(xp[:, b7 * (D + 2):(b7 + 1) * (D + 2)], ht[:, b7 * P:(b7 + 1) * P],
                                                 waug[:, :], start=True, stop=True)
                            last.then_inc(x_ready, 1)

                    @block.scalar
                    def _(act):
                        for j in range(NB // 7):
                            act.wait_ge(turned, j + 1)
                            if j:
                                act.wait_ge(x_ready, j)
                            act.activation(ht[0:D, :], hp[0:D, 0:7 * P], ACT.Copy).then_inc(ht_ready, 1)

                    @block.vector
                    def _(dve):
                        dve.memset(ht[D:D + 1, :], 1.0).then_inc(w_copied, 1)
                        dve.memset(xn[:, :, D + 2:D + 3], 0.0)
                        dve.wait_ge(w_ready, 1)
                        dve.tensor_copy(waug[:, :], wp[0:D + 1, 0:D + 2]).then_inc(w_copied, 1)
                        for j in range(NB // 7):
                            dve.wait_ge(x_ready, j + 1)
                            dve.tensor_copy(xn[:, 7 * j:7 * j + 7, 0:D + 2],
                                            xp[:, 0:7 * (D + 2)].rearrange("p (b f) -> p b f", f=D + 2)).then_inc(x_copied, 1)

        def expand(tag, xn, zk):
            with phase() as c:
                at_start = sb(f"at_start{tag}", [P, W], F32, c)
                first = sb(f"first{tag}", [P, TW], F32, c)
                scattered, firsts = lasting(f"e_sc{tag}"), lasting(f"e_fi{tag}")
                loaded, chain = sem(f"e_lo{tag}"), sem(f"e_ch{tag}")
                with nc.Block() as block:
                    @block.gpsimd
                    def _(pool):
                        for b in range(NB):
                            pool.indirect_dma_start(a_starts, bass.IndirectOffsetOnAxis(ap=start_i[:, b:b + 1], axis=0),
                                                    xn[:, b, D:D + 1], None, bounds_check=EP - 1,
                                                    oob_is_err=False).then_inc(scattered, 16)
                        pool.indirect_dma_start(first[:, :], None, table,
                                                bass.IndirectOffsetOnAxis(ap=dst0_i[:, 0:1], axis=0)).then_inc(firsts, 16)

                    @block.sync
                    def _(sp):
                        sp.wait_ge(scattered, 16 * NB)
                        sp.dma_start(at_start[:, :], a_starts.rearrange("(p t) f -> p (t f)", p=P)).then_inc(loaded, 16)

                    @block.vector
                    def _(dve):
                        then = chained(dve, chain)
                        dve.wait_ge(loaded, 16)
                        dve.wait_ge(firsts, 16)
                        then(dve.tensor_copy(at_start[:, 0:1], first[:, D:D + 1]))
                        then(dve.tensor_tensor_scan(at_start[:, :], cont[:, :], at_start[:, :], 0.0, ALU.mult, ALU.add))
                        then(dve.tensor_tensor(zk[:, :], zk[:, :], at_start[:, :], ALU.add))

        def split(dve, then, value, rest, parts):
            then(dve.tensor_copy(parts[..., 0], value))
            then(dve.tensor_tensor(rest, value, parts[..., 0], ALU.subtract))
            then(dve.tensor_copy(parts[..., 1], rest))
            then(dve.tensor_tensor(parts[..., 2], rest, parts[..., 1], ALU.subtract))

        def onehot(dve, out, values, g, width):
            return dve.tensor_tensor(out, mid(iota[:, 0:width], [P, GT, width]),
                                     bcast(values[:, bass.ds(g * GT, GT)], [P, GT, width]), ALU.is_equal)

        def tile_maxima(tag, parts, dest, load=None, beside=None):
            with phase() as c:
                slot = sb(f"slot{tag}", [P, UNROLL, HALF, 2, TALL], BF16, c)
                right = sb(f"right{tag}", [P, UNROLL, HALF, P], BF16, c)
                left = sb(f"left{tag}", [P, UNROLL, HALF, P], BF16, c)
                factor = sb(f"factor{tag}", [P, 1], F32, c)
                column = sb(f"column{tag}", [P, 2, TALL], F32, c)
                pick = sb(f"pick{tag}", [P, P], BF16, c)
                picked = sb(f"mpick{tag}", [P, 2, TALL], F32, c)
                bp = [pb(f"bp{tag}{j}", [P, 8 * P], BF16, c) for j in range(2)]
                fp = pb(f"mfp{tag}", [P, 4 * P], F32, c)
                mp = pb(f"mp{tag}", [P, 2, 2, 4, P], F32, c)
                ready, cleared, slot_ready, turned, sides, pairs, topped, begun, made = (
                    sem(f"m_{n}{tag}") for n in ("re", "cl", "sl", "tu", "si", "pa", "to", "be", "ma"))
                dig = digits[:, :].rearrange("p (t k) -> p t k", k=DIGITS)
                with nc.Block() as block:
                    @block.gpsimd
                    def _(pool):
                        static = parts.shape[1] == 1
                        pool.memset(slot[:, :, :, :, :], 0.0).then_inc(cleared, 1)
                        pool.wait_ge(cleared, 1)
                        if static:
                            pool.tensor_copy(slot[:, :, :, :, VALUE:VALUE + 3].rearrange("p u a h k -> p (u a h) k"),
                                             parts[:, 0:1, :].to_broadcast([P, UNROLL * GT, 3])).then_inc(cleared, 1)
                            pool.wait_ge(cleared, 2)
                        pool.sem_inc(turned, UNROLL)

                        def fill(g, u):
                            pool.wait_ge(turned, g + 1)
                            pool.sem_inc(begun, 1)
                            if not static:
                                pool.tensor_copy(slot[:, u, :, :, VALUE:VALUE + 3].rearrange("p a h k -> p h a k"),
                                                 parts[:, bass.ds(g * GT, GT), :].rearrange("p (h a) k -> p h a k", h=2))
                            pool.tensor_copy(slot[:, u, :, :, 0:VALUE].rearrange("p a h k -> p h a k"),
                                             dig[:, bass.ds(g * GT, GT), 0:VALUE].rearrange("p (h a) k -> p h a k", h=2)).then_inc(slot_ready, 1)

                        over_groups(pool, fill)

                    @block.tensor
                    def _(pe):
                        pe.wait_ge(ready, 2)
                        pe.transpose(fp[:, 0:P], column[:, :, :].rearrange("p t k -> p (t k)"), ident[:, :])
                        pe.transpose(fp[:, P:2 * P], picked[:, :, :].rearrange("p t k -> p (t k)"), ident[:, :]).then_inc(ready, 1)
                        pe.wait_ge(ready, 5)

                        def turn(g, u):
                            pe.wait_ge(sides, g + 1)
                            pe.wait_ge(slot_ready, g + 1)
                            pe.sem_inc(begun, 1)
                            for a in range(HALF):
                                last = pe.transpose(bp[u % 2][:, a * P:(a + 1) * P], slot[:, u, a].rearrange("p h k -> p (h k)"),
                                                    identb[:, :])
                            last.then_inc(turned, 1)

                        def pair(g, u):
                            pe.wait_ge(sides, g + 3)
                            pe.wait_ge(topped, g + 1)
                            for t in range(GT):
                                own = slice(t // HALF * TALL, t // HALF * TALL + TALL)
                                pe.matmul(mp[:, u % 2, t // HALF, t % HALF], left[own, u, t % HALF], right[own, u, t % HALF],
                                          start=True, stop=False)
                                last = pe.matmul(mp[:, u % 2, t // HALF, t % HALF], pick[own, :], right[own, u, t % HALF],
                                                 start=False, stop=True)
                            last.then_inc(pairs, 1)

                        over_groups_skewed(pe, turn, pair)

                    @block.scalar
                    def _(act):
                        act.sem_inc(sides, 2)
                        act.sem_inc(pairs, UNROLL)
                        act.wait_ge(ready, 5)

                        def copy_rows(g, u):
                            act.wait_ge(turned, g + (UNROLL + 1))
                            act.wait_ge(pairs, g + 1)
                            act.activation(right[:, u].rearrange("p a j -> p (a j)"), bp[u % 2][:, 0:HALF * P], ACT.Copy)
                            act.activation(left[:, u].rearrange("p a j -> p (a j)"), bp[u % 2][:, 0:HALF * P], ACT.Identity, scale=factor[:, 0:1]).then_inc(sides, 1)

                        over_groups(act, copy_rows)

                    @block.vector
                    def _(dve):
                        dve.sem_inc(topped, 2)
                        then = chained(dve, made)
                        then(dve.memset(column[:, :, :], 0.0))
                        then(dve.memset(column[:, :, 0:BITS], 1.0))
                        dve.memset(column[:, :, BITS:BITS + 1], -float(BITS)).then_inc(ready, 1)
                        then(dve.memset(picked[:, :, :], 0.0))
                        dve.memset(picked[:, :, VALUE:VALUE + 3], 1.0).then_inc(ready, 1)
                        dve.wait_ge(ready, 3)
                        dve.tensor_copy(factor[:, :], fp[:, 0:1]).then_inc(ready, 1)
                        dve.tensor_copy(pick[:, :], fp[:, P:2 * P]).then_inc(ready, 1)

                        def maxima(g, u):
                            dve.wait_ge(pairs, g + (UNROLL + 1))
                            dve.tensor_reduce(dest[:, bass.ds(g * GT, GT)].rearrange("p (h a) -> p h a", h=2), mp[:, u % 2, :, 0:HALF], AX.X, ALU.max).then_inc(topped, 1)

                        if beside is None:
                            over_groups(dve, maxima)
                        else:
                            beside(dve, maxima)

                    if load is not None:
                        @block.sync
                        def _(sp):
                            load(sp)

        def leaders():
            with phase() as c:
                own = sb("own", [P, 1, 3], BF16, c)
                begin = sem("l_be")
                with nc.Block() as block:
                    @block.vector
                    def _(dve):
                        dve.memset(own[:, :, :], 0.0).then_inc(begin, 1)
                        dve.wait_ge(begin, 1)
                        dve.tensor_copy(own[:, 0, 0:1], lane[:, :])

                att = sb("att", [P, UNROLL, GT, R], F32, c)
                prod = sb("prod", [P, 2, GT, R], F32, c)
                att_in = [sem(f"att_in{u}") for u in range(UNROLL)]
                prod_ready, terms = sem("prod_ready"), sem("terms")

                def load(sp):
                    with sp.Fori(0, NG // UNROLL) as i:
                        for u in range(UNROLL):
                            sp.wait_ge(prod_ready, i * UNROLL + (u + 1))
                            sp.dma_start(att[:, u], attr[:, bass.ds((i * UNROLL + u) * GT, GT), :]).then_inc(att_in[u], 16)

                def edge_terms(dve, maxima):
                    dve.sem_inc(prod_ready, UNROLL)
                    dve.sem_inc(terms, 2)
                    with dve.Fori(0, NG // UNROLL) as i:
                        for u in range(UNROLL):
                            g = i * UNROLL + u
                            dve.wait_ge(att_in[u], i * 16 + 16)
                            dve.wait_ge(terms, g + 1)
                            dve.tensor_tensor(prod[:, u % 2], att[:, u], mid(v[:, 0, 0:R], [P, GT, R]), ALU.mult)\
                               .then_inc(prod_ready, 1)
                            maxima(g, u)
                            dve.wait_ge(prod_ready, g + (UNROLL + 1))
                            dve.tensor_reduce(z[0][:, bass.ds(g * GT, GT)], prod[:, u % 2], AX.X, ALU.add).then_inc(terms, 1)
                    dve.wait_ge(terms, NG + 2)
                    dve.tensor_scalar(z[0][:, :], z[0][:, :], bias[:, 0:1], None, ALU.add)

                tile_maxima("l", own[:, :, :], lead, load, edge_terms)
                chain = sem("l_ch")
                with nc.Block() as block:
                    @block.vector
                    def _(dve):
                        then = chained(dve, chain)
                        then(dve.tensor_scalar(lead[:, :], lead[:, :], lane[:, 0:1], None, ALU.is_equal))
                        then(dve.scalar_tensor_tensor(lead[:, :], blk[:, :], 1.0, lead[:, :], ALU.add, ALU.mult))
                        then(dve.tensor_scalar(lead[:, :], lead[:, :], -1.0, None, ALU.add))

        def value_columns(pool, hot_ready, begun, hot_blk, parts, hot_val, val_ready):
            def columns(g, u):
                pool.wait_ge(hot_ready, g + 1)
                pool.sem_inc(begun, 1)
                pool.tensor_tensor(hot_val[:, u], hot_blk[:, u].unsqueeze(2).to_broadcast([P, GT, 3, NB]),
                                   parts[:, bass.ds(g * GT, GT), :].unsqueeze(3).to_broadcast([P, GT, 3, NB]),
                                   ALU.mult).then_inc(val_ready, 1)

            over_groups(pool, columns)

        def peaks(tag, parts, peak):
            with phase() as c:
                hot_lo = sb(f"g_lo{tag}", [P, UNROLL, GT, P], BF16, c)
                hot_blk = sb(f"g_blk{tag}", [P, UNROLL, GT, NB], BF16, c)
                hot_big = sb(f"g_big{tag}", [P, UNROLL, GT, NB], BF16, c)
                hot_val = sb(f"g_val{tag}", [P, UNROLL, GT, 3, NB], BF16, c)
                best = sb(f"best{tag}", [P, NB], F32, c)
                minus_big = sb(f"mb{tag}", [1, GT * NB], BF16, c)
                one = sb(f"one{tag}", [1, P], BF16, c)
                gp = [pb(f"gp{tag}{j}", [P, GT, NB], F32, c) for j in range(2)]
                ready, hot_ready, lo_ready, begun, big_ready, val_ready, grid, best_ready, peaked = (
                    sem(f"g_{n}{tag}") for n in ("re", "ho", "lo", "bg", "bi", "va", "gr", "be", "pe"))
                with nc.Block() as block:
                    @block.vector
                    def _(dve):
                        dve.memset(minus_big[:, :], -BIG).then_inc(ready, 1)
                        dve.memset(one[:, :], 1.0).then_inc(ready, 1)
                        dve.memset(peak[:, :], -BIG).then_inc(ready, 1)
                        dve.wait_ge(ready, 3)
                        dve.sem_inc(best_ready, 2)
                        dve.sem_inc(grid, UNROLL)
                        dve.sem_inc(peaked, 1)

                        def onehot_blk(g, u):
                            dve.wait_ge(grid, g + 1)
                            onehot(dve, hot_blk[:, u], lead, g, NB).then_inc(hot_ready, 1)

                        def onehot_lo(g, u):
                            onehot(dve, hot_lo[:, u], lo, g, P).then_inc(lo_ready, 1)

                        def maxima(g, u):
                            dve.wait_ge(grid, g + (UNROLL + 1))
                            dve.wait_ge(peaked, g + 1)
                            dve.tensor_reduce(best[:, :], gp[u % 2][:, :, :].rearrange("p t b -> p b t"), AX.X,
                                              ALU.max).then_inc(best_ready, 1)

                        def keep(g):
                            dve.wait_ge(best_ready, g + 3)
                            dve.tensor_tensor(peak[:, :], peak[:, :], best[:, :], ALU.max).then_inc(peaked, 1)

                        for g in range(2):
                            onehot_blk(g, g)
                            onehot_lo(g, g)
                        with dve.Fori(0, NG // UNROLL - 1) as i:
                            for u in range(UNROLL):
                                onehot_blk(i * UNROLL + (u + 2), (u + 2) % UNROLL)
                                maxima(i * UNROLL + u, u)
                                onehot_lo(i * UNROLL + (u + 2), (u + 2) % UNROLL)
                                keep(i * UNROLL + u)
                        for g in range(NG - UNROLL, NG):
                            if g + 2 < NG:
                                onehot_blk(g + 2, (g + 2) % UNROLL)
                                onehot_lo(g + 2, (g + 2) % UNROLL)
                            maxima(g, g % UNROLL)
                            keep(g)

                    @block.gpsimd
                    def _(pool):
                        value_columns(pool, hot_ready, begun, hot_blk, parts, hot_val, val_ready)

                    @block.scalar
                    def _(act):
                        def scale_big(g, u):
                            act.wait_ge(hot_ready, g + 1)
                            act.activation(hot_big[:, u], hot_blk[:, u], ACT.Copy, scale=BIG).then_inc(big_ready, 1)

                        over_groups(act, scale_big)

                    @block.tensor
                    def _(pe):
                        pe.wait_ge(ready, 3)

                        def scatter(g, u):
                            pe.wait_ge(big_ready, g + 1)
                            pe.wait_ge(lo_ready, g + 1)
                            pe.wait_ge(val_ready, g + 1)
                            pe.wait_ge(best_ready, g + 1)
                            pe.matmul(gp[u % 2][:, :, :].rearrange("p t b -> p (t b)"), one[:, :], minus_big[:, :],
                                      start=True, stop=False)
                            for t in range(GT):
                                pe.matmul(gp[u % 2][:, t], hot_lo[:, u, t], hot_big[:, u, t], start=False, stop=False)
                                for k in range(3):
                                    last = pe.matmul(gp[u % 2][:, t], hot_lo[:, u, t], hot_val[:, u, t, k], start=False,
                                                     stop=t == GT - 1 and k == 2)
                            last.then_inc(grid, 1)

                        over_groups(pe, scatter)

        def lookups(tag, pair, found):
            with phase() as c:
                pair_parts = sb(f"pp{tag}", [P, 3, 2 * NB], BF16, c)
                rest = sb(f"pr{tag}", [P, 2 * NB], F32, c)
                slot = sb(f"x_slot{tag}", [P, UNROLL, GT * DIGITS], BF16, c)
                line = sb(f"x_line{tag}", [GT * DIGITS, UNROLL, P], BF16, c)
                hot_t = sb(f"x_t{tag}", [P, UNROLL, GT, P], BF16, c)
                hot_blk = sb(f"x_blk{tag}", [P, UNROLL, GT, NB], BF16, c)
                picked = sb(f"picked{tag}", [P, UNROLL, GT, 2, NB], F32, c)
                lane_digits = sb(f"x_ld{tag}", [GT * DIGITS, GT, P], BF16, c)
                lane_i = sb(f"x_li{tag}", [P, 1], I32, c)
                bit_i = sb(f"x_bi{tag}", [P, 1], I32, c)
                digit_cols = sb(f"x_dc{tag}", [P, GT, GT, DIGITS], BF16, c)
                minus = sb(f"x_mi{tag}", [P, 1], F32, c)
                tp = [pb(f"tp{tag}{j}", [GT * DIGITS, 8 * P], BF16, c) for j in range(2)]
                ep = [pb(f"ep{tag}{j}", [P, GT * P], F32, c) for j in range(2)]
                fp = [pb(f"fp{tag}{j}", [P, GT, 2, NB], F32, c) for j in range(FB)]
                lp = pb(f"lp{tag}", [GT * DIGITS, 8 * P], BF16, c)
                chain, lanes, hot_ready, turned, lined, agreed, t_ready, found_ready, picked_ready, summed, slot_ready, begun = (
                    sem(f"x_{n}{tag}") for n in ("ch", "la", "ho", "tu", "li", "ag", "t", "fo", "pi", "su", "sl", "bg"))
                with nc.Block() as block:
                    @block.vector
                    def _(dve):
                        then = chained(dve, chain)
                        then(dve.memset(minus[:, :], 1.0 - LOW))
                        then(dve.tensor_copy(lane_i[:, :], lane[:, :]))
                        then(dve.memset(digit_cols[:, :, :, :], 0.0))
                        for k in range(LOW):
                            then(dve.tensor_scalar(bit_i[:, :], lane_i[:, :], 1 << k, None, ALU.bitwise_and))
                            for t in range(GT):
                                then(dve.tensor_scalar(digit_cols[:, t, t, k:k + 1], bit_i[:, :], 2.0 * SIGN / (1 << k), -SIGN,
                                                       ALU.mult, ALU.add))
                        split(dve, then, pair[:, :, :].rearrange("p k b -> p (k b)"), rest[:, :],
                              pair_parts[:, :, :].rearrange("p k n -> p n k"))
                        dve.wait_ge(lanes, 1)
                        dve.tensor_copy(lane_digits[:, :, :].rearrange("p t j -> p (t j)"), lp[:, 0:GT * P]).then_inc(lanes, 1)

                    @block.tensor
                    def _(pe):
                        pe.wait_ge(chain, 3 + (1 + GT) * LOW)
                        for t in range(GT):
                            last = pe.transpose(lp[:, t * P:(t + 1) * P], digit_cols[:, t].rearrange("p a k -> p (a k)"), identb[:, :])
                        last.then_inc(lanes, 1)

                with nc.Block() as block:
                    @block.vector
                    def _(dve):
                        dve.sem_inc(summed, UNROLL)
                        dve.sem_inc(picked_ready, FB)

                        def onehots(g, u):
                            if not isinstance(g, int) or g >= UNROLL:
                                dve.wait_ge(picked_ready, g + (FB + 1 - UNROLL))
                            onehot(dve, hot_blk[:, u], blk, g, NB).then_inc(hot_ready, 1)

                        def select(g, u):
                            dve.wait_ge(found_ready, g + (UNROLL + 1))
                            dve.wait_ge(hot_ready, g + 1)
                            dve.wait_ge(summed, g + 1)
                            dve.tensor_tensor(picked[:, u], fp[u % FB][:, :, :, :],
                                              hot_blk[:, u].unsqueeze(2).to_broadcast([P, GT, 2, NB]), ALU.mult).then_inc(picked_ready, 1)

                        def total(g, u):
                            dve.wait_ge(picked_ready, g + (FB + 1))
                            dve.tensor_reduce(found[:, bass.ds(g * GT, GT), :], picked[:, u], AX.X, ALU.add).then_inc(summed, 1)

                        for g in range(3):
                            onehots(g, g)
                        select(0, 0)
                        with dve.Fori(0, NG // UNROLL - 1) as i:
                            for u in range(UNROLL):
                                onehots(i * UNROLL + (u + 3), (u + 3) % UNROLL)
                                select(i * UNROLL + (u + 1), (u + 1) % UNROLL)
                                total(i * UNROLL + u, u)
                        for g in range(NG - UNROLL, NG):
                            if g + 3 < NG:
                                onehots(g + 3, (g + 3) % UNROLL)
                            if g + 1 < NG:
                                select(g + 1, (g + 1) % UNROLL)
                            total(g, g % UNROLL)

                    @block.gpsimd
                    def _(pool):
                        pool.sem_inc(turned, UNROLL)

                        def fill(g, u):
                            pool.wait_ge(turned, g + 1)
                            pool.sem_inc(begun, 1)
                            pool.tensor_copy(slot[:, u], digits[:, bass.ds(g * (GT * DIGITS), GT * DIGITS)]).then_inc(slot_ready, 1)

                        over_groups(pool, fill)

                    @block.tensor
                    def _(pe):
                        def turn(g, u):
                            pe.wait_ge(lined, g + 1)
                            pe.wait_ge(slot_ready, g + 1)
                            pe.sem_inc(begun, 1)
                            pe.transpose(tp[u % 2][:, 0:P], slot[:, u], identb[:, :]).then_inc(turned, 1)

                        def agree(g, u):
                            pe.wait_ge(lined, g + 3)
                            pe.wait_ge(t_ready, g + 1)
                            for t in range(GT):
                                last = pe.matmul(ep[u % 2][:, t * P:(t + 1) * P], lane_digits[:, t], line[:, u], start=True, stop=True)
                            last.then_inc(agreed, 1)

                        def find(g, u):
                            pe.wait_ge(t_ready, g + 3)
                            pe.wait_ge(picked_ready, g + 1)
                            for t in range(GT):
                                for k in range(3):
                                    last = pe.matmul(fp[u % FB][:, t, :, :].rearrange("p k b -> p (k b)"), hot_t[:, u, t],
                                                     pair_parts[:, k], start=k == 0, stop=k == 2)
                            last.then_inc(found_ready, 1)

                        turn(0, 0)
                        turn(1, 1)
                        agree(0, 0)
                        with pe.Fori(0, NG // UNROLL - 1) as i:
                            for u in range(UNROLL):
                                turn(i * UNROLL + (u + 2), (u + 2) % UNROLL)
                                agree(i * UNROLL + (u + 1), (u + 1) % UNROLL)
                                find(i * UNROLL + u, u)
                        for g in range(NG - UNROLL, NG):
                            if g + 2 < NG:
                                turn(g + 2, (g + 2) % UNROLL)
                            if g + 1 < NG:
                                agree(g + 1, (g + 1) % UNROLL)
                            find(g, g % UNROLL)

                    @block.scalar
                    def _(act):
                        act.sem_inc(lined, 2)
                        act.sem_inc(t_ready, 2)
                        act.sem_inc(found_ready, UNROLL)

                        def copy_line(g, u):
                            act.wait_ge(turned, g + (UNROLL + 1))
                            act.activation(line[:, u], tp[u % 2][:, 0:P], ACT.Copy).then_inc(lined, 1)

                        def equal(g, u):
                            act.wait_ge(agreed, g + 1)
                            act.wait_ge(found_ready, g + 1)
                            act.activation(hot_t[:, u].rearrange("p t j -> p (t j)"), ep[u % 2][:, :], ACT.Relu,
                                           bias=minus[:, :], scale=1.0 / BIG).then_inc(t_ready, 1)

                        over_groups_skewed(act, copy_line, equal)

        def sums_by_src(tag, parts, total):
            with phase() as c:
                hot_lo = sb(f"u_lo{tag}", [P, UNROLL, GT, P], BF16, c)
                hot_blk = sb(f"u_blk{tag}", [P, UNROLL, GT, NB], BF16, c)
                hot_val = sb(f"u_val{tag}", [P, UNROLL, GT, 3, NB], BF16, c)
                sums = pb(f"sums{tag}", [P, NB], F32, c)
                hot_ready, lo_ready, begun, val_ready, added = (sem(f"u_{n}{tag}") for n in ("ho", "lo", "bg", "va", "ad"))
                with nc.Block() as block:
                    @block.vector
                    def _(dve):
                        def weighed(g, u):
                            dve.wait_ge(added, g + 1)
                            onehot(dve, hot_blk[:, u], blk, g, NB).then_inc(hot_ready, 1)
                            onehot(dve, hot_lo[:, u], lo, g, P).then_inc(lo_ready, 1)

                        over_groups(dve, weighed)
                        dve.wait_ge(added, NG + UNROLL)
                        dve.tensor_copy(total, sums[:, :])

                    @block.gpsimd
                    def _(pool):
                        value_columns(pool, hot_ready, begun, hot_blk, parts, hot_val, val_ready)

                    @block.tensor
                    def _(pe):
                        pe.sem_inc(added, UNROLL)

                        def add(g, u, start=False, stop=False):
                            pe.wait_ge(lo_ready, g + 1)
                            pe.wait_ge(val_ready, g + 1)
                            for t in range(GT):
                                for k in range(3):
                                    last = pe.matmul(sums[:, :], hot_lo[:, u, t], hot_val[:, u, t, k],
                                                     start=start and t == 0 and k == 0, stop=stop and t == GT - 1 and k == 2)
                            last.then_inc(added, 1)

                        accumulate(pe, add)

        def softmax_terms(tag, zk, xn):
            with phase() as c:
                parts = sb(f"parts{tag}", [P, W, 3], BF16, c)
                top = sb(f"top{tag}", [P, W], F32, c)
                peak = sb(f"peak{tag}", [P, NB], F32, c)
                pair = sb(f"pair{tag}", [P, 2, NB], F32, c)
                tmp = sb(f"a_tmp{tag}", [P, NB], F32, c)
                found = sb(f"found{tag}", [P, W, 2], F32, c)
                chain, chain2, exped, chain3, chain4, inverted, stored = (
                    sem(f"a_{n}{tag}") for n in ("c1", "c2", "ex", "c3", "c4", "in", "st"))
                with nc.Block() as block:
                    @block.vector
                    def _(dve):
                        split(dve, chained(dve, chain), zk[:, :], top[:, :], parts[:, :, :])
                tile_maxima(tag, parts[:, :, :], top)
                with nc.Block() as block:
                    @block.vector
                    def _(dve):
                        split(dve, chained(dve, chain2), top[:, :], found[:, :, 0], parts[:, :, :])
                peaks(tag, parts, peak)
                with nc.Block() as block:
                    @block.vector
                    def _(dve):
                        then = chained(dve, chain3)
                        then(dve.tensor_copy(pair[:, 0], xn[:, :, D + 1]))
                        then(dve.tensor_tensor(tmp[:, :], xn[:, :, D + 1], peak[:, :], ALU.add))
                        then(dve.scalar_tensor_tensor(pair[:, 1], tmp[:, :], 0.01, tmp[:, :], ALU.mult, ALU.max))
                lookups(tag, pair, found)
                with nc.Block() as block:
                    @block.vector
                    def _(dve):
                        then = chained(dve, chain4)
                        then(dve.tensor_tensor(zk[:, :], zk[:, :], found[:, :, 0], ALU.add))
                        then(dve.scalar_tensor_tensor(zk[:, :], zk[:, :], 0.01, zk[:, :], ALU.mult, ALU.max))
                        then(dve.tensor_tensor(zk[:, :], zk[:, :], found[:, :, 1], ALU.subtract))
                        dve.wait_ge(exped, 1)
                        split(dve, then, zk[:, :], top[:, :], parts[:, :, :])

                    @block.scalar
                    def _(act):
                        act.wait_ge(chain4, 3)
                        act.activation(zk[:, :], zk[:, :], ACT.Exp).then_inc(exped, 1)
                sums_by_src(tag, parts, tmp[:, :])
                with nc.Block() as block:
                    @block.vector
                    def _(dve):
                        dve.tensor_scalar(tmp[:, :], tmp[:, :], 1e-16, None, ALU.add).then_inc(inverted, 1)
                        dve.wait_ge(inverted, 1)
                        dve.reciprocal(xn[:, :, D + 2], tmp[:, :]).then_inc(inverted, 1)

                    @block.sync
                    def _(sp):
                        sp.wait_ge(inverted, 2)
                        sp.dma_start(table[0:NP, :].rearrange("(b p) f -> p b f", p=P), xn[:, :, :]).then_inc(stored, 16)
                        sp.wait_ge(stored, 16)

        def chunk_carries(tag, last, width, peak, dest):
            with phase() as c:
                seg = sb(f"seg{tag}", [width, 3, P], F32, c)
                run = sb(f"run{tag}", [width, P], F32, c)
                carry = sb(f"carry{tag}", [width, P], F32, c)
                pen = sb(f"pen{tag}", [width, P], F32, c)
                ends = sb(f"ends{tag}", [P, width], F32, c)
                fetched = lasting(f"k_fe{tag}")
                sp_full = pb(f"segp{tag}", [P, 512], F32, c)
                sp_ = sp_full[0:width, :]
                turned, chain, carried = (sem(f"k_{n}{tag}") for n in ("tu", "ch", "ca"))
                chain_steps = 7 if peak else 4
                with nc.Block() as block:
                    @block.tensor
                    def _(pe):
                        for k, m in enumerate((last, through[:, 0:1].to_broadcast([P, width]),
                                               strad[:, 0:1].to_broadcast([P, width]))):
                            ins = pe.transpose(sp_[:, k * P:(k + 1) * P], m, ident[:, :])
                        ins.then_inc(turned, 1)
                        pe.wait_ge(chain, chain_steps)
                        pe.transpose(sp_full[:, 0:width], carry[:, :], ident[0:width, 0:width]).then_inc(turned, 1)

                    @block.vector
                    def _(dve):
                        then = chained(dve, chain)
                        dve.wait_ge(turned, 1)
                        then(dve.tensor_copy(seg[:, :, :], sp_[:, 0:3 * P].rearrange("f (k p) -> f k p", k=3)))
                        if peak:
                            then(dve.tensor_scalar(pen[:, :], seg[:, 1], BIG, -BIG, ALU.mult, ALU.add))
                            then(dve.tensor_tensor_scan(run[:, :], pen[:, :], seg[:, 0], -BIG, ALU.add, ALU.max))
                        else:
                            then(dve.tensor_tensor_scan(run[:, :], seg[:, 1], seg[:, 0], 0.0, ALU.mult, ALU.add))
                        then(dve.memset(carry[:, 0:1], -BIG if peak else 0.0))
                        then(dve.tensor_tensor(carry[:, 1:P], run[:, 0:P - 1], seg[:, 2, 1:P], ALU.mult))
                        if peak:
                            then(dve.tensor_scalar(pen[:, :], seg[:, 2], BIG, -BIG, ALU.mult, ALU.add))
                            then(dve.tensor_tensor(carry[:, 1:P], carry[:, 1:P], pen[:, 1:P], ALU.add))
                        dve.wait_ge(turned, 2)
                        dve.wait_ge(fetched, 16)
                        dve.tensor_tensor(ends[:, :], ends[:, :], sp_full[:, 0:width], ALU.max if peak else ALU.add).then_inc(carried, 1)

                    @block.gpsimd
                    def _(pool):
                        pool.indirect_dma_start(ends[:, :], None, dest, bass.IndirectOffsetOnAxis(
                            ap=first_end_i[:, 0:1], axis=0)).then_inc(fetched, 16)
                        pool.wait_ge(carried, 1)
                        pool.indirect_dma_start(dest, bass.IndirectOffsetOnAxis(ap=first_end_i[:, 0:1], axis=0),
                                                ends[:, :], None, bounds_check=EP - 1, oob_is_err=False).then_inc(fetched, 16)
                        pool.wait_ge(fetched, 32)

        def messages(tag, ex, znext=None):
            with phase() as c:
                got = sb(f"got{tag}", [P, UNROLL, GT, TW], F32, c)
                att = sb(f"s_att{tag}", [P, UNROLL, GT, R], F32, c)
                msg = sb(f"msg{tag}", [P, UNROLL, GT, M], F32, c)
                acc = sb(f"acc{tag}", [P, UNROLL, GT, M], F32, c)
                gathered = [lasting(f"s_ga{tag}{u}") for u in range(UNROLL)]
                att_in = [sem(f"s_at{tag}{u}") for u in range(UNROLL)]
                stored = [sem(f"s_st{tag}{u}") for u in range(UNROLL)]
                index = sb(f"index{tag}", [P, UNROLL, GT], I32, c)
                index_ready, begun = sem(f"s_ix{tag}"), sem(f"s_be{tag}")
                prod = sb(f"s_prod{tag}", [P, GT, R], F32, c)
                prod_ready, terms = sem(f"s_pr{tag}"), sem(f"s_te{tag}")
                weighed, msg_ready, summed = sem(f"s_we{tag}"), sem(f"s_ms{tag}"), sem(f"s_su{tag}")
                with nc.Block() as block:
                    @block.gpsimd
                    def _(pool):
                        with pool.Fori(0, NG // UNROLL) as i:
                            for u in range(UNROLL):
                                g = i * UNROLL + u
                                pool.wait_ge(index_ready, g + 1)
                                pool.sem_inc(begun, 1)
                                for t in range(GT):
                                    pool.indirect_dma_start(got[:, u, t], None, table, bass.IndirectOffsetOnAxis(
                                        ap=index[:, u, t:t + 1], axis=0)).then_inc(gathered[u], 16)

                    @block.sync
                    def _(sp):
                        with sp.Fori(0, NG // UNROLL) as i:
                            for u in range(UNROLL):
                                g = i * UNROLL + u
                                sp.wait_ge(msg_ready, g * 2 + 2)
                                sp.dma_start(att[:, u], attr[:, bass.ds(g * GT, GT), :]).then_inc(att_in[u], 16)

                    @block.vector
                    def _(dve):
                        dve.sem_inc(msg_ready, 2 * UNROLL)
                        dve.sem_inc(terms, 1)
                        dve.memset(acc[:, UNROLL - 1, GT - 1], 0.0).then_inc(summed, 1)

                        def group(g, u, i=None):
                            dve.wait_ge(gathered[u], 16 * GT if i is None else i * (16 * GT) + 16 * GT)
                            dve.wait_ge(att_in[u], 16 if i is None else i * 16 + 16)
                            dve.wait_ge(summed, g * GT + 1)
                            w = msg[:, u, :, M - 1]
                            dve.tensor_tensor(w, got[:, u, :, D + 2], ex[:, bass.ds(g * GT, GT)], ALU.mult).then_inc(weighed, 1)
                            dve.wait_ge(weighed, g + 1)
                            dve.tensor_tensor(msg[:, u, :, 0:D], got[:, u, :, 0:D], bcast(w, [P, GT, D]), ALU.mult).then_inc(msg_ready, 1)
                            if znext is not None:
                                dve.wait_ge(terms, g + 1)
                                dve.tensor_tensor(prod[:, :, :], att[:, u], mid(v[:, 1, 0:R], [P, GT, R]), ALU.mult).then_inc(prod_ready, 1)
                            dve.tensor_tensor(msg[:, u, :, D:D + R], att[:, u], bcast(w, [P, GT, R]), ALU.mult).then_inc(msg_ready, 1)
                            dve.wait_ge(msg_ready, g * 2 + (2 * UNROLL + 2))
                            if i is not None:
                                dve.wait_ge(stored[u], i * 16)
                            for t in range(GT):
                                before = acc[:, u, t - 1] if t else acc[:, (u - 1) % UNROLL, GT - 1]
                                if t:
                                    dve.wait_ge(summed, g * GT + t + 1)
                                dve.scalar_tensor_tensor(acc[:, u, t], before, cont[:, bass.ds(g * GT + t, 1)], msg[:, u, t],
                                                         ALU.mult, ALU.add).then_inc(summed, 1)
                                if t == 0 and znext is not None:
                                    dve.wait_ge(prod_ready, g + 1)
                                    dve.tensor_reduce(znext[:, bass.ds(g * GT, GT)], prod[:, :, :], AX.X, ALU.add).then_inc(terms, 1)

                        for u in range(UNROLL):
                            group(u, u)
                        with dve.Fori(1, NG // UNROLL) as i:
                            for u in range(UNROLL):
                                group(i * UNROLL + u, u, i)
                        if znext is not None:
                            dve.wait_ge(terms, NG + 1)
                            dve.tensor_scalar(znext[:, :], znext[:, :], bias[:, 1:2], None, ALU.add)

                    @block.scalar
                    def _(act):
                        wide = rows[0:EP, :].rearrange("(p t) f -> p t f", p=P)

                        def indices(g, u):
                            act.wait_ge(msg_ready, g * 2 + 2)
                            act.activation(index[:, u], src_i[:, bass.ds(g * GT, GT)], ACT.Copy).then_inc(index_ready, 1)

                        def store(g, u):
                            act.wait_ge(summed, g * GT + (GT + 1))
                            act.dma_start(wide[:, bass.ds(g * GT, GT), :], acc[:, u]).then_inc(stored[u], 16)

                        over_groups_skewed(act, indices, store, UNROLL)
                        for u in range(UNROLL):
                            act.wait_ge(stored[u], 16 * (NG // UNROLL))
                chunk_carries(f"s{tag}", acc[:, UNROLL - 1, GT - 1], M, False, rows)

        def node_rows(tag, source, dest):
            with phase() as c:
                fetched = lasting(f"r_fe{tag}")
                with nc.Block() as block:
                    @block.gpsimd
                    def _(pool):
                        for b in range(NB):
                            pool.indirect_dma_start(dest[:, b], None, source, bass.IndirectOffsetOnAxis(
                                ap=end_i[:, b:b + 1], axis=0)).then_inc(fetched, 16)
                        pool.wait_ge(fetched, 16 * NB)

        def convolved(tag):
            with phase() as c:
                agg = sb(f"agg{tag}", [P, NB, M], F32, c)
                et = sb(f"et{tag}", [R + 1, 7 * P], F32, c)
                tp = pb(f"ctp{tag}", [R + 1, 1024], F32, c)
                ep = pb(f"cep{tag}", [P, 512], F32, c)
                node_rows(tag, rows, agg)
                turned, copied, e_ready, added = (sem(f"c_{n}{tag}") for n in ("tu", "co", "e", "ad"))
                with nc.Block() as block:
                    @block.vector
                    def _(dve):
                        for j in range(NB // 7):
                            part = slice(7 * j, 7 * j + 7)
                            dve.wait_ge(e_ready, j + 1)
                            dve.tensor_tensor(h[:, part, :], agg[:, part, 0:D], ep[:, 0:7 * D].rearrange("p (b f) -> p b f", f=D),
                                              ALU.add).then_inc(added, 1)
                        dve.wait_ge(added, NB // 7)
                        dve.tensor_scalar(h[:, :, :], h[:, :, :], 0.0, None, ALU.max)

                    @block.tensor
                    def _(pe):
                        for j in range(NB // 7):
                            if j:
                                pe.wait_ge(copied, j)
                            for b7 in range(7):
                                last = pe.transpose(tp[:, b7 * P:(b7 + 1) * P], agg[:, 7 * j + b7, D:M], ident[:, :])
                            last.then_inc(turned, 1)
                            pe.wait_ge(copied, j + 1)
                            if j:
                                pe.wait_ge(added, j)
                            for b7 in range(7):
                                last = pe.matmul(ep[:, b7 * D:(b7 + 1) * D], et[:, b7 * P:(b7 + 1) * P], rel_t[:, :],
                                                 start=True, stop=True)
                            last.then_inc(e_ready, 1)

                    @block.scalar
                    def _(act):
                        for j in range(NB // 7):
                            act.wait_ge(turned, j + 1)
                            if j:
                                act.wait_ge(e_ready, j)
                            act.activation(et[:, :], tp[:, 0:7 * P], ACT.Copy).then_inc(copied, 1)

        norm_relu("a")
        leaders()
        for k, (w, b, ai_w, aj_w) in enumerate(((c1_w, c1_b, c1_ai_w, c1_aj_w), (c2_w, c2_b, c2_ai_w, c2_aj_w))):
            with phase() as c:
                xn = sb(f"xn{k}", [P, NB, TW], F32, c)
                project(k, w, b, ai_w, aj_w, xn)
                expand(k, xn, z[k])
                softmax_terms(k, z[k], xn)
            messages(k, z[k], z[1] if k == 0 else None)
            convolved(k)
        with phase() as c:
            with nc.Block() as block:
                @block.vector
                def _(dve):
                    dve.tensor_tensor(x_sb[:, :, :], x_sb[:, :, :], h[:, :, :], ALU.add)
        norm_relu("b")

        w2_sb = sb("w2_sb", [2 * D, D], F32)
        b2_sb = sb("b2_sb", [P, D], F32)
        with phase() as c:
            wt = sb("wt", [D + 1, 2, D], F32, c)
            ht = sb("w_ht", [D + 1, 7 * P], F32, c)
            ab = sb("ab", [P, NB, 2, D], F32, c)
            hp = pb("w_hp", [P, 1024], F32, c)
            xp = pb("w_xp", [P, 1024], F32, c)
            w_in, w_ready, turned, ht_ready, x_ready, x_copied, stored = (sem(f"w_{n}") for n in ("in", "re", "tu", "ht", "xr", "xc", "st"))
            starts, firsts = lasting("w_starts"), lasting("w_firsts")
            first = sb("w_first", [P, D], F32, c)
            with nc.Block() as block:
                @block.sync
                def _(sp):
                    sp.dma_start(wt[0:D, 0], w1[0:D, :]).then_inc(w_in, 16)
                    sp.dma_start(wt[0:D, 1], w1[D:2 * D, :]).then_inc(w_in, 16)
                    sp.dma_start(wt[D:D + 1, 0], b1.rearrange("(a d) -> a d", a=1)).then_inc(w_in, 16)
                    sp.dma_start(w2_sb[0:D, :], w2).then_inc(w_in, 16)
                    sp.dma_start(w2_sb[D:2 * D, :], w2).then_inc(w_in, 16)
                    sp.dma_start(b2_sb[:, :], b2.partition_broadcast(P)).then_inc(w_in, 16)
                    sp.wait_ge(x_copied, NB // 7)
                    sp.dma_start(a_table[0:NP, :].rearrange("(b p) f -> p b f", p=P), ab[:, :, 0]).then_inc(stored, 16)
                    sp.dma_start(b_table[0:NP, :].rearrange("(b p) f -> p b f", p=P), ab[:, :, 1]).then_inc(stored, 16)
                    sp.wait_ge(stored, 32)
                    sp.wait_ge(firsts, 16)
                    sp.wait_ge(starts, 16 * NB)
                    sp.dma_start(row_starts.rearrange("(p t) f -> p t f", p=P)[:, 0, :], first[:, :]).then_inc(stored, 16)
                    sp.wait_ge(stored, 48)

                @block.gpsimd
                def _(pool):
                    pool.wait_ge(x_copied, NB // 7)
                    for b in range(NB):
                        pool.indirect_dma_start(row_starts, bass.IndirectOffsetOnAxis(ap=start_i[:, b:b + 1], axis=0),
                                                ab[:, b, 0], None, bounds_check=EP - 1, oob_is_err=False).then_inc(starts, 16)
                    pool.wait_ge(stored, 32)
                    pool.indirect_dma_start(first[:, :], None, a_table, bass.IndirectOffsetOnAxis(
                        ap=dst0_i[:, 0:1], axis=0)).then_inc(firsts, 16)

                @block.tensor
                def _(pe):
                    for j in range(NB // 7):
                        if j:
                            pe.wait_ge(ht_ready, j)
                        for b7 in range(7):
                            last = pe.transpose(hp[0:D, b7 * P:(b7 + 1) * P], h[:, 7 * j + b7, :], ident[:, :])
                        last.then_inc(turned, 1)
                        pe.wait_ge(ht_ready, j + 1)
                        pe.wait_ge(w_ready, 3)
                        if j:
                            pe.wait_ge(x_copied, j)
                        for b7 in range(7):
                            last = pe.matmul(xp[:, b7 * 2 * D:(b7 + 1) * 2 * D], ht[:, b7 * P:(b7 + 1) * P],
                                             wt[:, :, :].rearrange("p k f -> p (k f)"), start=True, stop=True)
                        last.then_inc(x_ready, 1)

                @block.scalar
                def _(act):
                    for j in range(NB // 7):
                        act.wait_ge(turned, j + 1)
                        if j:
                            act.wait_ge(x_ready, j)
                        act.activation(ht[0:D, :], hp[0:D, 0:7 * P], ACT.Copy).then_inc(ht_ready, 1)

                @block.vector
                def _(dve):
                    dve.memset(ht[D:D + 1, :], 1.0).then_inc(w_ready, 1)
                    dve.memset(wt[D:D + 1, 1], 0.0).then_inc(w_ready, 1)
                    dve.wait_ge(w_in, 96)
                    dve.tensor_tensor(wt[0:D, 0], wt[0:D, 0], wt[0:D, 1], ALU.subtract).then_inc(w_ready, 1)
                    for j in range(NB // 7):
                        dve.wait_ge(x_ready, j + 1)
                        dve.tensor_copy(ab[:, 7 * j:7 * j + 7].rearrange("p b k f -> p (b k f)"), xp[:, 0:14 * D]).then_inc(x_copied, 1)

        with phase() as c:
            got = sb("e_got", [P, UNROLL, GT, D], F32, c)
            rs = sb("e_rs", [P, UNROLL, GT, D], F32, c)
            a_row = sb("e_a", [P, UNROLL, GT, D], F32, c)
            pre = sb("e_pre", [P, UNROLL, GT, D], F32, c)
            hid = sb("e_hid", [2 * D, UNROLL, GT // 2 * P], F32, c)
            acc = sb("e_acc", [P, UNROLL, GT, D], F32, c)
            pen = sb("e_pen", [P, W], F32, c)
            tp = [pb(f"e_tp{j}", [2 * D, GT // 2 * P], F32, c) for j in range(2)]
            mp = [[pb(f"e_mp{j}{k}", [P, GT // 2, D], F32, c) for k in range(2)] for j in range(2)]
            index = sb("e_index", [P, UNROLL, GT], I32, c)
            index_ready, begun = sem("e_ix"), sem("e_be")
            gathered = [lasting(f"e_ga{u}") for u in range(UNROLL)]
            rs_in = [sem(f"e_rs{u}") for u in range(UNROLL)]
            stored = [sem(f"e_st{u}") for u in range(UNROLL)]
            ready, a_ready, pre_ready, turned, hid_ready, m_ready, maxed = (sem(f"e_{n}") for n in ("re", "ar", "pr", "tu", "hi", "me", "ma"))
            with nc.Block() as block:
                @block.gpsimd
                def _(pool):
                    with pool.Fori(0, NG // UNROLL) as i:
                        for u in range(UNROLL):
                            g = i * UNROLL + u
                            pool.wait_ge(index_ready, g + 1)
                            pool.sem_inc(begun, 1)
                            for t in range(GT):
                                pool.indirect_dma_start(got[:, u, t], None, b_table, bass.IndirectOffsetOnAxis(
                                    ap=index[:, u, t:t + 1], axis=0)).then_inc(gathered[u], 16)

                @block.sync
                def _(sp):
                    wide = row_starts.rearrange("(p t) f -> p t f", p=P)
                    with sp.Fori(0, NG // UNROLL) as i:
                        for u in range(UNROLL):
                            g = i * UNROLL + u
                            sp.wait_ge(pre_ready, g + 1)
                            sp.dma_start(rs[:, u], wide[:, bass.ds(g * GT, GT), :]).then_inc(rs_in[u], 16)

                @block.vector
                def _(dve):
                    dve.memset(acc[:, UNROLL - 1, GT - 1], -BIG).then_inc(ready, 1)
                    dve.memset(a_row[:, UNROLL - 1, GT - 1], 0.0).then_inc(ready, 1)
                    dve.tensor_scalar(pen[:, :], cont[:, :], BIG, -BIG, ALU.mult, ALU.add).then_inc(ready, 1)
                    dve.wait_ge(ready, 3)
                    dve.sem_inc(pre_ready, UNROLL)
                    dve.sem_inc(a_ready, 1)
                    dve.sem_inc(maxed, 2 * GT)

                    def before(g, u, i):
                        dve.wait_ge(rs_in[u], i * 16 + 16)
                        for t in range(GT):
                            prev = a_row[:, u, t - 1] if t else a_row[:, (u - 1) % UNROLL, GT - 1]
                            dve.wait_ge(a_ready, g * GT + (t + 1))
                            dve.scalar_tensor_tensor(a_row[:, u, t], prev, cont[:, bass.ds(g * GT + t, 1)], rs[:, u, t],
                                                     ALU.mult, ALU.add).then_inc(a_ready, 1)
                            yield

                    def plus(g, u, i):
                        dve.wait_ge(a_ready, g * GT + (GT + 1))
                        dve.wait_ge(gathered[u], i * (16 * GT) + 16 * GT)
                        dve.wait_ge(turned, g + 1)
                        dve.tensor_tensor(pre[:, u], a_row[:, u], got[:, u], ALU.add).then_inc(pre_ready, 1)

                    def after(g, u, i=None):
                        dve.wait_ge(m_ready, g + 1)
                        if i is not None:
                            dve.wait_ge(stored[u], i * 16)
                        for t in range(GT):
                            prev = acc[:, u, t - 1] if t else acc[:, (u - 1) % UNROLL, GT - 1]
                            dve.wait_ge(maxed, g * GT + (t + 2 * GT))
                            dve.scalar_tensor_tensor(acc[:, u, t], prev, pen[:, bass.ds(g * GT + t, 1)],
                                                     mp[u % 2][t % 2][:, t // 2],
                                                     ALU.add, ALU.max).then_inc(maxed, 1)
                            yield

                    dve.sem_inc(turned, UNROLL)

                    def step(g, u, i, iu=None):
                        ahead, au = i + (u + 2) // UNROLL, (u + 2) % UNROLL
                        for _ in zip(before(g + 2, au, ahead), after(g, u, iu)):
                            pass
                        plus(g + 2, au, ahead)

                    for g in range(2):
                        for _ in before(g, g, 0):
                            pass
                        plus(g, g, 0)
                    for u in range(UNROLL):
                        step(u, u, 0)
                    with dve.Fori(1, NG // UNROLL - 1) as i:
                        for u in range(UNROLL):
                            step(i * UNROLL + u, u, i, i)
                    for g in range(NG - UNROLL, NG):
                        if g + 2 < NG:
                            step(g, g % UNROLL, g // UNROLL, g // UNROLL)
                        else:
                            for _ in after(g, g % UNROLL, g // UNROLL):
                                pass

                @block.tensor
                def _(pe):
                    def turn(g, u):
                        pe.wait_ge(pre_ready, g + (UNROLL + 1))
                        pe.wait_ge(hid_ready, g + 1)
                        for t in range(0, GT, 2):
                            last = pe.transpose(tp[u % 2][:, t // 2 * P:(t // 2 + 1) * P],
                                                pre[:, u, t:t + 2].rearrange("p t f -> p (t f)"), ident[:, :])
                        last.then_inc(turned, 1)

                    def multiply(g, u):
                        pe.wait_ge(hid_ready, g + 3)
                        pe.wait_ge(maxed, g * GT + GT)
                        for t in range(GT):
                            half = slice(t % 2 * D, t % 2 * D + D)
                            last = pe.matmul(mp[u % 2][t % 2][:, t // 2], hid[half, u, t // 2 * P:(t // 2 + 1) * P], w2_sb[half, :],
                                             start=True, stop=True)
                        last.then_inc(m_ready, 1)

                    def both(g, u):
                        turn(g, u)
                        multiply(g, u)

                    over_groups(pe, both)

                @block.scalar
                def _(act):
                    act.sem_inc(hid_ready, 2)
                    wide = peak_rows[0:EP, :].rearrange("(p t) f -> p t f", p=P)

                    def relu(g, u):
                        act.wait_ge(turned, g + (UNROLL + 1))
                        act.activation(hid[:, u], tp[u % 2][:, :], ACT.Relu).then_inc(hid_ready, 1)

                    def store(g, u):
                        act.wait_ge(maxed, g * GT + 3 * GT)
                        act.dma_start(wide[:, bass.ds(g * GT, GT), :], acc[:, u]).then_inc(stored[u], 16)

                    def indices(g, u):
                        act.wait_ge(pre_ready, g + 1)
                        act.activation(index[:, u], src_i[:, bass.ds(g * GT, GT)], ACT.Copy).then_inc(index_ready, 1)

                    for u in range(UNROLL):
                        indices(u, u)
                    relu(0, 0)
                    relu(1, 1)
                    with act.Fori(0, NG // UNROLL - 1) as i:
                        for u in range(UNROLL):
                            indices(i * UNROLL + (u + UNROLL), u)
                            relu(i * UNROLL + (u + 2), (u + 2) % UNROLL)
                            store(i * UNROLL + u, u)
                    for g in range(NG - UNROLL, NG):
                        if g + 2 < NG:
                            relu(g + 2, (g + 2) % UNROLL)
                        store(g, g % UNROLL)
                    for u in range(UNROLL):
                        act.wait_ge(stored[u], 16 * (NG // UNROLL))
            chunk_carries("m", acc[:, UNROLL - 1, GT - 1], D, True, peak_rows)

        with phase() as c:
            agg = sb("f_agg", [P, NB, D], F32, c)
            node_rows("m", peak_rows, agg)
            chain, done, stored = sem("f_chain"), sem("f_done"), sem("f_stored")
            with nc.Block() as block:
                @block.vector
                def _(dve):
                    then = chained(dve, chain)
                    then(dve.tensor_tensor(agg[:, :, :], agg[:, :, :], mid(b2_sb[:, :], [P, NB, D]), ALU.add))
                    then(dve.tensor_tensor(agg[:, :, :], agg[:, :, :], bcast(has[:, :], [P, NB, D]), ALU.mult))
                    dve.tensor_tensor(agg[:, :, :], agg[:, :, :], x_sb[:, :, :], ALU.add).then_inc(done, 1)

                @block.sync
                def _(sp):
                    sp.wait_ge(done, 1)
                    full = N // P
                    sp.dma_start(out[0:full * P, :].rearrange("(b p) f -> p b f", p=P), agg[:, 0:full]).then_inc(stored, 16)
                    sp.dma_start(out[full * P:N, :], agg[0:N - full * P, full]).then_inc(stored, 16)
                    sp.wait_ge(stored, 32)


def bass_col(ap):
    return ap.rearrange("(d a) -> d a", a=1)


def accumulate(pe, add_group):
    for g in range(UNROLL):
        add_group(g, g, start=g == 0)
    with pe.Fori(0, NG // UNROLL - 2) as i:
        for u in range(UNROLL):
            add_group(i * UNROLL + (UNROLL + u), u)
    for g in range(NG - UNROLL, NG):
        add_group(g, g % UNROLL, stop=g == NG - 1)

_C = ("lin_w", "lin_b", "ai_w", "ai_b", "aj_w", "aj_b", "ew_w", "ew_b")
ORDER = (["x", "src", "dst", "edge_attr_32", "L0_gnn_rel_w", "L0_gnn_rel_b"]
         + [f"L0_gnn_c{k}_{n}" for k in (1, 2) for n in _C]
         + ["L1_gnn_W1", "L1_gnn_b1", "L1_gnn_W2", "L1_gnn_b2"])


def kernel(**inputs):
    import numpy as np
    import concourse.bacc as bacc
    from concourse.bass_utils import run_bass_kernel_spmd

    def edges(a, fill):
        a = np.asarray(a)
        pad = [(0, EP - E)] + [(0, 0)] * (a.ndim - 1)
        return np.ascontiguousarray(np.pad(a, pad, constant_values=fill).reshape((P, W) + a.shape[1:]))

    arrays = {k: np.ascontiguousarray(np.asarray(a)) for k, a in inputs.items()}
    arrays["x"] = np.pad(arrays["x"], [(0, NP - N), (0, 0)])
    arrays["src"] = edges(inputs["src"], PAD_NODE)
    arrays["dst"] = edges(inputs["dst"], PAD_NODE)
    arrays["edge_attr_32"] = edges(inputs["edge_attr_32"], 0)
    nc = bacc.Bacc("TRN2", target_bir_lowering=False, num_devices=1)
    fed, args = {}, []
    for name in ORDER:
        fed[f"in_{name}"] = arrays[name]
        args.append(nc.dram_tensor(f"in_{name}", arrays[name].shape, mybir.dt.from_np(arrays[name].dtype),
                                   kind="ExternalInput").ap())
    out = nc.dram_tensor("out", [N, D], F32, kind="ExternalOutput").ap()
    gnn_kernel(nc, *args, out)
    return run_bass_kernel_spmd(nc, [fed], core_ids=[0]).results[0]["out"]
```
